# Optimizing a Trainium2 kernel written in Bass

```python
import numpy as np
import jax
import jax.numpy as jnp

def _softmax(x, axis=-1):
    return jax.nn.softmax(x, axis=axis)

def _gelu(x):
    return jax.nn.gelu(x, approximate=True)

def _silu(x):
    return jax.nn.silu(x)

def _sigmoid(x):
    return jax.nn.sigmoid(x)

def _layernorm(x, axis=-1, eps=1e-05):
    m = jnp.mean(x, axis=axis, keepdims=True)
    v = jnp.var(x, axis=axis, keepdims=True)
    return (x - m) / jnp.sqrt(v + eps)

def _scatter_add(tgt, idx, src, axis=0):
    return tgt.at[idx].add(src)

def _segment_sum(src, seg, n):
    return jax.ops.segment_sum(src, seg, n)
kernel_name = 'mk_decoder_postln_d1_seqx_r8_dbd14a'

def setup_inputs(seed: int=0):
    np.random.seed(seed)
    _w = jnp.asarray

    def _rec_inputs():
        import jax
        import jax.numpy as jnp
        _rk = jax.random.key(seed)
        x = -0.0002928 + 1 * jax.random.normal(jax.random.fold_in(_rk, 1), (32, 128, 128), jnp.float32)
        _lenS = 128 - jax.random.randint(jax.random.fold_in(_rk, 7), (32,), 0, max(1, 128 // 4) + 1, jnp.int32)
        _lenS2 = 128 - jax.random.randint(jax.random.fold_in(_rk, 8), (32,), 0, max(1, 128 // 4) + 1, jnp.int32)
        _ctx_1024P = jax.random.normal(jax.random.fold_in(_rk, 11), (32, 16, 128), jnp.float32)
        _ctx_1024c = jax.random.dirichlet(jax.random.fold_in(_rk, 511), 0.3 * jnp.ones((16,), jnp.float32), (32, 128))
        _ctx_1024t = jnp.einsum('bsk,bkd->bsd', _ctx_1024c, _ctx_1024P)
        _ctx_1024t = _ctx_1024t * jax.lax.rsqrt(jnp.mean(jnp.square(_ctx_1024t)) + 1e-12) * 0.953939
        ctx_1024 = -1.39393e-06 + 0.999914 * (_ctx_1024t + 0.3 * jax.random.normal(jax.random.fold_in(_rk, 611), (32, 128, 128), jnp.float32))
        return (x, ctx_1024)
    x, ctx_1024 = _rec_inputs()

    def _L0_attn_setup():
        import jax, jax.numpy as jnp
        import numpy as np
        D_MODEL = 128
        D_STATE = 64
        D_CONV = 4
        EXPAND = 2
        HEADDIM = 128
        NGROUPS = 1
        CHUNK = 32
        D_INNER = EXPAND * D_MODEL
        NHEADS = D_INNER // HEADDIM
        D_IN_PROJ = 2 * D_INNER + 2 * NGROUPS * D_STATE + NHEADS
        CONV_DIM = D_INNER + 2 * NGROUPS * D_STATE
        EPS = 1e-05

        def segsum(x):
            T = x.shape[-1]
            xe = jnp.broadcast_to(x[..., :, None], x.shape + (T,))
            xe = jnp.where(jnp.tril(jnp.ones((T, T), dtype=bool), -1), xe, 0.0)
            seg = jnp.cumsum(xe, axis=-2)
            return jnp.where(jnp.tril(jnp.ones((T, T), dtype=bool), 0), seg, -jnp.inf)

        def ssd(x, A, B, C, block_len):
            b, l, h, p = x.shape
            g, n = (B.shape[2], B.shape[3])
            c = l // block_len
            x = x.reshape(b, c, block_len, h, p)
            A = A.reshape(b, c, block_len, h).transpose(0, 3, 1, 2)
            B = jnp.repeat(B.reshape(b, c, block_len, g, n), h // g, axis=3)
            C = jnp.repeat(C.reshape(b, c, block_len, g, n), h // g, axis=3)
            A_cumsum = jnp.cumsum(A, axis=-1)
            L = jnp.exp(segsum(A))
            Y_diag = jnp.einsum('bclhn,bcshn,bhcls,bcshp->bclhp', C, B, L, x)
            decay_states = jnp.exp(A_cumsum[..., -1:] - A_cumsum)
            states = jnp.einsum('bclhn,bhcl,bclhp->bchpn', B, decay_states, x)
            states = jnp.concatenate([jnp.zeros_like(states[:, :1]), states], axis=1)
            A_last = jnp.pad(A_cumsum[..., -1], ((0, 0), (0, 0), (1, 0)))
            decay_chunk = jnp.exp(segsum(A_last))
            new_states = jnp.einsum('bhzc,bchpn->bzhpn', decay_chunk, states)
            states, final_state = (new_states[:, :-1], new_states[:, -1])
            state_decay_out = jnp.exp(A_cumsum)
            Y_off = jnp.einsum('bclhn,bchpn,bhcl->bclhp', C, states, state_decay_out)
            return ((Y_diag + Y_off).reshape(b, l, h, p), final_state)

        def depthwise_conv(x, w, b):
            y = jax.lax.conv_general_dilated(x, w, window_strides=(1,), padding=((D_CONV - 1, D_CONV - 1),), dimension_numbers=('NWC', 'WIO', 'NWC'), feature_group_count=x.shape[-1])
            return y + b
        key = jax.random.key(seed)
        ks = jax.random.split(key, 8)
        b, l = (4, 512)
        u = jax.random.normal(ks[0], (b, l, D_MODEL), dtype=jnp.float32)
        W_in = jax.random.normal(ks[1], (D_MODEL, D_IN_PROJ), dtype=jnp.float32) * D_MODEL ** (-0.5)
        conv_w = jax.random.normal(ks[2], (D_CONV, 1, CONV_DIM), dtype=jnp.float32) * D_CONV ** (-0.5)
        conv_b = jnp.zeros((CONV_DIM,), dtype=jnp.float32)
        dt = jnp.exp(jax.random.uniform(ks[3], (NHEADS,)) * (jnp.log(0.1) - jnp.log(0.001)) + jnp.log(0.001))
        dt = jnp.clip(dt, min=0.0001)
        dt_bias = dt + jnp.log(-jnp.expm1(-dt))
        A_log = jnp.log(jax.random.uniform(ks[4], (NHEADS,), minval=1.0, maxval=16.0))
        D = jnp.ones((NHEADS,), dtype=jnp.float32)
        norm_scale = jnp.ones((D_INNER,), dtype=jnp.float32)
        W_out = jax.random.normal(ks[5], (D_INNER, D_MODEL), dtype=jnp.float32) * D_INNER ** (-0.5)
        return {'u': u, 'W_in': W_in, 'conv_w': conv_w, 'conv_b': conv_b, 'dt_bias': dt_bias, 'A_log': A_log, 'D': D, 'norm_scale': norm_scale, 'W_out': W_out}
    _L0_attn_all = _L0_attn_setup()
    _L0_attn_in = {k: v for k, v in _L0_attn_all.items() if k in ('W_in', 'conv_w', 'conv_b', 'dt_bias', 'A_log', 'D', 'norm_scale', 'W_out')}
    del _L0_attn_all

    def _L0_xattn_setup():
        import jax, jax.numpy as jnp
        import numpy as np
        import math
        B, S, DM, H = (2, 256, 128, 16)
        HD = DM // H
        key = jax.random.key(seed)
        ks = jax.random.split(key, 7)
        mk = lambda k, shp, s=1.0: jax.random.normal(k, shp, dtype=jnp.float32) * s
        return {'q': mk(ks[0], (B, S, DM)), 'k': mk(ks[1], (B, S, DM)), 'v': mk(ks[2], (B, S, DM)), 'wq': mk(ks[3], (DM, DM), 0.02), 'wk': mk(ks[4], (DM, DM), 0.02), 'wv': mk(ks[5], (DM, DM), 0.02), 'wo': mk(ks[6], (DM, DM), 0.02)}
    _L0_xattn_all = _L0_xattn_setup()
    _L0_xattn_in = {k: v for k, v in _L0_xattn_all.items() if k in ('wq', 'wk', 'wv', 'wo')}
    del _L0_xattn_all

    def _L0_ffn_setup():
        import jax, jax.numpy as jnp
        import numpy as np
        B, S, H, F, E, TOP_K = (4, 256, 128, 512, 8, 2)
        key = jax.random.key(seed)
        ks = jax.random.split(key, 5)
        scale = 0.02
        return {'hidden_states': jax.random.normal(ks[0], (B, S, H), dtype=jnp.float32), 'router_w': jax.random.normal(ks[1], (E, H), dtype=jnp.float32) * scale, 'gate_w': jax.random.normal(ks[2], (E, F, H), dtype=jnp.float32) * scale, 'up_w': jax.random.normal(ks[3], (E, F, H), dtype=jnp.float32) * scale, 'down_w': jax.random.normal(ks[4], (E, H, F), dtype=jnp.float32) * scale}
    _L0_ffn_all = _L0_ffn_setup()
    _L0_ffn_in = {k: v for k, v in _L0_ffn_all.items() if k in ('router_w', 'gate_w', 'up_w', 'down_w')}
    del _L0_ffn_all
    return {'x': x, 'ctx_1024': ctx_1024, 'L0_attn_W_in': _L0_attn_in['W_in'], 'L0_attn_conv_w': _L0_attn_in['conv_w'], 'L0_attn_conv_b': _L0_attn_in['conv_b'], 'L0_attn_dt_bias': _L0_attn_in['dt_bias'], 'L0_attn_A_log': _L0_attn_in['A_log'], 'L0_attn_D': _L0_attn_in['D'], 'L0_attn_norm_scale': _L0_attn_in['norm_scale'], 'L0_attn_W_out': _L0_attn_in['W_out'], 'L0_xattn_wq': _L0_xattn_in['wq'], 'L0_xattn_wk': _L0_xattn_in['wk'], 'L0_xattn_wv': _L0_xattn_in['wv'], 'L0_xattn_wo': _L0_xattn_in['wo'], 'L0_ffn_router_w': _L0_ffn_in['router_w'], 'L0_ffn_gate_w': _L0_ffn_in['gate_w'], 'L0_ffn_up_w': _L0_ffn_in['up_w'], 'L0_ffn_down_w': _L0_ffn_in['down_w']}

def reference(x, ctx_1024, L0_attn_W_in, L0_attn_conv_w, L0_attn_conv_b, L0_attn_dt_bias, L0_attn_A_log, L0_attn_D, L0_attn_norm_scale, L0_attn_W_out, L0_xattn_wq, L0_xattn_wk, L0_xattn_wv, L0_xattn_wo, L0_ffn_router_w, L0_ffn_gate_w, L0_ffn_up_w, L0_ffn_down_w):
    import jax
    import jax.numpy as jnp

    def _L0_attn_ref(u, W_in, conv_w, conv_b, dt_bias, A_log, D, norm_scale, W_out):
        import jax, jax.numpy as jnp
        import numpy as np
        D_MODEL = 128
        D_STATE = 64
        D_CONV = 4
        EXPAND = 2
        HEADDIM = 128
        NGROUPS = 1
        CHUNK = 32
        D_INNER = EXPAND * D_MODEL
        NHEADS = D_INNER // HEADDIM
        D_IN_PROJ = 2 * D_INNER + 2 * NGROUPS * D_STATE + NHEADS
        CONV_DIM = D_INNER + 2 * NGROUPS * D_STATE
        EPS = 1e-05

        def segsum(x):
            T = x.shape[-1]
            xe = jnp.broadcast_to(x[..., :, None], x.shape + (T,))
            xe = jnp.where(jnp.tril(jnp.ones((T, T), dtype=bool), -1), xe, 0.0)
            seg = jnp.cumsum(xe, axis=-2)
            return jnp.where(jnp.tril(jnp.ones((T, T), dtype=bool), 0), seg, -jnp.inf)

        def ssd(x, A, B, C, block_len):
            b, l, h, p = x.shape
            g, n = (B.shape[2], B.shape[3])
            c = l // block_len
            x = x.reshape(b, c, block_len, h, p)
            A = A.reshape(b, c, block_len, h).transpose(0, 3, 1, 2)
            B = jnp.repeat(B.reshape(b, c, block_len, g, n), h // g, axis=3)
            C = jnp.repeat(C.reshape(b, c, block_len, g, n), h // g, axis=3)
            A_cumsum = jnp.cumsum(A, axis=-1)
            L = jnp.exp(segsum(A))
            Y_diag = jnp.einsum('bclhn,bcshn,bhcls,bcshp->bclhp', C, B, L, x)
            decay_states = jnp.exp(A_cumsum[..., -1:] - A_cumsum)
            states = jnp.einsum('bclhn,bhcl,bclhp->bchpn', B, decay_states, x)
            states = jnp.concatenate([jnp.zeros_like(states[:, :1]), states], axis=1)
            A_last = jnp.pad(A_cumsum[..., -1], ((0, 0), (0, 0), (1, 0)))
            decay_chunk = jnp.exp(segsum(A_last))
            new_states = jnp.einsum('bhzc,bchpn->bzhpn', decay_chunk, states)
            states, final_state = (new_states[:, :-1], new_states[:, -1])
            state_decay_out = jnp.exp(A_cumsum)
            Y_off = jnp.einsum('bclhn,bchpn,bhcl->bclhp', C, states, state_decay_out)
            return ((Y_diag + Y_off).reshape(b, l, h, p), final_state)

        def depthwise_conv(x, w, b):
            y = jax.lax.conv_general_dilated(x, w, window_strides=(1,), padding=((D_CONV - 1, D_CONV - 1),), dimension_numbers=('NWC', 'WIO', 'NWC'), feature_group_count=x.shape[-1])
            return y + b
        b, l, _ = u.shape
        zxbcdt = u @ W_in
        z, xBC, dt = jnp.split(zxbcdt, (D_INNER, D_INNER + CONV_DIM), axis=-1)
        dt = jax.nn.softplus(dt + dt_bias)
        xBC = jax.nn.silu(depthwise_conv(xBC, conv_w, conv_b))[:, :l, :]
        x, B, C = jnp.split(xBC, (D_INNER, D_INNER + NGROUPS * D_STATE), axis=-1)
        x = x.reshape(b, l, NHEADS, HEADDIM) * dt[..., None]
        A = -jnp.exp(A_log)
        y, _ = ssd(x, A * dt, B.reshape(b, l, NGROUPS, D_STATE), C.reshape(b, l, NGROUPS, D_STATE), CHUNK)
        y = y + x * D[None, None, :, None]
        y = y.reshape(b, l, D_INNER) * z
        y = y * jax.lax.rsqrt(jnp.mean(jnp.square(y), axis=-1, keepdims=True) + EPS) * norm_scale
        return y @ W_out

    def _L0_xattn_ref(q, k, v, wq, wk, wv, wo):
        import jax, jax.numpy as jnp
        import numpy as np
        import math
        B, S, DM, H = (2, 256, 128, 16)
        HD = DM // H
        bsz, seqlen, _ = q.shape

        def proj(x, w):
            y = jnp.einsum('bsd,ed->bse', x, w)
            return y.reshape(bsz, seqlen, H, HD).transpose(0, 2, 1, 3)
        xq, xk, xv = (proj(q, wq), proj(k, wk), proj(v, wv))
        scores = jnp.einsum('bhqd,bhkd->bhqk', xq, xk) / math.sqrt(HD)
        causal = jnp.tril(jnp.ones((seqlen, seqlen), dtype=bool))
        scores = jnp.where(causal[None, None], scores, -jnp.inf)
        probs = jax.nn.softmax(scores.astype(jnp.float32), axis=-1).astype(xq.dtype)
        out = jnp.einsum('bhqk,bhkd->bhqd', probs, xv)
        out = out.transpose(0, 2, 1, 3).reshape(bsz, seqlen, DM)
        return jnp.einsum('bsd,ed->bse', out, wo)

    def _L0_ffn_ref(hidden_states, router_w, gate_w, up_w, down_w):
        import jax, jax.numpy as jnp
        import numpy as np
        B, S, H, F, E, TOP_K = (4, 256, 128, 512, 8, 2)
        b, s, h = hidden_states.shape
        x = hidden_states.reshape(-1, h)
        router_logits = x @ router_w.T
        routing_weights = jax.nn.softmax(router_logits.astype(jnp.float32), axis=-1)
        top_k_weights, top_k_index = jax.lax.top_k(routing_weights, TOP_K)
        top_k_weights = top_k_weights.astype(x.dtype)
        w_full = jnp.sum(jax.nn.one_hot(top_k_index, E, dtype=x.dtype) * top_k_weights[..., None], axis=1)

        def expert_step(acc, ew):
            gw, uw, dw, w = ew
            hid = jax.nn.silu(x @ gw.T) * (x @ uw.T)
            return (acc + w[:, None] * (hid @ dw.T), None)
        out0 = jnp.zeros_like(x)
        out, _ = jax.lax.scan(expert_step, out0, (gate_w, up_w, down_w, w_full.T))
        return out.reshape(b, s, h)
    x = _layernorm(x + _L0_attn_ref(x, L0_attn_W_in, L0_attn_conv_w, L0_attn_conv_b, L0_attn_dt_bias, L0_attn_A_log, L0_attn_D, L0_attn_norm_scale, L0_attn_W_out), axis=-1)
    x = _layernorm(x + _L0_xattn_ref(x, ctx_1024, ctx_1024, L0_xattn_wq, L0_xattn_wk, L0_xattn_wv, L0_xattn_wo), axis=-1)
    x = _layernorm(x + _L0_ffn_ref(x, L0_ffn_router_w, L0_ffn_gate_w, L0_ffn_up_w, L0_ffn_down_w), axis=-1)
    return x

_drawn_inputs = setup_inputs


def setup_inputs(seed=0):
    import zlib

    import numpy as np

    out = dict(_drawn_inputs(seed))
    spreads = {'L0_attn_conv_b': (0.0, 0.1), 'L0_attn_D': (1.0, 0.6), 'L0_attn_norm_scale': (1.0, 0.2)}
    factors = {'L0_xattn_wq': 8.0,
     'L0_xattn_wk': 8.0,
     'L0_ffn_router_w': 8.0,
     'L0_ffn_gate_w': 8.0,
     'L0_ffn_up_w': 8.0,
     'L0_ffn_down_w': 8.0}
    for name, (base, spread) in spreads.items():
        noise = np.random.default_rng([zlib.crc32(name.encode()), seed]).standard_normal(out[name].shape)
        drawn = base * np.exp(spread * noise) if base else spread * noise
        out[name] = jnp.asarray(drawn.astype(out[name].dtype))
    for name, factor in factors.items():
        out[name] = (out[name] * factor).astype(out[name].dtype)
    return out
```

```python
from contextlib import ExitStack

import concourse.bass as bass
from concourse import mybir

F32 = mybir.dt.float32
F32R = mybir.dt.float32r
BF16 = mybir.dt.bfloat16
I32 = mybir.dt.int32
ALU = mybir.AluOpType
ACT = mybir.ActivationFunctionType
AX_X = mybir.AxisListType.X
P = 128
EPS = 1e-5
NEG = -30000.0


def build(nc, t, out):
    NB, S, D = t["x"].shape
    DI = t["L0_attn_W_out"].shape[0]
    NH = t["L0_attn_D"].shape[0]
    TAPS, _, CC = t["L0_attn_conv_w"].shape
    NS = (CC - DI) // 2
    NPAIR = NB // 2
    assert (S, D, DI, NH, TAPS, NS) == (P, P, 2 * P, 2, 4, 64)
    ZX = DI
    DTC = DI + CC

    x_rows = t["x"].rearrange("b s d -> s b d")
    ctx_rows = t["ctx_1024"].rearrange("b s d -> s b d")
    out_rows = out.rearrange("b s d -> s b d")

    with ExitStack() as ctx:
        own = [ctx]

        def sb(name, shape, dt=F32):
            return own[-1].enter_context(nc.sbuf_tensor(name, shape, dt))

        def sem(name):
            return ctx.enter_context(nc.semaphore(name))

        def sem2(name):
            return [sem(name + "0"), sem(name + "1")]

        bank = [ctx.enter_context(nc.psum_tensor(f"bank{i}", [P, 512], F32)) for i in range(8)]

        ident = sb("ident", [P, P])
        x_nat = sb("x_nat", [P, NB, D])
        minus_half = sb("minus_half", [P, 2])
        eps_pool = sb("eps_pool", [P, 2])
        spare_pool = sb("spare_pool", [1, 1])
        spare_dve = sb("spare_dve", [1, 1])
        xr = [[sb(f"xr{p}{j}", [P, D]) for j in range(2)] for p in range(2)]
        stats = [[sb(f"stats{p}{j}", [P, 6]) for j in range(2)] for p in range(2)]
        mv = [sb(f"mv{p}", [P, 2, 2]) for p in range(2)]
        v_eps = [sb(f"v_eps{p}", [P, 2]) for p in range(2)]
        r_ln = [sb(f"r_ln{p}", [P, 2]) for p in range(2)]
        early = ExitStack()
        own.append(early)
        ident_bf = sb("ident_bf", [P, P], BF16)
        ones_f = sb("ones_f", [P, 1])
        half_ones = sb("ones_bf", [3, 2 * P], BF16)
        after = sb("after", [P, P])
        upto = sb("upto", [P, NH, P])
        future = sb("future", [P, NH, P], BF16)
        w_in = sb("w_in", [P, 2 * DI + 2 * NS + NH])
        cw = sb("cw", [P, TAPS, CC])
        wconv = sb("wconv", [P, TAPS, CC])
        wconv_h = sb("wconv_h", [P, TAPS, CC], F32R)
        wconv_l = sb("wconv_l", [P, TAPS, CC], F32R)
        wz_h = sb("wz_h", [P, DI], F32R)
        wz_l = sb("wz_l", [P, DI], F32R)
        cb = sb("cb", [3, CC])
        cb_part = [sb(f"cb_part{i}", [3, CC], BF16) for i in range(3)]
        cb_rest = sb("cb_rest", [3, CC])
        cb_rows = sb("cb_rows", [3, CC], BF16)
        w_out = sb("w_out", [P, NH, D])
        nscale = sb("nscale", [P, NH])
        a_log = sb("a_log", [P, NH])
        a_neg = sb("a_neg", [P, NH])
        dt_bias = sb("dt_bias", [P, NH])
        d_skip = sb("d_skip", [P, NH])
        d_diag = sb("d_diag", [P, NH, P])
        xT = sb("xT", [P, NB, S])
        dt_v = sb("dt_v", [P, NB, NH])
        dt_e = sb("dt_e", [P, NB, NH])
        dt_half = sb("dt_half", [P, NB, NH])
        dt_a = sb("dt_a", [P, NB, NH])
        xh = [sb(f"xh{p}", [P, 2, S + 4], F32R) for p in range(2)]
        xl = [sb(f"xl{p}", [P, 2, S + 4], F32R) for p in range(2)]
        t_bc = sb("t_bc", [P, 2 * S])
        b_sb = [sb(f"b_sb{p}", [NS, 2 * S]) for p in range(2)]
        c_sb = [sb(f"c_sb{p}", [NS, 2 * S]) for p in range(2)]
        z_sb = [sb(f"z_sb{p}", [P, NH, 2 * S]) for p in range(2)]
        t_x = [sb(f"t_x{j}", [P, DI]) for j in range(2)]
        x_s = [sb(f"x_s{j}", [P, DI]) for j in range(2)]
        xdt = [[sb(f"xdt{p}{j}", [P, DI]) for j in range(2)] for p in range(2)]
        ua = [sb(f"ua{j}", [P, NH, S]) for j in range(2)]
        e_sb = [sb(f"e_sb{j}", [P, NH, S]) for j in range(2)]
        w_sb = [sb(f"w_sb{j}", [P, NH, S]) for j in range(2)]
        y_sb = [sb(f"y_sb{j}", [P, NH, S]) for j in range(2)]
        sq_sb = [sb(f"sq_sb{j}", [P, NH, S]) for j in range(2)]

        pr = [[sb(f"pr{p}{j}", [P, D]) for j in range(2)] for p in range(2)]
        ss_eps = [sb(f"ss_eps{p}", [P, 2]) for p in range(2)]
        r_gate = [sb(f"r_gate{p}", [P, 2]) for p in range(2)]
        HEADS, HD, HG = 16, 8, 4
        NPART = 3
        KROWS = NPART * NPART * HD
        wx_nat = {k: sb(f"{k}_nat", [P, D]) for k in ("wq", "wk", "wv", "wo")}
        wx_T = {k: sb(f"{k}_T", [P, D]) for k in ("wq", "wk", "wv", "wo")}
        wo_pad = sb("wo_pad", [P, HG, D])
        sel_sum = sb("sel_sum", [P, P])
        sel_max = sb("sel_max", [NPART * HEADS, HEADS, P], BF16)
        mask_q = sb("mask_q", [P, HG, P], BF16)
        mask_k = sb("mask_k", [P, HG, P], BF16)
        a_in = [sb(f"a_in{p}", [P, 2, 2, D]) for p in range(2)]
        a_T = [sb(f"a_T{p}", [P, 2, 2 * S]) for p in range(2)]
        qk_part = [sb(f"qk_part{p}", [P, NPART, 2, 2 * S], BF16) for p in range(2)]
        qk_rest = sb("qk_rest", [P, 2, 2 * S])
        stack = [[sb(f"stack{p}{s_}", [KROWS, HEADS, 2 * S], BF16) for s_ in range(2)] for p in range(2)]
        v_pad = [[sb(f"v_pad{p}{j}", [P, HEADS, 32]) for j in range(2)] for p in range(2)]
        mx = [sb(f"mx{j}", [P, HEADS]) for j in range(2)]
        nm_part = [sb(f"nm_part{j}", [P, P // HEADS, HEADS], BF16) for j in range(2)]
        nm_rest = [sb(f"nm_rest{j}", [P, HEADS]) for j in range(2)]
        nm_T = [sb(f"nm_T{j}", [NPART * HEADS, P], BF16) for j in range(2)]
        pT = [sb(f"pT{j}", [P, HG, HG * P]) for j in range(2)]
        att = [sb(f"att{j}", [P, HG * P]) for j in range(2)]
        inv = [sb(f"inv{j}", [P, HG * P]) for j in range(2)]
        scr = [nc.dram_tensor(f"scr{p}", (HEADS, 5, HD, 2, 2 * S), BF16, kind="Internal").ap() for p in range(2)]

        early.close()
        own.pop()
        NE = t["L0_ffn_gate_w"].shape[0]
        F = t["L0_ffn_gate_w"].shape[1]
        FC = F // P
        TOPK = 2
        TOKENS = NB * S
        NTILE = TOKENS * TOPK // P + NE
        CAP = TOKENS + P
        PAD_ROW = NE * CAP
        WIDE = D + 2
        slots = nc.dram_tensor("slots", (PAD_ROW + P, WIDE), F32, kind="Internal").ap()
        parts = nc.dram_tensor("parts", (TOKENS * TOPK + 2 * P, D), F32, kind="Internal").ap()
        rw_nat = sb("rw_nat", [NE, D])
        rw_T = sb("rw_T", [P, NE])
        before = sb("before", [P, P], BF16)
        ones_b = sb("ones_b", [P, P], BF16)
        iota_e = sb("iota_e", [P, NE])
        e_base = sb("e_base", [P, NE])
        base = sb("base", [P, NE])
        place = sb("place", [P, NB, TOPK])
        pad_rows = sb("pad_rows", [P, WIDE])
        tile_no = sb("tile_no", [1, NTILE])
        row = [[sb(f"row{p}{k}", [P, 2, WIDE]) for k in range(TOPK)] for p in range(2)]
        x2T = [sb(f"x2T{p}", [P, 2 * S]) for p in range(2)]
        lg = [sb(f"lg{p}", [P, 2, NE]) for p in range(2)]
        top = [sb(f"top{p}", [P, 2, 8]) for p in range(2)]
        top_i = [sb(f"top_i{p}", [P, 2, 8], mybir.dt.uint32) for p in range(2)]
        ex = [sb(f"ex{p}", [P, 2, NE + 1]) for p in range(2)]
        esum = [sb(f"esum{p}", [P, 2]) for p in range(2)]
        top_f = [sb(f"top_f{p}", [P, 2, TOPK]) for p in range(2)]
        hot = [sb(f"hot{p}", [P, 2, TOPK, NE]) for p in range(2)]
        both = [sb(f"both{p}", [P, 2, NE], BF16) for p in range(2)]
        pos = [sb(f"pos{p}", [P, 2, NE]) for p in range(2)]
        picked = [sb(f"picked{p}", [P, 2, TOPK, NE]) for p in range(2)]
        slot_f = [sb(f"slot_f{p}", [P, 2 * TOPK]) for p in range(2)]
        slot_i = [sb(f"slot_i{p}", [P, 2 * TOPK], I32) for p in range(2)]
        cnt = sb("cnt", [1, NE])
        ntile = sb("ntile", [1, NE])
        start = sb("start", [1, NE + 1])
        coef = sb("coef", [1, NE - 1])
        passed = sb("passed", [1, NTILE, NE - 1])
        passed_c = sb("passed_c", [1, NTILE, NE - 1])
        tile_e = sb("tile_e", [1, NTILE])
        tile_r = sb("tile_r", [1, NTILE])
        tile_v = sb("tile_v", [1, NTILE])
        tile_col = sb("tile_col", [1, NTILE], I32)
        tile_row = sb("tile_row", [1, NTILE], I32)
        pad_at = sb("pad_at", [1, NE], I32)
        wg = [sb(f"wg{i}", [P, NE * F], F32R) for i in range(2)]
        wu = [sb(f"wu{i}", [P, NE * F], F32R) for i in range(2)]
        wd = sb("wd", [P, NE * F])
        w_nat = [sb(f"w_nat{k}", [P, FC, P]) for k in range(3)]
        xs_in = [sb(f"xs_in{q}", [P, WIDE]) for q in range(2)]
        xeh = [sb(f"xeh{q}", [P, P], F32R) for q in range(2)]
        xel = [sb(f"xel{q}", [P, P], F32R) for q in range(2)]
        sg = [sb(f"sg{q}", [P, F]) for q in range(2)]
        hid = [sb(f"hid{q}", [P, F]) for q in range(2)]
        hT = [sb(f"hT{q}", [P, F]) for q in range(2)]
        y_out = [sb(f"y_out{q}", [P, D]) for q in range(2)]
        is_pad = sb("is_pad", [P, 1])
        part_f = sb("part_f", [P, 1])
        part_i = [sb(f"part_i{q}", [P, 1], I32) for q in range(2)]
        NG = NB // 4
        y_in = [sb(f"y_in{q}", [P, TOPK, 4, D]) for q in range(2)]
        fin = [sb(f"fin{q}", [P, 4, D]) for q in range(2)]
        f_st = [sb(f"f_st{q}", [P, 4, 6]) for q in range(2)]
        f_mv = [sb(f"f_mv{q}", [P, 4, 2]) for q in range(2)]
        f_ve = [sb(f"f_ve{q}", [P, 4]) for q in range(2)]
        f_r = [sb(f"f_r{q}", [P, 4]) for q in range(2)]
        f_b = [sb(f"f_b{q}", [P, 4]) for q in range(2)]
        f_o = [sb(f"f_o{q}", [P, 4, D]) for q in range(2)]
        minus_half4 = sb("minus_half4", [P, 4])

        s_w = sem("weights_loaded")
        s_win = sem("w_in_loaded")
        s_xl = [sem(f"x_loaded{g}") for g in range(NB // 4)]
        s_pool = sem("pool_consts")
        s_prep = sem("dve_prep")
        s_aprep = sem("act_prep")
        s_cbrow = sem("conv_bias_rows")
        s_xtr = sem("x_transposed")
        s_xT = sem("xT_ready")
        s_dtps = sem("dt_psum")
        s_dt = sem("dt_ready")
        s_dtx = sem("dt_exp")
        split_hi, split_lo = sem("split_hi"), sem("split_lo")
        bc_ps, z_ps, x_ps = sem("bc_ps"), sem("z_ps"), sem2("x_ps")
        t_bc_r, z_ev, t_x_r = sem("t_bc_r"), sem("z_ev"), sem2("t_x_r")
        bc_gated, x_gated, xdt_r = sem("bc_gated"), sem2("x_gated"), sem2("xdt_r")
        ua_r, sg_ps, e_r = sem2("ua_r"), sem2("sg_ps"), sem2("e_r")
        w_raw, w_r = sem2("w_raw"), sem2("w_r")
        y_ps, y_r, sq_r = sem2("y_ps"), sem2("y_r"), sem2("sq_r")
        o_ps, o_ev = sem2("o_ps"), sem2("o_ev")
        s_out = sem("out_written")
        rg_r = sem("rg_r")
        ln_x, ln_s, ln_v, ln_r, ln_d = sem("ln_x"), sem("ln_s"), sem("ln_v"), sem("ln_r"), sem("ln_done")
        ln_e = sem("ln_e")
        s_wx = sem("attn_weights_loaded")
        s_wT = sem("attn_weights_T")
        s_wTr = sem("attn_weights_T_ready")
        s_wop = sem("wo_pad_written")
        a_ld = sem2("a_loaded")
        tr_ps, aT_r, qk_ps, qa_r, q_st, v_ps, v_r = (sem(n) for n in ("tr_ps", "aT_r", "qk_ps", "qa_r", "q_split", "v_ps", "v_r"))
        scr_w, st_ld = sem2("scratch_written"), sem2("stack_loaded")
        s_ps, red = sem2("s_ps"), sem("red")
        nm_s, nmT_ps, nmT_r = sem("nm_split"), sem("nmT_ps"), sem("nmT_r")
        t_ps, p_r, pv_ps, att_r = sem("t_ps"), sem("p_r"), sem("pv_ps"), sem("att_r")
        z2_ps, lnz, inv_r, an_r, o2_ps, o2_r = (sem(n) for n in ("z2_ps", "lnz", "inv_r", "an_r", "o2_ps", "o2_r"))

        spare_w = sem("spare_written")
        early_done = sem("early_phases_done")
        c3, rw_ld, rw_t, rw_r = sem("consts3"), sem("rw_loaded"), sem("rw_turned"), sem("rw_ready")
        pad_w, pad_d = sem("pad_row_written"), sem("pad_rows_placed")
        row_c, r_tr, r_T, r_lg = sem("row_copied"), sem("r_tr"), sem("r_T"), sem("r_logits")
        rt, r_ex, r_cnt, r_slot, sc_d = sem("rt_chain"), sem("r_ex"), sem("r_cnt"), sem("r_slot"), sem2("scattered")
        tab = sem("table_chain")
        wn_ld = [sem(f"wn_ld{k}") for k in range(3)]
        wn_tr, wn_hi, wn_free = sem("wn_tr"), sem("wn_hi"), [sem(f"wn_free{k}") for k in range(3)]
        xs_ld = sem2("xs_loaded")
        m_tr, m_hi, m_lo, m_g, m_u = (sem(n) for n in ("m_tr", "m_hi", "m_lo", "m_g", "m_u"))
        m_sg, m_hid, m_ht, m_hT, m_o, m_y, m_ix = (sem(n) for n in ("m_sg", "m_hid", "m_ht", "m_hT", "m_o", "m_y", "m_ix"))
        p_sc = sem2("parts_scattered")
        f_ld = sem2("f_loaded")
        f_c, f_v, f_rr, f_bb, f_n, f_w = sem("f_chain"), sem("f_v"), sem("f_rr"), sem("f_bb"), sem("f_n"), sem2("f_written")

        block = ctx.enter_context(nc.Block())

        def hand_over(eng):
            eng.drain().then_inc(early_done, 1)
            eng.wait_ge(early_done, 5)
        NW = 9

        def wait(eng, s, v):
            if not isinstance(v, int) or v > 0:
                eng.wait_ge(s, v)

        def wait_apart(eng, s, v, written=0):
            eng.wait_ge(s, v)
            if eng is nc.gpsimd:
                wait(eng, spare_w, written)
                nc.gpsimd.tensor_tensor(spare_pool[:, :], minus_half[0:1, 0:1], minus_half[0:1, 0:1], ALU.add).then_inc(spare_w, 1)
            else:
                nc.vector.memset(spare_dve[:, :], 0.0)

        def pairs(eng, body):
            body(0, 0, True, True, 0)
            body(1, 1, True, True, 0)
            with eng.Fori(1, NPAIR // 2 - 1) as i:
                body(i * 2, 0, True, True, i)
                body(i * 2 + 1, 1, True, True, i)
            body(NPAIR - 2, 0, True, False, NPAIR // 2 - 1)
            body(NPAIR - 1, 1, False, False, NPAIR // 2 - 1)

        @block.sync
        def _(sp):
            for g in range(2):
                sp.dma_start(x_nat[:, 4 * g:4 * g + 4, :], x_rows[:, 4 * g:4 * g + 4, :]).then_inc(s_xl[g], 16)
            sp.dma_start(w_in[:, :], t["L0_attn_W_in"]).then_inc(s_win, 16)
            sp.dma_start(cw[:, :, :].rearrange("p k c -> p (k c)"),
                         t["L0_attn_conv_w"].rearrange("k a c -> a (k c)").to_broadcast([P, TAPS * CC])).then_inc(s_w, 16)
            sp.dma_start(cb[:, :], t["L0_attn_conv_b"][None, :].to_broadcast([3, CC])).then_inc(s_w, 16)
            sp.dma_start(w_out[:, :, :], t["L0_attn_W_out"].rearrange("(h p) e -> p h e", p=P)).then_inc(s_w, 16)
            with nc.allow_non_contiguous_dma(reason="256 scales, once"):
                sp.dma_start(nscale[:, :], t["L0_attn_norm_scale"].rearrange("(h p) -> p h", p=P)).then_inc(s_w, 16)
            for dst, name in ((a_log, "A_log"), (dt_bias, "dt_bias"), (d_skip, "D")):
                sp.dma_start(dst[:, :], t["L0_attn_" + name][None, :].to_broadcast([P, NH])).then_inc(s_w, 16)
            for g in range(2, NB // 4):
                sp.dma_start(x_nat[:, 4 * g:4 * g + 4, :], x_rows[:, 4 * g:4 * g + 4, :]).then_inc(s_xl[g], 16)
            for k in ("wq", "wk", "wv", "wo"):
                sp.dma_start(wx_nat[k][:, :], t["L0_xattn_" + k]).then_inc(s_wx, 16)
            sp.wait_ge(s_wTr, 4)
            for h in range(HEADS):
                g, q = divmod(h, HG)
                sp.dma_start(wo_pad[32 * q:32 * q + HD, g, :], wx_T["wo"][HD * h:HD * h + HD, :]).then_inc(s_wop, 16)

            def load_a(n, p):
                sp.wait_ge(ln_d, n + 1)
                if not isinstance(n, int) or n >= 2:
                    sp.wait_ge(tr_ps, n - 1)
                sp.dma_start(a_in[p][:, 0, :, :], x_nat[:, bass.ds(n * 2, 2), :]).then_inc(a_ld[p], 16)
                sp.dma_start(a_in[p][:, 1, :, :], ctx_rows[:, bass.ds(n * 2, 2), :]).then_inc(a_ld[p], 16)

            def restack(n, p, k):
                sp.wait_ge(q_st, 3 * n + 3)
                w = scr[p]
                for i in range(NPART):
                    sp.dma_start(w[:, i, :, :, :].rearrange("h d a s -> h d (a s)"),
                                 qk_part[p][:, i, :, :].rearrange("q a s -> q (a s)")).then_inc(scr_w[p], 16)
                for i in range(2):
                    sp.dma_start(w[:, NPART + i, :, 1, :], qk_part[p][:, i, 1, :]).then_inc(scr_w[p], 16)
                sp.wait_ge(scr_w[p], k * 80 + 80)
                if not isinstance(n, int) or n >= 2:
                    sp.wait_ge(t_ps, 8 * n - 8)
                for s_ in range(NPART):
                    for a, first in ((0, 0), (1, s_)):
                        sp.dma_start(stack[p][a][24 * s_:24 * s_ + 24, :, :],
                                     w[:, first:first + NPART, :, a, :].rearrange("h i d s -> (i d) h s")).then_inc(st_ld[p], 16)

            load_a(0, 0)
            load_a(1, 1)
            restack(0, 0, 0)

            def body(n, p, nxt, nxt2, turn):
                if nxt:
                    restack(n + 1, 1 - p, turn + p)
                if nxt2:
                    load_a(n + 2, p)
            pairs(sp, body)
            sp.wait_ge(ln_d, 2 * NPAIR)
            hand_over(sp)
            sp.dma_start(rw_nat[:, :], t["L0_ffn_router_w"]).then_inc(rw_ld, 16)
            srcs = [t["L0_ffn_gate_w"], t["L0_ffn_up_w"], t["L0_ffn_down_w"]]

            def load_w(k, e):
                if k < 2:
                    src = srcs[k][bass.ds(e, 1), :, :].rearrange("e (c f) d -> f (e c) d", c=FC)
                else:
                    src = srcs[k][bass.ds(e, 1), :, :].rearrange("e h (c f) -> h (e c) f", c=FC)
                sp.dma_start(w_nat[k][:, :, :], src).then_inc(wn_ld[k], 16)

            for k in range(3):
                load_w(k, 0)
            with sp.Fori(0, NE - 1) as e:
                for k in range(3):
                    sp.wait_ge(wn_tr, e * 3 + k + 1)
                    load_w(k, e + 1)
            sp.wait_ge(c3, C3N)
            sp.dma_start(slots[PAD_ROW:PAD_ROW + P, :], pad_rows[:, :]).then_inc(pad_w, 16)
            sp.wait_ge(tab, TABN)
            for k in range(2):
                sp.wait_ge(sc_d[k], 16 * 4 * NPAIR // 2)
            for e in range(NE):
                at = sp.value_load(pad_at[0:1, e:e + 1], min_val=e * CAP, max_val=e * CAP + TOKENS)
                sp.dma_start(slots[bass.ds(at, P), :], pad_rows[:, :]).then_inc(pad_w, 16)
            sp.wait_ge(pad_w, 16 * NE + 16)

            def load_tile(i, q):
                at = sp.value_load(tile_row[0:1, bass.ds(i, 1)], min_val=0, max_val=PAD_ROW)
                sp.dma_start(xs_in[q][:, :], slots[bass.ds(at, P), :]).then_inc(xs_ld[q], 16)

            load_tile(0, 0)
            load_tile(1, 1)
            with sp.Fori(0, NTILE // 2 - 1) as i:
                for q in range(2):
                    sp.wait_ge(m_y, i * 2 + q + 1)
                    load_tile(i * 2 + q + 2, q)

            for q in range(2):
                sp.wait_ge(p_sc[q], 16 * NTILE // 2)
            by_token = parts[0:TOKENS * TOPK, :].rearrange("(k m s) d -> s k m d", k=TOPK, s=S)

            def load_y(g, q):
                for k in range(TOPK):
                    sp.dma_start(y_in[q][:, k, :, :], by_token[:, k, bass.ds(g * 4, 4), :]).then_inc(f_ld[q], 16)

            def store(g, q):
                sp.wait_ge(f_n, g + 1)
                sp.dma_start(out_rows[:, bass.ds(g * 4, 4), :], f_o[q][:, :, :]).then_inc(f_w[q], 16)

            load_y(0, 0)
            load_y(1, 1)
            with sp.Fori(0, NG // 2 - 1) as i:
                for q in range(2):
                    store(i * 2 + q, q)
                    load_y(i * 2 + q + 2, q)
            for q in range(2):
                store(NG - 2 + q, q)
            for q in range(2):
                sp.wait_ge(f_w[q], 16 * NG // 2)

        @block.gpsimd
        def _(pool):
            def const(tile, fills, value):
                if const.n:
                    pool.wait_ge(s_pool, const.n)
                nc.gpsimd.memset(tile, value).then_inc(s_pool, 1)
                for op, base, pattern, cm, fill in fills:
                    const.n += 1
                    pool.wait_ge(s_pool, const.n)
                    nc.gpsimd.affine_select(out=tile, in_=tile, compare_op=op, fill=fill, base=base,
                                            pattern=pattern, channel_multiplier=cm).then_inc(s_pool, 1)
                const.n += 1
            const.n = 0
            const(ident[:, :], [(ALU.not_equal, 0, [[-1, P]], 1, 1.0)], 0.0)
            const(ident_bf[:, :], [(ALU.not_equal, 0, [[-1, P]], 1, 1.0)], 0.0)
            const(after[:, :], [(ALU.is_gt, 0, [[-1, P]], 1, 0.0)], 1.0)
            const(upto[:, :, :], [(ALU.is_ge, 0, [[0, NH], [1, P]], -1, 0.0)], 1.0)
            const(future[:, :, :], [(ALU.is_gt, 0, [[0, NH], [-1, P]], 1, 0.0)], NEG)
            const(ones_f[:, :], [], 1.0)
            const(half_ones[:, :], [], 1.0)
            for p in range(2):
                const(xh[p][:, :, :].bitcast(F32), [], 0.0)
                const(xl[p][:, :, :].bitcast(F32), [], 0.0)
            const(minus_half[:, :], [], -0.5)
            const(eps_pool[:, :], [], EPS)
            for j in range(2):
                const(nm_part[j][:, :, :], [], 0.0)
            for q in range(HG):
                const(sel_sum[:, 32 * q:32 * q + 32], [(ALU.not_equal, -(32 * q + HD), [[0, 32]], 1, 1.0)], 0.0)
            const(sel_max[:, :, :], [(ALU.not_equal, -HEADS * i, [[-1, HEADS], [0, P]], 1, 1.0) for i in range(NPART)], 0.0)
            const(mask_q[:, :, :], [(ALU.is_gt, 0, [[0, HG], [1, P]], -1, 0.0)], NEG)
            const(mask_k[:, :, :], [(ALU.is_gt, 0, [[0, HG], [-1, P]], 1, 0.0)], NEG)
            const(wo_pad[:, :, :], [], 0.0)
            for p in range(2):
                for j in range(2):
                    const(v_pad[p][j][:, :, :], [], 0.0)
                    const(v_pad[p][j][:, :, HD:HD + 1], [], 1.0)
            assert const.n == POOLN, const.n

            def ua_step(n, j):
                wait(pool, sg_ps[j], n)
                nc.gpsimd.tensor_tensor(ua[j][:, :, :], upto[:, :, :],
                                        dt_a[:, bass.ds(n * 2 + j, 1), :].rearrange("p b h -> p (b h)")[:, :, None].to_broadcast([P, NH, S]),
                                        ALU.mult).then_inc(ua_r[j], 1)

            def skip_step(n, j):
                pool.wait_ge(w_raw[j], n + 1)
                nc.gpsimd.tensor_tensor(w_sb[j][:, :, :], w_sb[j][:, :, :], d_diag[:, :, :],
                                        ALU.add).then_inc(w_r[j], 1)

            pool.wait_ge(s_dt, 4)
            pool.wait_ge(s_prep, PREP)
            for j in range(2):
                ua_step(0, j)

            def rms_step(n, p):
                pool.wait_ge(o_ev[1], n + 1)
                nc.gpsimd.tensor_tensor(r_gate[p][:, :], ss_eps[p][:, :], minus_half[:, :], ALU.pow).then_inc(rg_r, 1)

            def ln_rstd(n, p, base):
                pool.wait_ge(ln_v, (n + base) * 2 + 2)
                nc.gpsimd.tensor_tensor(v_eps[p][:, :], mv[p][:, :, 1], eps_pool[:, :], ALU.add).then_inc(ln_e, 1)
                pool.wait_ge(ln_e, n + base + 1)
                nc.gpsimd.tensor_tensor(r_ln[p][:, :], v_eps[p][:, :], minus_half[:, :], ALU.pow).then_inc(ln_r, 1)

            def body(n, p, nxt, nxt2, turn):
                for j in range(2):
                    if nxt:
                        ua_step(n + 1, j)
                    skip_step(n, j)
                rms_step(n, p)
                ln_rstd(n, p, 0)
            pairs(pool, body)

            def body(n, p, nxt, nxt2, turn):
                ln_rstd(n, p, NPAIR)
            pairs(pool, body)
            hand_over(pool)
            made = [0]

            def const3(ins):
                made[0] += 1
                ins.then_inc(c3, 1)

            def sel3(tile, op, base_, pattern, fill):
                pool.wait_ge(c3, made[0])
                const3(nc.gpsimd.affine_select(out=tile, in_=tile, compare_op=op, fill=fill, base=base_, pattern=pattern,
                                               channel_multiplier=-1))
            const3(nc.gpsimd.memset(before[:, :], 1.0))
            sel3(before[:, :], ALU.is_gt, 0, [[1, P]], 0.0)
            const3(nc.gpsimd.memset(ones_b[:, :], 1.0))
            const3(nc.gpsimd.iota(iota_e[:, :], pattern=[[1, NE]], base=0, channel_multiplier=0, allow_small_or_imprecise_dtypes=True))
            const3(nc.gpsimd.iota(e_base[:, :], pattern=[[CAP, NE]], base=0, channel_multiplier=0, allow_small_or_imprecise_dtypes=True))
            const3(nc.gpsimd.iota(base[:, :], pattern=[[CAP, NE]], base=0, channel_multiplier=0, allow_small_or_imprecise_dtypes=True))
            const3(nc.gpsimd.iota(place[:, :, :], pattern=[[S, NB], [TOKENS, TOPK]], base=0, channel_multiplier=1, allow_small_or_imprecise_dtypes=True))
            const3(nc.gpsimd.memset(pad_rows[:, 0:D + 1], 0.0))
            const3(nc.gpsimd.iota(pad_rows[:, D + 1:D + 2], pattern=[[0, 1]], base=TOKENS * TOPK, channel_multiplier=1, allow_small_or_imprecise_dtypes=True))
            const3(nc.gpsimd.iota(tile_no[:, :], pattern=[[1, NTILE]], base=0, channel_multiplier=0, allow_small_or_imprecise_dtypes=True))
            const3(nc.gpsimd.memset(minus_half4[:, :], -0.5))
            assert made[0] == C3N

            def scatter(n, p, j, k):
                if j == 0 and k == 0:
                    pool.wait_ge(r_slot, n + 1)
                    wait_apart(pool, row_c, n + 1, n)
                nc.gpsimd.indirect_dma_start(out=slots, out_offset=bass.IndirectOffsetOnAxis(ap=slot_i[p][:, 2 * j + k:2 * j + k + 1], axis=0),
                                             in_=row[p][k][:, j, :], in_offset=None).then_inc(sc_d[p], 16)

            def body(n, p, nxt, nxt2, turn):
                for j in range(2):
                    for k in range(TOPK):
                        scatter(n, p, j, k)
            pairs(pool, body)

            with pool.Fori(0, NTILE // 2) as i:
                for q in range(2):
                    wait_apart(pool, m_y, i * 2 + q + 1, i * 2 + q + NPAIR)
                    nc.gpsimd.indirect_dma_start(out=parts, out_offset=bass.IndirectOffsetOnAxis(ap=part_i[q][:, 0:1], axis=0),
                                                 in_=y_out[q][:, :], in_offset=None).then_inc(p_sc[q], 16)
            with pool.Fori(0, NG // 2) as i:
                for q in range(2):
                    pool.wait_ge(f_v, i * 2 + q + 1)
                    nc.gpsimd.tensor_tensor(f_r[q][:, :], f_ve[q][:, :], minus_half4[:, :], ALU.pow).then_inc(f_rr, 1)

        def dt_products(pe, g):
            pe.wait_ge(s_xT, g + 1)
            for k in range(4):
                m = 4 * g + k
                last = pe.matmul(bank[2][:, NH * m:NH * m + NH], xT[:, m, :], w_in[:, DTC:DTC + NH], start=True, stop=True)
            last.then_inc(s_dtps, 1)

        @block.tensor
        def _(pe):
            pe.wait_ge(s_pool, 10)
            for g in range(NB // 4):
                pe.wait_ge(s_xl[g], 16)
                if g >= 2:
                    pe.wait_ge(s_xT, g - 1)
                for k in range(4):
                    last = pe.transpose(bank[g % 2][:, k * P:(k + 1) * P], x_nat[:, 4 * g + k, :], ident[:, :])
                last.then_inc(s_xtr, 1)
                if g == 0:
                    pe.wait_ge(s_win, 16)
                if g >= 1:
                    dt_products(pe, g - 1)
            dt_products(pe, NB // 4 - 1)

            pe.wait_ge(s_prep, PREP)
            pe.wait_ge(s_pool, POOLN)
            pe.wait_ge(s_dt, 1)

            pe.wait_ge(s_cbrow, 1)

            def front_bc(n, p):
                pe.wait_ge(split_lo, n + 1)
                wait(pe, bc_gated, n)
                o = bank[0][:, 0:2 * S]
                pe.matmul(o, cb_rows[:, DI:CC], half_ones[:, :], start=True, stop=False)
                for k in range(TAPS):
                    for wt, xx in ((wconv_h, xh), (wconv_h, xl), (wconv_l, xh)):
                        last = pe.matmul(o, wt[:, k, DI:CC], xx[p][:, :, k:k + S], start=False,
                                         stop=(k == TAPS - 1 and wt is wconv_l))
                last.then_inc(bc_ps, 1)

            def front_z(n, p):
                wait(pe, z_ev, n)
                for h in range(NH):
                    o = bank[1][:, h * 2 * S:(h + 1) * 2 * S]
                    for q, (wt, xx) in enumerate(((wz_h, xh), (wz_h, xl), (wz_l, xh))):
                        last = pe.matmul(o, wt[:, h * P:(h + 1) * P], xx[p][:, :, TAPS - 1:TAPS - 1 + S],
                                         start=(q == 0), stop=(q == 2))
                last.then_inc(z_ps, 1)

            def front_x(n, p, j):
                wait(pe, x_gated[j], n)
                o = bank[2 + j][:, 0:DI]
                pe.matmul(o, half_ones[:, 0:P], cb_rows[:, 0:DI], start=True, stop=False)
                for k in range(TAPS):
                    for xx, wt in ((xh, wconv_h), (xl, wconv_h), (xh, wconv_l)):
                        last = pe.matmul(o, xx[p][:, j, k:k + S], wt[:, k, 0:DI], start=False,
                                         stop=(k == TAPS - 1 and wt is wconv_l))
                last.then_inc(x_ps[j], 1)

            def seg(n, p, j):
                pe.wait_ge(bc_gated, n + 1)
                pe.wait_ge(ua_r[j], n + 1)
                wait(pe, w_raw[j], n)
                b = bank[4 + j]
                pe.matmul(b[:, 0:S], b_sb[p][:, j * S:(j + 1) * S], c_sb[p][:, j * S:(j + 1) * S], start=True, stop=True)
                o = b[:, S:S + NH * S]
                pe.matmul(o, ident_bf[:, :], future[:, :, :], start=True, stop=False)
                pe.matmul(o, after[:, :], ua[j][:, :, :], start=False, stop=True).then_inc(sg_ps[j], 1)

            def yy(n, p, j):
                pe.wait_ge(w_r[j], n + 1)
                pe.wait_ge(xdt_r[j], n + 1)
                if j == 0:
                    wait(pe, y_r[1], n)
                else:
                    pe.wait_ge(y_r[0], n + 1)
                for h in range(NH):
                    last = pe.matmul(bank[6][:, h * S:(h + 1) * S], xdt[p][j][:, h * P:(h + 1) * P],
                                     w_sb[j][:, h, :], start=True, stop=True)
                last.then_inc(y_ps[j], 1)

            def oo(n, p, j):
                pe.wait_ge(sq_r[j], n + 1)
                if j == 0:
                    wait(pe, o_ev[1], n)
                else:
                    pe.wait_ge(o_ev[0], n + 1)
                for h in range(NH):
                    pe.matmul(bank[7][:, 0:D], y_sb[j][:, h, :], w_out[:, h, :], start=(h == 0), stop=(h == 1))
                for h in range(NH):
                    last = pe.matmul(bank[7][:, D:D + 1], sq_sb[j][:, h, :], ones_f[:, :], start=(h == 0), stop=(h == 1))
                last.then_inc(o_ps[j], 1)

            front_bc(0, 0)
            front_z(0, 0)
            front_x(0, 0, 0)
            front_x(0, 0, 1)

            def body(n, p, nxt, nxt2, turn):
                seg(n, p, 0)
                if nxt:
                    front_bc(n + 1, 1 - p)
                seg(n, p, 1)
                if nxt:
                    front_z(n + 1, 1 - p)
                yy(n, p, 0)
                if nxt:
                    front_x(n + 1, 1 - p, 0)
                yy(n, p, 1)
                oo(n, p, 0)
                if nxt:
                    front_x(n + 1, 1 - p, 1)
                oo(n, p, 1)
            pairs(pe, body)

            pe.wait_ge(s_wx, 64)
            for k, name in enumerate(("wq", "wk", "wv", "wo")):
                last = pe.transpose(bank[0][:, k * P:(k + 1) * P], wx_nat[name][:, :], ident[:, :])
            last.then_inc(s_wT, 4)
            def front_tr(n, p, k):
                pe.wait_ge(a_ld[p], k * 32 + 32)
                wait(pe, v_r, n)
                for a in range(2):
                    for j in range(2):
                        last = pe.transpose(bank[0][:, (2 * a + j) * P:(2 * a + j + 1) * P], a_in[p][:, a, j, :], ident[:, :])
                last.then_inc(tr_ps, 1)

            def front_qk(n, p):
                pe.wait_ge(aT_r, n + 1)
                wait(pe, q_st, 3 * n)
                for a, name in ((0, "wq"), (1, "wk")):
                    last = pe.matmul(bank[1][:, a * 2 * S:(a + 1) * 2 * S], wx_T[name][:, :], a_T[p][:, a, :], start=True, stop=True)
                last.then_inc(qk_ps, 1)

            def front_v(n, p):
                for j in range(2):
                    last = pe.matmul(bank[0][:, j * P:(j + 1) * P], a_T[p][:, 1, j * S:(j + 1) * S], wx_T["wv"][:, :], start=True, stop=True)
                last.then_inc(v_ps, 1)

            def scores(n, p, j, g, k):
                m = n * 2 + j
                if g == 0:
                    pe.wait_ge(st_ld[p], k * 96 + 96)
                    wait(pe, nmT_r, m)
                if g >= 2:
                    pe.wait_ge(red, m * 4 + g - 1)
                elif g == 1:
                    wait(pe, red, m * 4)
                b = bank[2 + g % 2]
                pe.matmul(b[:, :], ident_bf[:, :], mask_q[:, :, :], start=True, stop=False)
                for q in range(HG):
                    h = HG * g + q
                    last = pe.matmul(b[:, q * P:(q + 1) * P], stack[p][0][:, h, j * S:(j + 1) * S], stack[p][1][:, h, j * S:(j + 1) * S],
                                     start=False, stop=(q == HG - 1))
                last.then_inc(s_ps[g % 2], 1)

            def turn_max(n, j):
                m = n * 2 + j
                pe.wait_ge(nm_s, m * 4 + 4)
                pe.transpose(bank[2][:, 0:P // 2].bitcast(BF16), nm_part[j][:, :, :].rearrange("p i h -> p (i h)"),
                             ident_bf[:, :]).then_inc(nmT_ps, 1)

            def scores_T(n, p, j, g):
                m = n * 2 + j
                if g == 0:
                    pe.wait_ge(nmT_r, m + 1)
                if g >= 2:
                    pe.wait_ge(p_r, m * 4 + g - 1)
                else:
                    wait(pe, p_r, m * 4)
                b = bank[4 + g % 2]
                pe.matmul(b[:, :], ident_bf[:, :], mask_k[:, :, :], start=True, stop=False)
                for q in range(HG):
                    h = HG * g + q
                    o = b[:, q * P:(q + 1) * P]
                    pe.matmul(o, stack[p][1][:, h, j * S:(j + 1) * S], stack[p][0][:, h, j * S:(j + 1) * S], start=False, stop=False)
                    last = pe.matmul(o, sel_max[:, h, :], nm_T[j][:, :], start=False, stop=(q == HG - 1))
                last.then_inc(t_ps, 1)

            def values(n, p, j, g):
                m = n * 2 + j
                pe.wait_ge(p_r, m * 4 + g + 1)
                if g == 0:
                    pe.wait_ge(v_r, n + 1)
                    wait(pe, att_r, m)
                for q in range(HG):
                    last = pe.matmul(bank[6][32 * q:32 * q + 32, g * P:(g + 1) * P], v_pad[p][j][:, HG * g + q, :],
                                     pT[j][:, g, q * P:(q + 1) * P], start=True, stop=True)
                if g == HG - 1:
                    last.then_inc(pv_ps, 1)

            def sums(n, j):
                m = n * 2 + j
                pe.wait_ge(att_r, m + 1)
                wait(pe, ln_x, (m + NPAIR * 2))
                pe.matmul(bank[7][:, :], sel_sum[:, :], att[j][:, :], start=True, stop=True).then_inc(z2_ps, 1)

            def out_proj(n, j):
                m = n * 2 + j
                pe.wait_ge(an_r, m + 1)
                for g in range(HG):
                    last = pe.matmul(bank[7][:, 0:D], att[j][:, g * P:(g + 1) * P], wo_pad[:, g, :], start=(g == 0), stop=(g == HG - 1))
                last.then_inc(o2_ps, 1)

            pe.wait_ge(s_wTr, 4)
            pe.wait_ge(s_wop, 16 * HEADS)
            front_tr(0, 0, 0)
            front_qk(0, 0)
            front_v(0, 0)
            for g in range(HG):
                scores(0, 0, 0, g, 0)
            turn_max(0, 0)

            def body(n, p, nxt, nxt2, turn):
                if nxt:
                    front_tr(n + 1, 1 - p, turn + p)
                for g in range(HG):
                    scores_T(n, p, 0, g)
                    if g == 0 and nxt:
                        front_qk(n + 1, 1 - p)
                        front_v(n + 1, 1 - p)
                    scores(n, p, 1, g, turn)
                    if g:
                        values(n, p, 0, g - 1)
                values(n, p, 0, 3)
                turn_max(n, 1)
                sums(n, 0)
                for g in range(HG):
                    scores_T(n, p, 1, g)
                    if g == 1:
                        out_proj(n, 0)
                    if nxt:
                        scores(n + 1, 1 - p, 0, g, turn + p)
                    if g:
                        values(n, p, 1, g - 1)
                values(n, p, 1, 3)
                if nxt:
                    turn_max(n + 1, 0)
                sums(n, 1)
                out_proj(n, 1)
            pairs(pe, body)
            pe.wait_ge(ln_d, 2 * NPAIR)
            hand_over(pe)
            pe.wait_ge(rw_ld, 16)
            pe.transpose(bank[0][:, 0:NE], rw_nat[:, :], ident[0:NE, 0:NE]).then_inc(rw_t, 1)
            with pe.Fori(0, NE) as e:
                for k in range(3):
                    pe.wait_ge(wn_ld[k], e * 16 + 16)
                    pe.wait_ge(wn_free[k], e + 1)
                    for c in range(FC):
                        last = pe.transpose(bank[1 + k][:, c * P:(c + 1) * P], w_nat[k][:, c, :], ident[:, :])
                    last.then_inc(wn_tr, 1)

            pe.wait_ge(rw_r, 1)
            pe.wait_ge(c3, C3N)

            def body(n, p, nxt, nxt2, turn):
                pe.wait_ge(row_c, n + 1)
                for j in range(2):
                    last = pe.transpose(bank[4][:, j * P:(j + 1) * P], row[p][0][:, j, 0:D], ident[:, :])
                last.then_inc(r_tr, 1)
                pe.wait_ge(r_T, n + 1)
                for j in range(2):
                    last = pe.matmul(bank[5][:, j * NE:(j + 1) * NE], x2T[p][:, j * S:(j + 1) * S], rw_T[:, :], start=True, stop=True)
                last.then_inc(r_lg, 1)
                pe.wait_ge(rt, n * RT + 8)
                pe.matmul(bank[6][:, 0:NE], before[:, :], both[p][:, 0, :], start=True, stop=True)
                pe.matmul(bank[6][:, NE:2 * NE], before[:, :], both[p][:, 1, :], start=True, stop=False)
                pe.matmul(bank[6][:, NE:2 * NE], ones_b[:, :], both[p][:, 0, :], start=False, stop=True)
                pe.matmul(bank[6][:, 2 * NE:3 * NE], ones_b[:, :], both[p][:, 0, :], start=True, stop=False)
                pe.matmul(bank[6][:, 2 * NE:3 * NE], ones_b[:, :], both[p][:, 1, :], start=False, stop=True).then_inc(r_cnt, 1)
            pairs(pe, body)

            pe.wait_ge(tab, TABN)

            def turn_tile(i, q, turn):
                pe.wait_ge(xs_ld[q], turn * 16 + 16)
                wait(pe, m_lo, i)
                pe.transpose(bank[0][:, 0:P], xs_in[q][:, 0:D], ident[:, :]).then_inc(m_tr, 1)

            def gate_up(i, q):
                col = pe.value_load(tile_col[0:1, bass.ds(i, 1)], min_val=0, max_val=(NE - 1) * F)
                pe.wait_ge(m_lo, i + 1)
                for w, b, s_, free, in ((wg, bank[1], m_g, m_sg), (wu, bank[2], m_u, m_hid)):
                    wait(pe, free, i)
                    for z_, (xx, part) in enumerate(((xeh, 0), (xel, 0), (xeh, 1))):
                        last = pe.matmul(b[:, :], xx[q][:, :], w[part][:, bass.ds(col, F)], start=(z_ == 0), stop=(z_ == 2))
                    last.then_inc(s_, 1)

            def turn_hid(i, q):
                pe.wait_ge(m_hid, i + 1)
                wait(pe, m_hT, i)
                for c in range(FC):
                    last = pe.transpose(bank[3][:, c * P:(c + 1) * P], hid[q][:, c * P:(c + 1) * P], ident[:, :])
                last.then_inc(m_ht, 1)

            def down(i, q):
                col = pe.value_load(tile_col[0:1, bass.ds(i, 1)], min_val=0, max_val=(NE - 1) * F)
                pe.wait_ge(m_hT, i + 1)
                wait(pe, m_y, i)
                for c in range(FC):
                    last = pe.matmul(bank[4][:, 0:D], hT[q][:, c * P:(c + 1) * P], wd[:, bass.ds(col + c * P, P)],
                                     start=(c == 0), stop=(c == FC - 1))
                last.then_inc(m_o, 1)

            def tiles(eng, first, body):
                first()
                body(0, 0, True, 0)
                body(1, 1, True, 0)
                with eng.Fori(1, NTILE // 2 - 1) as i:
                    body(i * 2, 0, True, i)
                    body(i * 2 + 1, 1, True, i)
                body(NTILE - 2, 0, True, NTILE // 2 - 1)
                body(NTILE - 1, 1, False, NTILE // 2 - 1)

            def first():
                turn_tile(0, 0, 0)
                gate_up(0, 0)

            def body(i, q, nxt, turn):
                if nxt:
                    turn_tile(i + 1, 1 - q, turn + q)
                turn_hid(i, q)
                if nxt:
                    gate_up(i + 1, 1 - q)
                down(i, q)
            tiles(pe, first, body)

        @block.scalar
        def _(act):
            nc.scalar.preload_act_table_set("natural_log_exp_and_others")
            for g in range(NB // 4):
                act.wait_ge(s_xtr, g + 1)
                nc.scalar.activation(xT[:, 4 * g:4 * g + 4, :], bank[g % 2][:, :].rearrange("p (b s) -> p b s", b=4),
                                     ACT.Copy).then_inc(s_xT, 1)
            act.wait_ge(s_w, 16 * 7)
            nc.scalar.activation(a_neg[:, :], a_log[:, :], ACT.Exp).then_inc(s_aprep, 1)
            act.wait_ge(s_dt, 1)
            nc.scalar.activation(dt_e[:, :, :], dt_v[:, :, :], ACT.Abs).then_inc(s_dtx, 1)
            act.wait_ge(s_dtx, 1)
            nc.scalar.activation(dt_e[:, :, :], dt_e[:, :, :], ACT.Exp, scale=-1.0).then_inc(s_dtx, 1)
            act.wait_ge(s_dtx, 2)
            nc.scalar.activation(dt_e[:, :, :], dt_e[:, :, :], ACT.Ln, bias=1.0).then_inc(s_dtx, 1)
            nc.scalar.preload_act_table_set("exp_and_others")

            def hi(n, p):
                if not isinstance(n, int) or n >= 2:
                    act.wait_ge(x_ps[1], n - 1)
                nc.scalar.activation(xh[p][:, :, TAPS - 1:TAPS - 1 + S], xT[:, bass.ds(n * 2, 2), :], ACT.Copy).then_inc(split_hi, 1)

            def tanh_bc(n):
                act.wait_ge(bc_ps, n + 1)
                nc.scalar.activation(t_bc[:, :], bank[0][:, 0:2 * S], ACT.Tanh, scale=0.5).then_inc(t_bc_r, 1)

            def z_copy(n, p):
                act.wait_ge(z_ps, n + 1)
                if not isinstance(n, int) or n >= 2:
                    act.wait_ge(y_r[1], n - 1)
                nc.scalar.activation(z_sb[p][:, :, :].rearrange("p h s -> p (h s)"), bank[1][:, :], ACT.Copy).then_inc(z_ev, 1)

            def tanh_x(n, j):
                act.wait_ge(x_ps[j], n + 1)
                nc.scalar.activation(t_x[j][:, :], bank[2 + j][:, 0:DI], ACT.Tanh, scale=0.5).then_inc(t_x_r[j], 1)

            def xdt_step(n, p, j):
                act.wait_ge(x_gated[j], n + 1)
                if not isinstance(n, int) or n >= 2:
                    act.wait_ge(y_ps[j], n - 1)
                for h in range(NH):
                    last = nc.scalar.activation(xdt[p][j][:, h * P:(h + 1) * P], x_s[j][:, h * P:(h + 1) * P], ACT.Copy,
                                                scale=dt_half[:, bass.ds(n * 2 + j, 1), h])
                last.then_inc(xdt_r[j], 1)

            def e_step(n, j):
                act.wait_ge(sg_ps[j], n + 1)
                wait(act, w_raw[j], n)
                nc.scalar.activation(e_sb[j][:, :, :].rearrange("p h s -> p (h s)"), bank[4 + j][:, S:S + NH * S],
                                     ACT.Exp).then_inc(e_r[j], 1)

            def sq_step(n, j):
                act.wait_ge(y_r[j], n + 1)
                wait(act, o_ps[j], n)
                nc.scalar.activation(sq_sb[j][:, :, :], y_sb[j][:, :, :], ACT.Square, scale=1.0 / 16).then_inc(sq_r[j], 1)

            act.wait_ge(s_pool, POOLN)
            act.wait_ge(s_dt, 4)
            hi(0, 0)
            hi(1, 1)
            tanh_bc(0)
            z_copy(0, 0)
            for j in range(2):
                tanh_x(0, j)
                xdt_step(0, 0, j)

            def body(n, p, nxt, nxt2, turn):
                e_step(n, 0)
                if nxt:
                    tanh_bc(n + 1)
                e_step(n, 1)
                if nxt:
                    z_copy(n + 1, 1 - p)
                sq_step(n, 0)
                if nxt:
                    tanh_x(n + 1, 0)
                    xdt_step(n + 1, 1 - p, 0)
                sq_step(n, 1)
                if nxt2:
                    hi(n + 2, p)
                if nxt:
                    tanh_x(n + 1, 1)
                    xdt_step(n + 1, 1 - p, 1)
            pairs(act, body)
            for k, name in enumerate(("wq", "wk", "wv", "wo")):
                act.wait_ge(s_wT, 4)
                nc.scalar.activation(wx_T[name][:, :], bank[0][:, k * P:(k + 1) * P], ACT.Copy).then_inc(s_wTr, 1)
            nc.scalar.preload_act_table_set("natural_log_exp_and_others")

            def copy_aT(n, p):
                act.wait_ge(tr_ps, n + 1)
                nc.scalar.activation(a_T[p][:, :, :].rearrange("p a s -> p (a s)"), bank[0][:, :], ACT.Copy).then_inc(aT_r, 1)

            def first_part(n, p, k):
                act.wait_ge(qk_ps, n + 1)
                if not isinstance(n, int) or n >= 2:
                    act.wait_ge(scr_w[p], k * 80)
                nc.scalar.activation(qk_part[p][:, 0, :, :].rearrange("p a s -> p (a s)"), bank[1][:, :], ACT.Copy).then_inc(qa_r, 1)

            def copy_v(n, p):
                act.wait_ge(v_ps, n + 1)
                for j in range(2):
                    last = nc.scalar.activation(v_pad[p][j][:, :, 0:HD],
                                                bank[0][:, j * P:(j + 1) * P].rearrange("p (h d) -> p h d", d=HD), ACT.Copy)
                last.then_inc(v_r, 1)

            def exps(n, j, g):
                m = n * 2 + j
                act.wait_ge(t_ps, m * 4 + g + 1)
                nc.scalar.activation(pT[j][:, g, :], bank[4 + g % 2][:, :], ACT.Exp, scale=HD ** -0.5).then_inc(p_r, 1)

            def copy_att(n, j):
                m = n * 2 + j
                act.wait_ge(pv_ps, m + 1)
                nc.scalar.activation(att[j][:, :], bank[6][:, :], ACT.Copy).then_inc(att_r, 1)

            def invert(n, j):
                m = n * 2 + j
                act.wait_ge(z2_ps, m + 1)
                nc.scalar.activation(inv[j][:, :], bank[7][:, :], ACT.Ln).then_inc(lnz, 1)
                act.wait_ge(lnz, m + 1)
                nc.scalar.activation(inv[j][:, :], inv[j][:, :], ACT.Exp, scale=-1.0).then_inc(inv_r, 1)

            copy_aT(0, 0)
            first_part(0, 0, 0)
            copy_v(0, 0)

            def body(n, p, nxt, nxt2, turn):
                if nxt:
                    copy_aT(n + 1, 1 - p)
                for g in range(HG):
                    exps(n, 0, g)
                    if g == 0 and nxt:
                        first_part(n + 1, 1 - p, turn + p)
                if nxt:
                    copy_v(n + 1, 1 - p)
                copy_att(n, 0)
                invert(n, 0)
                for g in range(HG):
                    exps(n, 1, g)
                copy_att(n, 1)
                invert(n, 1)
            pairs(act, body)
            hand_over(act)
            act.wait_ge(rw_t, 1)
            nc.scalar.activation(rw_T[:, :], bank[0][:, 0:NE], ACT.Copy).then_inc(rw_r, 1)
            act.nop().then_inc(wn_free[2], 1)
            with act.Fori(0, NE) as e:
                for k, dst in enumerate((wg[0], wu[0], wd)):
                    act.wait_ge(wn_tr, e * 3 + k + 1)
                    nc.scalar.activation(dst[:, bass.ds(e * F, F)], bank[1 + k][:, :], ACT.Copy).then_inc(wn_hi if k < 2 else wn_free[2], 1)

            act.wait_ge(c3, C3N)

            def copy_row(n, p, turn):
                if not isinstance(n, int) or n >= 2:
                    act.wait_ge(sc_d[p], turn * 64)
                for k in range(TOPK):
                    nc.scalar.activation(row[p][k][:, :, 0:D], x_nat[:, bass.ds(n * 2, 2), :], ACT.Copy)
                    last = nc.scalar.activation(row[p][k][:, :, D + 1], place[:, bass.ds(n * 2, 2), k], ACT.Copy)
                last.then_inc(row_c, 1)
            copy_row(0, 0, 0)

            def body(n, p, nxt, nxt2, turn):
                if nxt:
                    copy_row(n + 1, 1 - p, turn + p)
                act.wait_ge(r_tr, n + 1)
                nc.scalar.activation(x2T[p][:, :], bank[4][:, 0:2 * S], ACT.Copy).then_inc(r_T, 1)
                act.wait_ge(rt, n * RT + 5)
                nc.scalar.activation(ex[p][:, :, :], ex[p][:, :, :], ACT.Exp).then_inc(r_ex, 1)
            pairs(act, body)

            nc.scalar.preload_act_table_set("silu_and_others")

            def hi_tile(i, q):
                act.wait_ge(m_tr, i + 1)
                if not isinstance(i, int) or i >= 2:
                    act.wait_ge(m_u, i - 1)
                nc.scalar.activation(xeh[q][:, :], bank[0][:, 0:P], ACT.Copy).then_inc(m_hi, 1)

            def silu(i, q):
                act.wait_ge(m_g, i + 1)
                if not isinstance(i, int) or i >= 2:
                    act.wait_ge(m_hid, i - 1)
                nc.scalar.activation(sg[q][:, :], bank[1][:, :], ACT.Silu).then_inc(m_sg, 1)

            def copy_hT(i, q):
                act.wait_ge(m_ht, i + 1)
                if not isinstance(i, int) or i >= 2:
                    act.wait_ge(m_o, i - 1)
                nc.scalar.activation(hT[q][:, :], bank[3][:, :], ACT.Copy).then_inc(m_hT, 1)

            hi_tile(0, 0)
            silu(0, 0)
            hi_tile(1, 1)
            copy_hT(0, 0)
            silu(1, 1)
            def turn_of_tiles(i):
                for q in range(2):
                    hi_tile(i * 2 + 2 + q, q)
                    copy_hT(i * 2 + 1 + q, 1 - q)
                    silu(i * 2 + 2 + q, q)
            turn_of_tiles(0)
            with act.Fori(1, NTILE // 2 - 1) as i:
                turn_of_tiles(i)
            copy_hT(NTILE - 1, 1)

            def norm(g, q, turn):
                act.wait_ge(f_bb, g + 1)
                wait(act, f_w[q], turn * 16)
                for b in range(4):
                    last = nc.scalar.activation(f_o[q][:, b, :], fin[q][:, b, :], ACT.Identity, bias=f_b[q][:, b:b + 1],
                                                scale=f_r[q][:, b:b + 1])
                last.then_inc(f_n, 1)
            for q in range(2):
                norm(q, q, 0)
            with act.Fori(1, NG // 2) as i:
                for q in range(2):
                    norm(i * 2 + q, q, i)

        @block.vector
        def _(dve):
            made = [0]

            def prep(ins):
                made[0] += 1
                ins.then_inc(s_prep, 1)
                dve.wait_ge(s_prep, made[0])

            dve.wait_ge(s_w, 16 * 7)
            dve.wait_ge(s_win, 16)
            dve.wait_ge(s_pool, 10)
            prep(nc.vector.tensor_copy(wz_h[:, :], w_in[:, 0:DI]))
            prep(nc.vector.tensor_tensor(wz_l[:, :], w_in[:, 0:DI], wz_h[:, :].bitcast(F32), ALU.subtract))
            for k in range(TAPS):
                prep(nc.vector.tensor_tensor(wconv[:, k, :], cw[:, k, :], w_in[:, ZX:ZX + CC], ALU.mult))
            prep(nc.vector.tensor_copy(cb_part[0][:, :], cb[:, :]))
            prep(nc.vector.tensor_copy(wconv_h[:, :, :], wconv[:, :, :]))
            prep(nc.vector.tensor_tensor(wconv_l[:, :, :], wconv[:, :, :], wconv_h[:, :, :].bitcast(F32), ALU.subtract))
            prep(nc.vector.tensor_tensor(cb_rest[:, :], cb[:, :], cb_part[0][:, :], ALU.subtract))
            prep(nc.vector.tensor_copy(cb_part[1][:, :], cb_rest[:, :]))
            prep(nc.vector.tensor_tensor(cb_part[2][:, :], cb_rest[:, :], cb_part[1][:, :], ALU.subtract))
            prep(nc.vector.tensor_scalar(cb_rows[:, :], cb_part[0][:, :], ident[0:3, 0:1], None, ALU.mult))
            for i in (1, 2):
                prep(nc.vector.scalar_tensor_tensor(out=cb_rows[:, :], in0=cb_part[i][:, :], scalar=ident[0:3, i:i + 1],
                                                    in1=cb_rows[:, :], op0=ALU.mult, op1=ALU.add))
            nc.vector.nop().then_inc(s_cbrow, 1)
            for h in range(NH):
                prep(nc.vector.tensor_scalar(w_out[:, h, :], w_out[:, h, :], nscale[:, h:h + 1], None, ALU.mult))
                prep(nc.vector.tensor_scalar(d_diag[:, h, :], ident[:, :], d_skip[:, h:h + 1], None, ALU.mult))
            assert made[0] == PREP, made[0]
            dve.wait_ge(s_dtps, NB // 4)
            nc.vector.tensor_tensor(dt_v[:, :, :], bank[2][:, 0:NB * NH].rearrange("p (b h) -> p b h", h=NH),
                                    dt_bias[:, None, :].to_broadcast([P, NB, NH]), ALU.add).then_inc(s_dt, 1)
            dve.wait_ge(s_dtx, 3)
            nc.vector.scalar_tensor_tensor(out=dt_v[:, :, :], in0=dt_v[:, :, :], scalar=0.0, in1=dt_e[:, :, :],
                                           op0=ALU.max, op1=ALU.add).then_inc(s_dt, 1)
            dve.wait_ge(s_dt, 2)
            nc.vector.tensor_scalar(dt_half[:, :, :], dt_v[:, :, :], 0.5, None, ALU.mult).then_inc(s_dt, 1)
            dve.wait_ge(s_aprep, 1)
            nc.vector.scalar_tensor_tensor(out=dt_a[:, :, :], in0=dt_v[:, :, :], scalar=-1.0,
                                           in1=a_neg[:, None, :].to_broadcast([P, NB, NH]), op0=ALU.mult,
                                           op1=ALU.mult).then_inc(s_dt, 1)

            def lo(n, p):
                dve.wait_ge(split_hi, n + 1)
                nc.vector.tensor_tensor(xl[p][:, :, TAPS - 1:TAPS - 1 + S], xT[:, bass.ds(n * 2, 2), :],
                                        xh[p][:, :, TAPS - 1:TAPS - 1 + S].bitcast(F32), ALU.subtract).then_inc(split_lo, 1)

            def gate_bc(n, p):
                dve.wait_ge(t_bc_r, n + 1)
                if not isinstance(n, int) or n >= 2:
                    dve.wait_ge(sg_ps[1], n - 1)
                for half, dst in ((0, b_sb[p]), (NS, c_sb[p])):
                    last = nc.vector.scalar_tensor_tensor(out=dst[:, :], in0=t_bc[half:half + NS, :], scalar=1.0,
                                                          in1=bank[0][half:half + NS, 0:2 * S], op0=ALU.add, op1=ALU.mult)
                last.then_inc(bc_gated, 1)

            def gate_x(n, j):
                dve.wait_ge(t_x_r[j], n + 1)
                wait(dve, xdt_r[j], n)
                nc.vector.scalar_tensor_tensor(out=x_s[j][:, :], in0=t_x[j][:, :], scalar=1.0, in1=bank[2 + j][:, 0:DI],
                                               op0=ALU.add, op1=ALU.mult).then_inc(x_gated[j], 1)

            def w_step(n, j):
                dve.wait_ge(e_r[j], n + 1)
                wait(dve, y_ps[j], n)
                nc.vector.scalar_tensor_tensor(out=w_sb[j][:, :, :], in0=e_sb[j][:, :, :], scalar=0.25,
                                               in1=bank[4 + j][:, None, 0:S].to_broadcast([P, NH, S]),
                                               op0=ALU.mult, op1=ALU.mult).then_inc(w_raw[j], 1)

            def y_step(n, p, j):
                dve.wait_ge(y_ps[j], n + 1)
                dve.wait_ge(z_ev, n + 1)
                wait(dve, o_ps[j], n)
                wait(dve, sq_r[j], n)
                nc.vector.tensor_tensor(y_sb[j][:, :, :], z_sb[p][:, :, j * S:(j + 1) * S],
                                        bank[6][:, 0:NH * S].rearrange("p (h s) -> p h s", h=NH), ALU.mult).then_inc(y_r[j], 1)

            def o_step(n, p, j):
                dve.wait_ge(o_ps[j], n + 1)
                nc.vector.tensor_copy(pr[p][j][:, :], bank[7][:, 0:D])
                nc.vector.tensor_scalar(ss_eps[p][:, j:j + 1], bank[7][:, D:D + 1], EPS, None, ALU.add).then_inc(o_ev[j], 1)

            def ln_stats(n, p, base):
                for j in range(2):
                    dve.wait_ge(ln_x, (n + base) * 2 + j + 1)
                    nc.vector.bn_stats(stats[p][j][:, :], xr[p][j][:, :]).then_inc(ln_s, 1)
                wait_apart(dve, ln_s, (n + base) * 2 + 2)
                for j in range(2):
                    nc.vector.bn_aggr(mv[p][:, j, :], stats[p][j][:, :]).then_inc(ln_v, 1)

            def ln_first(n, p):
                dve.wait_ge(rg_r, n + 1)
                for j in range(2):
                    nc.vector.scalar_tensor_tensor(out=xr[p][j][:, None, :], in0=pr[p][j][:, None, :], scalar=r_gate[p][:, j:j + 1],
                                                   in1=x_nat[:, bass.ds(n * 2 + j, 1), :], op0=ALU.mult, op1=ALU.add).then_inc(ln_x, 1)
                ln_stats(n, p, 0)

            def ln_norm(n, p, base):
                dve.wait_ge(ln_r, n + base + 1)
                for j in range(2):
                    last = nc.vector.tensor_scalar(x_nat[:, bass.ds(n * 2 + j, 1), :], xr[p][j][:, None, :], mv[p][:, j, 0:1],
                                                   r_ln[p][:, j:j + 1], ALU.subtract, ALU.mult)
                last.then_inc(ln_d, 1)

            dve.wait_ge(s_pool, POOLN)
            lo(0, 0)
            lo(1, 1)
            gate_bc(0, 0)
            gate_x(0, 0)
            gate_x(0, 1)

            def body(n, p, nxt, nxt2, turn):
                w_step(n, 0)
                if nxt:
                    gate_bc(n + 1, 1 - p)
                w_step(n, 1)
                y_step(n, p, 0)
                if nxt:
                    gate_x(n + 1, 0)
                y_step(n, p, 1)
                if nxt2:
                    lo(n + 2, p)
                o_step(n, p, 0)
                if nxt:
                    gate_x(n + 1, 1)
                o_step(n, p, 1)
                ln_first(n, p)
                ln_norm(n, p, 0)
            pairs(dve, body)
            def split_qk(n, p):
                dve.wait_ge(qa_r, n + 1)
                qk = bank[1][:, :].rearrange("p (a s) -> p a s", a=2)
                nc.vector.tensor_tensor(qk_rest[:, :, :], qk, qk_part[p][:, 0, :, :], ALU.subtract).then_inc(q_st, 1)
                dve.wait_ge(q_st, 3 * n + 1)
                nc.vector.tensor_copy(qk_part[p][:, 1, :, :], qk_rest[:, :, :]).then_inc(q_st, 1)
                dve.wait_ge(q_st, 3 * n + 2)
                nc.vector.tensor_tensor(qk_part[p][:, 2, :, :], qk_rest[:, :, :], qk_part[p][:, 1, :, :], ALU.subtract).then_inc(q_st, 1)

            def reduce_max(n, j):
                m = n * 2 + j
                for g in range(HG):
                    dve.wait_ge(s_ps[g % 2], 2 * m + g // 2 + 1)
                    nc.vector.tensor_reduce(mx[j][:, HG * g:HG * g + HG], bank[2 + g % 2][:, :].rearrange("p (h k) -> p h k", h=HG),
                                            AX_X, ALU.max).then_inc(red, 1)

            def split_max(n, j):
                m = n * 2 + j
                dve.wait_ge(red, m * 4 + 4)
                nc.vector.tensor_scalar(nm_part[j][:, 0, :], mx[j][:, :], -1.0, None, ALU.mult).then_inc(nm_s, 1)
                dve.wait_ge(nm_s, m * 4 + 1)
                nc.vector.scalar_tensor_tensor(out=nm_rest[j][:, :], in0=mx[j][:, :], scalar=-1.0, in1=nm_part[j][:, 0, :],
                                               op0=ALU.mult, op1=ALU.subtract).then_inc(nm_s, 1)
                dve.wait_ge(nm_s, m * 4 + 2)
                nc.vector.tensor_copy(nm_part[j][:, 1, :], nm_rest[j][:, :]).then_inc(nm_s, 1)
                dve.wait_ge(nm_s, m * 4 + 3)
                nc.vector.tensor_tensor(nm_part[j][:, 2, :], nm_rest[j][:, :], nm_part[j][:, 1, :], ALU.subtract).then_inc(nm_s, 1)

            def copy_nmT(n, j):
                m = n * 2 + j
                dve.wait_ge(nmT_ps, m + 1)
                nc.vector.tensor_copy(nm_T[j][:, :], bank[2][0:NPART * HEADS, 0:P // 2].bitcast(BF16)).then_inc(nmT_r, 1)

            def normalise(n, j):
                m = n * 2 + j
                dve.wait_ge(inv_r, m + 1)
                nc.vector.tensor_tensor(att[j][:, :], att[j][:, :], inv[j][:, :], ALU.mult).then_inc(an_r, 1)

            def residual(n, p, j):
                m = n * 2 + j
                dve.wait_ge(o2_ps, m + 1)
                nc.vector.tensor_tensor(xr[p][j][:, None, :], x_nat[:, bass.ds(m, 1), :], bank[7][:, None, 0:D], ALU.add).then_inc(ln_x, 1)

            split_qk(0, 0)
            reduce_max(0, 0)
            split_max(0, 0)
            copy_nmT(0, 0)

            def body(n, p, nxt, nxt2, turn):
                if nxt:
                    split_qk(n + 1, 1 - p)
                reduce_max(n, 1)
                split_max(n, 1)
                copy_nmT(n, 1)
                normalise(n, 0)
                residual(n, p, 0)
                if nxt:
                    reduce_max(n + 1, 0)
                    split_max(n + 1, 0)
                    copy_nmT(n + 1, 0)
                normalise(n, 1)
                residual(n, p, 1)
                ln_stats(n, p, NPAIR)
                ln_norm(n, p, NPAIR)
            pairs(dve, body)
            hand_over(dve)
            for k in range(2):
                dve.nop().then_inc(wn_free[k], 1)
            with dve.Fori(0, NE) as e:
                for k, dst in enumerate((wg, wu)):
                    dve.wait_ge(wn_hi, e * 2 + k + 1)
                    nc.vector.tensor_tensor(dst[1][:, bass.ds(e * F, F)], bank[1 + k][:, :],
                                            dst[0][:, bass.ds(e * F, F)].bitcast(F32), ALU.subtract).then_inc(wn_free[k], 1)
            dve.wait_ge(c3, C3N)

            def route(n, p, turn):
                at = [0]

                def link(ins, apart=False):
                    at[0] += 1
                    ins.then_inc(rt, 1)
                    if apart:
                        wait_apart(dve, rt, n * RT + at[0])
                    else:
                        dve.wait_ge(rt, n * RT + at[0])

                dve.wait_ge(r_lg, n + 1)
                link(nc.vector.tensor_copy(lg[p][:, :, :], bank[5][:, 0:2 * NE].rearrange("p (b e) -> p b e", e=NE)), apart=True)
                nc.vector.max(top[p][:, 0, :], lg[p][:, 0, :])
                link(nc.vector.max(top[p][:, 1, :], lg[p][:, 1, :]), apart=True)
                nc.vector.max_index(top_i[p][:, 0, :], top[p][:, 0, :], lg[p][:, 0, :])
                link(nc.vector.max_index(top_i[p][:, 1, :], top[p][:, 1, :], lg[p][:, 1, :]))
                link(nc.vector.tensor_tensor(ex[p][:, :, 0:NE], lg[p][:, :, :], top[p][:, :, 0:1].to_broadcast([P, 2, NE]), ALU.subtract))
                link(nc.vector.tensor_tensor(ex[p][:, :, NE], top[p][:, :, 1], top[p][:, :, 0], ALU.subtract))
                link(nc.vector.tensor_copy(top_f[p][:, :, :], top_i[p][:, :, 0:TOPK]))
                link(nc.vector.tensor_tensor(hot[p][:, :, :, :].rearrange("p b k e -> p (b k) e"),
                                             top_f[p][:, :, :].rearrange("p b k -> p (b k)")[:, :, None].to_broadcast([P, 2 * TOPK, NE]),
                                             iota_e[:, None, :].to_broadcast([P, 2 * TOPK, NE]), ALU.is_equal))
                link(nc.vector.tensor_tensor(both[p][:, :, :], hot[p][:, :, 0, :], hot[p][:, :, 1, :], ALU.add))
                dve.wait_ge(r_ex, n + 1)
                link(nc.vector.tensor_reduce(esum[p][:, :], ex[p][:, :, 0:NE], AX_X, ALU.add))
                if not isinstance(n, int) or n >= 2:
                    dve.wait_ge(sc_d[p], turn * 64)
                link(nc.vector.reciprocal(row[p][0][:, :, D], esum[p][:, :]))
                link(nc.vector.tensor_tensor(row[p][1][:, :, D], row[p][0][:, :, D], ex[p][:, :, NE], ALU.mult))
                dve.wait_ge(r_cnt, n + 1)
                link(nc.vector.tensor_tensor(pos[p][:, :, :], bank[6][:, 0:2 * NE].rearrange("p (b e) -> p b e", e=NE),
                                             base[:, None, :].to_broadcast([P, 2, NE]), ALU.add))
                link(nc.vector.tensor_tensor(base[:, :], bank[6][:, 2 * NE:3 * NE], base[:, :], ALU.add))
                link(nc.vector.tensor_tensor(picked[p][:, :, :, :], hot[p][:, :, :, :],
                                             pos[p][:, :, None, :].to_broadcast([P, 2, TOPK, NE]), ALU.mult))
                link(nc.vector.tensor_reduce(slot_f[p][:, :], picked[p][:, :, :, :].rearrange("p b k e -> p (b k) e"), AX_X, ALU.add))
                nc.vector.tensor_copy(slot_i[p][:, :], slot_f[p][:, :]).then_inc(r_slot, 1)
                assert at[0] == RT, at

            pairs(dve, lambda n, p, nxt, nxt2, turn: route(n, p, turn))

            at = [0]

            def link(ins):
                at[0] += 1
                ins.then_inc(tab, 1)
                dve.wait_ge(tab, at[0])

            one = slice(0, 1)
            ROUND = float(2 ** 23)
            dve.wait_ge(rt, NPAIR * RT)
            link(nc.vector.tensor_tensor(cnt[:, :], base[one, :], e_base[one, :], ALU.subtract))
            link(nc.vector.tensor_scalar(ntile[:, :], cnt[:, :], 1.0 / P, (P - 1) / (2.0 * P), ALU.mult, ALU.add))
            link(nc.vector.tensor_scalar(ntile[:, :], ntile[:, :], ROUND, ROUND, ALU.add, ALU.subtract))
            link(nc.vector.memset(start[:, 0:1], 0.0))
            for e in range(NE):
                link(nc.vector.tensor_tensor(start[:, e + 1:e + 2], start[:, e:e + 1], ntile[:, e:e + 1], ALU.add))
            link(nc.vector.tensor_scalar(coef[:, :], ntile[:, 0:NE - 1], -float(P), float(CAP), ALU.mult, ALU.add))
            link(nc.vector.tensor_tensor(passed[:, :, :], start[:, None, 1:NE].to_broadcast([1, NTILE, NE - 1]),
                                         tile_no[:, :, None].to_broadcast([1, NTILE, NE - 1]), ALU.is_le))
            link(nc.vector.tensor_reduce(tile_e[:, :], passed[:, :, :], AX_X, ALU.add))
            link(nc.vector.tensor_tensor(passed_c[:, :, :], passed[:, :, :], coef[:, None, :].to_broadcast([1, NTILE, NE - 1]), ALU.mult))
            link(nc.vector.tensor_reduce(tile_r[:, :], passed_c[:, :, :], AX_X, ALU.add))
            link(nc.vector.scalar_tensor_tensor(out=tile_r[:, :], in0=tile_no[:, :], scalar=float(P), in1=tile_r[:, :],
                                                op0=ALU.mult, op1=ALU.add))
            link(nc.vector.tensor_scalar(tile_v[:, :], tile_no[:, :], start[:, NE:NE + 1], None, ALU.is_lt))
            link(nc.vector.scalar_tensor_tensor(out=tile_r[:, :], in0=tile_r[:, :], scalar=-float(PAD_ROW), in1=tile_v[:, :],
                                                op0=ALU.add, op1=ALU.mult))
            link(nc.vector.tensor_scalar(tile_row[:, :], tile_r[:, :], float(PAD_ROW), None, ALU.add))
            link(nc.vector.tensor_scalar(tile_col[:, :], tile_e[:, :], float(F), None, ALU.mult))
            link(nc.vector.tensor_copy(pad_at[:, :], base[one, :]))
            assert at[0] == TABN, at

            def lo_tile(i, q):
                dve.wait_ge(m_hi, i + 1)
                nc.vector.tensor_tensor(xel[q][:, :], bank[0][:, 0:P], xeh[q][:, :].bitcast(F32), ALU.subtract).then_inc(m_lo, 1)

            def mul_up(i, q):
                dve.wait_ge(m_sg, i + 1)
                dve.wait_ge(m_u, i + 1)
                if not isinstance(i, int) or i >= 2:
                    dve.wait_ge(m_ht, i - 1)
                nc.vector.tensor_tensor(hid[q][:, :], sg[q][:, :], bank[2][:, :], ALU.mult).then_inc(m_hid, 1)

            def scale_out(i, q, turn):
                dve.wait_ge(m_o, i + 1)
                wait(dve, p_sc[q], turn * 16)
                if q:
                    nc.vector.tensor_scalar(is_pad[:, :], xs_in[q][:, D + 1:D + 2], float(TOKENS * TOPK), float(P), ALU.is_ge, ALU.mult).then_inc(m_ix, 1)
                    dve.wait_ge(m_ix, turn + 1)
                    nc.vector.tensor_tensor(part_i[q][:, :], xs_in[q][:, D + 1:D + 2], is_pad[:, :], ALU.add)
                else:
                    nc.vector.tensor_copy(part_i[q][:, :], xs_in[q][:, D + 1:D + 2])
                nc.vector.tensor_scalar(y_out[q][:, :], bank[4][:, 0:D], xs_in[q][:, D:D + 1], None, ALU.mult).then_inc(m_y, 1)

            lo_tile(0, 0)
            mul_up(0, 0)
            lo_tile(1, 1)
            mul_up(1, 1)
            scale_out(0, 0, 0)
            lo_tile(2, 0)
            mul_up(2, 0)
            scale_out(1, 1, 0)
            with dve.Fori(0, NTILE // 2 - 2) as i:
                lo_tile(i * 2 + 3, 1)
                mul_up(i * 2 + 3, 1)
                scale_out(i * 2 + 2, 0, i + 1)
                lo_tile(i * 2 + 4, 0)
                mul_up(i * 2 + 4, 0)
                scale_out(i * 2 + 3, 1, i + 1)
            lo_tile(NTILE - 1, 1)
            mul_up(NTILE - 1, 1)
            scale_out(NTILE - 2, 0, NTILE // 2 - 1)
            scale_out(NTILE - 1, 1, NTILE // 2 - 1)

            def finish(g, q, turn):
                FC_ = 8
                dve.wait_ge(f_ld[q], turn * 32 + 32)
                wait(dve, f_n, g - 1) if isinstance(g, int) else dve.wait_ge(f_n, g - 1)
                nc.vector.tensor_tensor(fin[q][:, :, :], y_in[q][:, 0, :, :], y_in[q][:, 1, :, :], ALU.add).then_inc(f_c, 1)
                dve.wait_ge(f_c, g * FC_ + 1)
                nc.vector.tensor_tensor(fin[q][:, :, :], fin[q][:, :, :], x_nat[:, bass.ds(g * 4, 4), :], ALU.add).then_inc(f_c, 1)
                dve.wait_ge(f_c, g * FC_ + 2)
                for b in range(4):
                    last = nc.vector.bn_stats(f_st[q][:, b, :], fin[q][:, b, :])
                last.then_inc(f_c, 1)
                wait_apart(dve, f_c, g * FC_ + 3)
                for b in range(4):
                    last = nc.vector.bn_aggr(f_mv[q][:, b, :], f_st[q][:, b, :])
                last.then_inc(f_c, 1)
                dve.wait_ge(f_c, g * FC_ + 4)
                nc.vector.tensor_scalar(f_ve[q][:, :], f_mv[q][:, :, 1], EPS, None, ALU.add).then_inc(f_v, 1)
                dve.nop().then_inc(f_c, 4)
                dve.wait_ge(f_rr, g + 1)
                nc.vector.scalar_tensor_tensor(out=f_b[q][:, :], in0=f_mv[q][:, :, 0], scalar=-1.0, in1=f_r[q][:, :],
                                               op0=ALU.mult, op1=ALU.mult).then_inc(f_bb, 1)
            for q in range(2):
                finish(q, q, 0)
            with dve.Fori(1, NG // 2) as i:
                for q in range(2):
                    finish(i * 2 + q, q, i)


POOLN = 5 * 2 + 2 + 4 + 4 + 8 + 4 + 4 + 1 + 8
PREP = 19
C3N = 11
RT = 15
TABN = 23


_INS = ["x", "ctx_1024", "L0_attn_W_in", "L0_attn_conv_w", "L0_attn_conv_b", "L0_attn_dt_bias", "L0_attn_A_log",
        "L0_attn_D", "L0_attn_norm_scale", "L0_attn_W_out", "L0_xattn_wq", "L0_xattn_wk", "L0_xattn_wv", "L0_xattn_wo",
        "L0_ffn_router_w", "L0_ffn_gate_w", "L0_ffn_up_w", "L0_ffn_down_w"]


def kernel(**inputs):
    import numpy as _np
    import concourse.bacc as _bacc
    from concourse import mybir as _mybir
    from concourse.bass_utils import run_bass_kernel_spmd as _run

    nc = _bacc.Bacc("TRN2", target_bir_lowering=False, num_devices=1)
    arrays, aps = {}, {}
    for name in _INS:
        a = _np.ascontiguousarray(inputs[name])
        arrays[f"in_{name}_dram"] = a
        aps[name] = nc.dram_tensor(f"in_{name}_dram", a.shape, _mybir.dt.from_np(a.dtype), kind="ExternalInput").ap()
    out = nc.dram_tensor("out_0_dram", inputs["x"].shape, _mybir.dt.float32, kind="ExternalOutput").ap()
    build(nc, aps, out)
    r = _run(nc, [arrays], core_ids=[0])
    return r.results[0]["out_0_dram"]
```

```python
from contextlib import ExitStack

import concourse.bass as bass
from concourse import mybir

F32 = mybir.dt.float32
F32R = mybir.dt.float32r
BF16 = mybir.dt.bfloat16
I32 = mybir.dt.int32
ALU = mybir.AluOpType
ACT = mybir.ActivationFunctionType
AX_X = mybir.AxisListType.X
P = 128
EPS = 1e-5
NEG = -30000.0


def build(nc, t, out):
    NB, S, D = t["x"].shape
    DI = t["L0_attn_W_out"].shape[0]
    NH = t["L0_attn_D"].shape[0]
    TAPS, _, CC = t["L0_attn_conv_w"].shape
    NS = (CC - DI) // 2
    NPAIR = NB // 2
    assert (S, D, DI, NH, TAPS, NS) == (P, P, 2 * P, 2, 4, 64)
    ZX = DI
    DTC = DI + CC

    x_rows = t["x"].rearrange("b s d -> s b d")
    ctx_rows = t["ctx_1024"].rearrange("b s d -> s b d")
    out_rows = out.rearrange("b s d -> s b d")

    with ExitStack() as ctx:
        own = [ctx]

        def sb(name, shape, dt=F32):
            return own[-1].enter_context(nc.sbuf_tensor(name, shape, dt))

        def sem(name):
            return ctx.enter_context(nc.semaphore(name))

        def sem2(name):
            return [sem(name + "0"), sem(name + "1")]

        bank = [ctx.enter_context(nc.psum_tensor(f"bank{i}", [P, 512], F32)) for i in range(8)]

        ident = sb("ident", [P, P])
        x_nat = sb("x_nat", [P, NB, D])
        minus_half = sb("minus_half", [P, 2])
        eps_pool = sb("eps_pool", [P, 2])
        spare_pool = sb("spare_pool", [1, 1])
        spare_dve = sb("spare_dve", [1, 1])
        xr = [[sb(f"xr{p}{j}", [P, D]) for j in range(2)] for p in range(2)]
        stats = [[sb(f"stats{p}{j}", [P, 6]) for j in range(2)] for p in range(2)]
        mv = [sb(f"mv{p}", [P, 2, 2]) for p in range(2)]
        v_eps = [sb(f"v_eps{p}", [P, 2]) for p in range(2)]
        r_ln = [sb(f"r_ln{p}", [P, 2]) for p in range(2)]
        NE = t["L0_ffn_gate_w"].shape[0]
        F = t["L0_ffn_gate_w"].shape[1]
        FC = F // P
        TOPK = 2
        TOKENS = NB * S
        CAP = TOKENS + P
        WIDE = D + 2
        rw_nat = sb("rw_nat", [NE, D])
        rw_T = sb("rw_T", [P, NE])
        before = sb("before", [P, P], BF16)
        ones_b = sb("ones_b", [P, P], BF16)
        iota_e = sb("iota_e", [P, NE])
        e_base = sb("e_base", [P, NE])
        base = sb("base", [P, NE])
        place = sb("place", [P, NB, TOPK])
        row = [[sb(f"row{p}{k}", [P, 2, WIDE]) for k in range(TOPK)] for p in range(2)]
        x2T = [sb(f"x2T{p}", [P, 2 * S]) for p in range(2)]
        lg = [sb(f"lg{p}", [P, 2, NE]) for p in range(2)]
        top = [sb(f"top{p}", [P, 2, 8]) for p in range(2)]
        top_i = [sb(f"top_i{p}", [P, 2, 8], mybir.dt.uint32) for p in range(2)]
        ex = [sb(f"ex{p}", [P, 2, NE + 1]) for p in range(2)]
        esum = [sb(f"esum{p}", [P, 2]) for p in range(2)]
        top_f = [sb(f"top_f{p}", [P, 2, TOPK]) for p in range(2)]
        hot = [sb(f"hot{p}", [P, 2, TOPK, NE]) for p in range(2)]
        both = [sb(f"both{p}", [P, 2, NE], BF16) for p in range(2)]
        pos = [sb(f"pos{p}", [P, 2, NE]) for p in range(2)]
        picked = [sb(f"picked{p}", [P, 2, TOPK, NE]) for p in range(2)]
        slot_f = [sb(f"slot_f{p}", [P, 2 * TOPK]) for p in range(2)]
        slot_i = [sb(f"slot_i{p}", [P, 2 * TOPK], I32) for p in range(2)]
        early = ExitStack()
        own.append(early)
        ident_bf = sb("ident_bf", [P, P], BF16)
        ones_f = sb("ones_f", [P, 1])
        half_ones = sb("ones_bf", [3, 2 * P], BF16)
        after = sb("after", [P, P])
        upto = sb("upto", [P, NH, P])
        future = sb("future", [P, NH, P], BF16)
        w_in = sb("w_in", [P, 2 * DI + 2 * NS + NH])
        wz_h = sb("wz_h", [P, DI], F32R)
        wz_l = sb("wz_l", [P, DI], F32R)
        cb = sb("cb", [3, CC])
        cb_part = [sb(f"cb_part{i}", [3, CC], BF16) for i in range(3)]
        cb_rest = sb("cb_rest", [3, CC])
        cb_rows = sb("cb_rows", [3, CC], BF16)
        w_out = sb("w_out", [P, NH, D])
        nscale = sb("nscale", [P, NH])
        a_log = sb("a_log", [P, NH])
        a_neg = sb("a_neg", [P, NH])
        dt_bias = sb("dt_bias", [P, NH])
        d_skip = sb("d_skip", [P, NH])
        d_diag = sb("d_diag", [P, NH, P])
        dt_v = sb("dt_v", [P, NB, NH])
        dt_e = sb("dt_e", [P, NB, NH])
        dt_half = sb("dt_half", [P, NB, NH])
        dt_a = sb("dt_a", [P, NB, NH])
        xh = [sb(f"xh{p}", [P, 2, S + 4], F32R) for p in range(2)]
        xl = [sb(f"xl{p}", [P, 2, S + 4], F32R) for p in range(2)]
        t_bc = sb("t_bc", [P, 2 * S])
        b_sb = [sb(f"b_sb{p}", [NS, 2 * S]) for p in range(2)]
        c_sb = [sb(f"c_sb{p}", [NS, 2 * S]) for p in range(2)]
        z_sb = [sb(f"z_sb{p}", [P, NH, 2 * S]) for p in range(2)]
        t_x = [sb(f"t_x{j}", [P, DI]) for j in range(2)]
        x_s = [sb(f"x_s{j}", [P, DI]) for j in range(2)]
        xdt = [[sb(f"xdt{p}{j}", [P, DI]) for j in range(2)] for p in range(2)]
        ua = [sb(f"ua{j}", [P, NH, S]) for j in range(2)]
        e_sb = [sb(f"e_sb{j}", [P, NH, S]) for j in range(2)]
        w_sb = [sb(f"w_sb{j}", [P, NH, S]) for j in range(2)]
        y_sb = [sb(f"y_sb{j}", [P, NH, S]) for j in range(2)]
        sq_sb = [sb(f"sq_sb{j}", [P, NH, S]) for j in range(2)]

        pr = [[sb(f"pr{p}{j}", [P, D]) for j in range(2)] for p in range(2)]
        ss_eps = [sb(f"ss_eps{p}", [P, 2]) for p in range(2)]
        r_gate = [sb(f"r_gate{p}", [P, 2]) for p in range(2)]
        HEADS, HD, HG = 16, 8, 4
        NPART = 3
        KROWS = NPART * NPART * HD
        wx_nat = {k: sb(f"{k}_nat", [P, D]) for k in ("wq", "wk", "wv", "wo")}
        wx_T = {k: sb(f"{k}_T", [P, D]) for k in ("wq", "wk", "wv", "wo")}
        wo_pad = sb("wo_pad", [P, HG, D])
        sel_sum = sb("sel_sum", [P, P])
        sel_max = sb("sel_max", [NPART * HEADS, HEADS, P], BF16)
        mask_q = sb("mask_q", [P, HG, P], BF16)
        mask_k = sb("mask_k", [P, HG, P], BF16)
        a_in = [sb(f"a_in{p}", [P, 2, 2, D]) for p in range(2)]
        a_T = [sb(f"a_T{p}", [P, 2, 2 * S]) for p in range(2)]
        qk_part = [sb(f"qk_part{p}", [P, NPART, 2, 2 * S], BF16) for p in range(2)]
        qk_rest = sb("qk_rest", [P, 2, 2 * S])
        v_pad = [[sb(f"v_pad{p}{j}", [P, HEADS, 32]) for j in range(2)] for p in range(2)]
        mx = [sb(f"mx{j}", [P, HEADS]) for j in range(2)]
        nm_part = [sb(f"nm_part{j}", [P, P // HEADS, HEADS], BF16) for j in range(2)]
        nm_rest = [sb(f"nm_rest{j}", [P, HEADS]) for j in range(2)]
        nm_T = [sb(f"nm_T{j}", [NPART * HEADS, P], BF16) for j in range(2)]
        pT = [sb(f"pT{j}", [P, HG, HG * P]) for j in range(2)]
        att = [sb(f"att{j}", [P, HG * P]) for j in range(2)]
        inv = [sb(f"inv{j}", [P, HG * P]) for j in range(2)]
        scr = [nc.dram_tensor(f"scr{p}", (HEADS, 5, HD, 2, 2 * S), BF16, kind="Internal").ap() for p in range(2)]

        first = ExitStack()
        own.append(first)
        cw = sb("cw", [P, TAPS, CC])
        wconv = sb("wconv", [P, TAPS, CC])
        wconv_h = sb("wconv_h", [P, TAPS, CC], F32R)
        wconv_l = sb("wconv_l", [P, TAPS, CC], F32R)
        xT = sb("xT", [P, NB, S])
        first.close()
        own.pop()
        stack = [[sb(f"stack{p}{s_}", [KROWS, HEADS, 2 * S], BF16) for s_ in range(2)] for p in range(2)]
        early.close()
        own.pop()
        NTILE = TOKENS * TOPK // P + NE
        PAD_ROW = NE * CAP
        slots = nc.dram_tensor("slots", (PAD_ROW + NE * P, WIDE), F32, kind="Internal").ap()
        parts = nc.dram_tensor("parts", (TOKENS * TOPK + 2 * NE * P, D), F32, kind="Internal").ap()
        pad_rows = sb("pad_rows", [P, 2 * NE, WIDE])
        tile_no = sb("tile_no", [1, NTILE])
        cnt = sb("cnt", [1, NE])
        ntile = sb("ntile", [1, NE])
        start = sb("start", [1, NE + 1])
        coef = sb("coef", [1, NE])
        passed = sb("passed", [1, NTILE, NE])
        passed_c = sb("passed_c", [1, NTILE, NE])
        tile_e = sb("tile_e", [1, NTILE])
        tile_r = sb("tile_r", [1, NTILE])
        tile_col = sb("tile_col", [1, NTILE], I32)
        tile_row = sb("tile_row", [1, NTILE], I32)
        pad_at = sb("pad_at", [1, NE], I32)
        wg = [sb(f"wg{i}", [P, NE * F], F32R) for i in range(2)]
        wu = [sb(f"wu{i}", [P, NE * F], F32R) for i in range(2)]
        wd = sb("wd", [P, NE * F])
        w_nat = [sb(f"w_nat{k}", [P, FC, P]) for k in range(3)]
        DEPTH = 4
        xs_in = [sb(f"xs_in{q}", [P, WIDE]) for q in range(DEPTH)]
        w_place = [sb(f"w_place{q}", [P, 2]) for q in range(DEPTH)]
        xeh = [sb(f"xeh{q}", [P, P], F32R) for q in range(DEPTH)]
        xel = [sb(f"xel{q}", [P, P], F32R) for q in range(DEPTH)]
        sg = [sb(f"sg{q}", [P, F]) for q in range(2)]
        hid = [sb(f"hid{q}", [P, F]) for q in range(2)]
        hT = [sb(f"hT{q}", [P, F]) for q in range(2)]
        y_out = [sb(f"y_out{q}", [P, D]) for q in range(DEPTH)]
        part_i = [sb(f"part_i{q}", [P, 1], I32) for q in range(DEPTH)]
        NG = NB // 4
        y_in = [sb(f"y_in{q}", [P, TOPK, 4, D]) for q in range(2)]
        fin = [sb(f"fin{q}", [P, 4, D]) for q in range(2)]
        f_st = [sb(f"f_st{q}", [P, 4, 6]) for q in range(2)]
        f_mv = [sb(f"f_mv{q}", [P, 4, 2]) for q in range(2)]
        f_ve = [sb(f"f_ve{q}", [P, 4]) for q in range(2)]
        f_r = [sb(f"f_r{q}", [P, 4]) for q in range(2)]
        f_b = [sb(f"f_b{q}", [P, 4]) for q in range(2)]
        f_o = [sb(f"f_o{q}", [P, 4, D]) for q in range(2)]
        minus_half4 = sb("minus_half4", [P, 4])

        s_w = sem("weights_loaded")
        s_win = sem("w_in_loaded")
        s_xl = [sem(f"x_loaded{g}") for g in range(NB // 4)]
        s_pool = sem("pool_consts")
        s_prep = sem("dve_prep")
        s_aprep = sem("act_prep")
        s_cbrow = sem("conv_bias_rows")
        s_xtr = sem("x_transposed")
        s_xT = sem("xT_ready")
        s_dtps = sem("dt_psum")
        s_dt = sem("dt_ready")
        s_dtx = sem("dt_exp")
        split_hi, split_lo = sem("split_hi"), sem("split_lo")
        bc_ps, z_ps, x_ps = sem("bc_ps"), sem("z_ps"), sem2("x_ps")
        t_bc_r, z_ev, t_x_r = sem("t_bc_r"), sem("z_ev"), sem2("t_x_r")
        bc_gated, x_gated, xdt_r = sem("bc_gated"), sem2("x_gated"), sem2("xdt_r")
        ua_r, sg_ps, e_r = sem2("ua_r"), sem2("sg_ps"), sem2("e_r")
        w_raw, w_r = sem2("w_raw"), sem2("w_r")
        y_ps, y_r, sq_r = sem2("y_ps"), sem2("y_r"), sem2("sq_r")
        o_ps, o_ev = sem2("o_ps"), sem2("o_ev")
        s_out = sem("out_written")
        rg_r = sem("rg_r")
        ln_x, ln_s, ln_v, ln_r, ln_d = sem("ln_x"), sem("ln_s"), sem("ln_v"), sem("ln_r"), sem("ln_done")
        ln_e = sem("ln_e")
        s_wx = sem("attn_weights_loaded")
        s_wT = sem("attn_weights_T")
        s_wTr = sem("attn_weights_T_ready")
        s_wop = sem("wo_pad_written")
        a_ld = sem2("a_loaded")
        tr_ps, aT_r, qk_ps, qa_r, q_st, v_ps, v_r = (sem(n) for n in ("tr_ps", "aT_r", "qk_ps", "qa_r", "q_split", "v_ps", "v_r"))
        scr_w, st_ld = sem2("scratch_written"), sem2("stack_loaded")
        s_ps, red = sem2("s_ps"), sem("red")
        nm_s, nmT_ps, nmT_r = sem("nm_split"), sem("nmT_ps"), sem("nmT_r")
        t_ps, p_r, pv_ps, att_r = sem("t_ps"), sem("p_r"), sem("pv_ps"), sem("att_r")
        z2_ps, lnz, inv_r, an_r, o2_ps, o2_r = (sem(n) for n in ("z2_ps", "lnz", "inv_r", "an_r", "o2_ps", "o2_r"))

        spare_w = sem("spare_written")
        early_done = sem("early_phases_done")
        c3, rw_ld, rw_t, rw_r = sem("consts3"), sem("rw_loaded"), sem("rw_turned"), sem("rw_ready")
        pad_w, pad_d = sem("pad_row_written"), sem("pad_rows_placed")
        row_c, r_tr, r_T, r_lg = sem("row_copied"), sem("r_tr"), sem("r_T"), sem("r_logits")
        rt, r_ex, r_cnt, r_slot, sc_d = sem("rt_chain"), sem("r_ex"), sem("r_cnt"), sem("r_slot"), sem2("scattered")
        tab = sem("table_chain")
        wn_ld = [sem(f"wn_ld{k}") for k in range(3)]
        wn_tr, wn_hi, wn_free = sem("wn_tr"), sem("wn_hi"), [sem(f"wn_free{k}") for k in range(3)]
        xs_ld = [sem(f"xs_loaded{q}") for q in range(DEPTH)]
        m_tr, m_hi, m_lo, m_g, m_u = (sem(n) for n in ("m_tr", "m_hi", "m_lo", "m_g", "m_u"))
        m_sg, m_hid, m_ht, m_hT, m_o, m_y = (sem(n) for n in ("m_sg", "m_hid", "m_ht", "m_hT", "m_o", "m_y"))
        p_sc = [sem(f"parts_scattered{q}") for q in range(DEPTH)]
        f_ld = sem2("f_loaded")
        f_c, f_v, f_rr, f_bb, f_n, f_w = sem("f_chain"), sem("f_v"), sem("f_rr"), sem("f_bb"), sem("f_n"), sem2("f_written")

        block = ctx.enter_context(nc.Block())

        def hand_over(eng):
            eng.drain().then_inc(early_done, 1)
            eng.wait_ge(early_done, 5)
        NW = 9

        def wait(eng, s, v):
            if not isinstance(v, int) or v > 0:
                eng.wait_ge(s, v)

        def wait_apart(eng, s, v, written=0):
            eng.wait_ge(s, v)
            if eng is nc.gpsimd:
                wait(eng, spare_w, written)
                nc.gpsimd.tensor_tensor(spare_pool[:, :], minus_half[0:1, 0:1], minus_half[0:1, 0:1], ALU.add).then_inc(spare_w, 1)
            else:
                nc.vector.memset(spare_dve[:, :], 0.0)

        def tiles(eng, *steps):
            def rounds(turn):
                for u in range(DEPTH):
                    for step, ahead in steps:
                        i = turn * DEPTH + u + ahead
                        if not isinstance(turn, int) or 0 <= i < NTILE:
                            step(i, (u + ahead) % DEPTH, turn + (u + ahead) // DEPTH)
            rounds(-1)
            rounds(0)
            with eng.Fori(1, NTILE // DEPTH - 1) as turn:
                rounds(turn)
            rounds(NTILE // DEPTH - 1)
            rounds(NTILE // DEPTH)

        def rounds_of_pairs(eng, half):
            def a_round(n, p, turn):
                for j in range(2):
                    half(n, p, turn, j, lambda k: not isinstance(n, int) or 0 <= n + k < NPAIR)
            for n in range(-2, 4):
                a_round(n, n % 2, n // 2)
            with eng.Fori(2, NPAIR // 2 - 1) as i:
                a_round(i * 2, 0, i)
                a_round(i * 2 + 1, 1, i)
            for n in range(NPAIR - 2, NPAIR + 2):
                a_round(n, n % 2, n // 2)

        def pair_at(n, p, turn, k):
            return n + k, (p + k) % 2, turn + (p + k) // 2

        def pairs(eng, body):
            body(0, 0, True, True, 0)
            body(1, 1, True, True, 0)
            with eng.Fori(1, NPAIR // 2 - 1) as i:
                body(i * 2, 0, True, True, i)
                body(i * 2 + 1, 1, True, True, i)
            body(NPAIR - 2, 0, True, False, NPAIR // 2 - 1)
            body(NPAIR - 1, 1, False, False, NPAIR // 2 - 1)

        @block.sync
        def _(sp):
            for g in range(2):
                sp.dma_start(x_nat[:, 4 * g:4 * g + 4, :], x_rows[:, 4 * g:4 * g + 4, :]).then_inc(s_xl[g], 16)
            sp.dma_start(w_in[:, :], t["L0_attn_W_in"]).then_inc(s_win, 16)
            sp.dma_start(cw[:, :, :].rearrange("p k c -> p (k c)"),
                         t["L0_attn_conv_w"].rearrange("k a c -> a (k c)").to_broadcast([P, TAPS * CC])).then_inc(s_w, 16)
            sp.dma_start(cb[:, :], t["L0_attn_conv_b"][None, :].to_broadcast([3, CC])).then_inc(s_w, 16)
            sp.dma_start(w_out[:, :, :], t["L0_attn_W_out"].rearrange("(h p) e -> p h e", p=P)).then_inc(s_w, 16)
            with nc.allow_non_contiguous_dma(reason="256 scales, once"):
                sp.dma_start(nscale[:, :], t["L0_attn_norm_scale"].rearrange("(h p) -> p h", p=P)).then_inc(s_w, 16)
            for dst, name in ((a_log, "A_log"), (dt_bias, "dt_bias"), (d_skip, "D")):
                sp.dma_start(dst[:, :], t["L0_attn_" + name][None, :].to_broadcast([P, NH])).then_inc(s_w, 16)
            for g in range(2, NB // 4):
                sp.dma_start(x_nat[:, 4 * g:4 * g + 4, :], x_rows[:, 4 * g:4 * g + 4, :]).then_inc(s_xl[g], 16)
            for k in ("wq", "wk", "wv", "wo"):
                sp.dma_start(wx_nat[k][:, :], t["L0_xattn_" + k]).then_inc(s_wx, 16)
            sp.dma_start(rw_nat[:, :], t["L0_ffn_router_w"]).then_inc(rw_ld, 16)
            sp.wait_ge(s_wTr, 4)
            for h in range(HEADS):
                g, q = divmod(h, HG)
                sp.dma_start(wo_pad[32 * q:32 * q + HD, g, :], wx_T["wo"][HD * h:HD * h + HD, :]).then_inc(s_wop, 16)

            def load_a(n, p):
                if isinstance(n, int) and n < 2:
                    sp.wait_ge(ln_d, n + 1)
                else:
                    sp.wait_ge(ln_d, NPAIR)
                    sp.wait_ge(tr_ps, n - 1)
                sp.dma_start(a_in[p][:, 0, :, :], x_nat[:, bass.ds(n * 2, 2), :]).then_inc(a_ld[p], 16)
                sp.dma_start(a_in[p][:, 1, :, :], ctx_rows[:, bass.ds(n * 2, 2), :]).then_inc(a_ld[p], 16)

            def restack(n, p, k):
                sp.wait_ge(q_st, 3 * n + 3)
                w = scr[p]
                for i in range(NPART):
                    sp.dma_start(w[:, i, :, :, :].rearrange("h d a s -> h d (a s)"),
                                 qk_part[p][:, i, :, :].rearrange("q a s -> q (a s)")).then_inc(scr_w[p], 16)
                for i in range(2):
                    sp.dma_start(w[:, NPART + i, :, 1, :], qk_part[p][:, i, 1, :]).then_inc(scr_w[p], 16)
                sp.wait_ge(scr_w[p], k * 80 + 80)
                if not isinstance(n, int) or n >= 2:
                    sp.wait_ge(t_ps, 8 * n - 8)
                for s_ in range(NPART):
                    for a, first in ((0, 0), (1, s_)):
                        sp.dma_start(stack[p][a][24 * s_:24 * s_ + 24, :, :],
                                     w[:, first:first + NPART, :, a, :].rearrange("h i d s -> (i d) h s")).then_inc(st_ld[p], 16)

            load_a(0, 0)
            load_a(1, 1)

            def half(n, p, turn, j, has):
                if j == 0 and has(0) and has(2):
                    load_a(n + 2, p)
                if j == 1 and has(2):
                    restack(*pair_at(n, p, turn, 2))
            rounds_of_pairs(sp, half)
            sp.wait_ge(row_c, NPAIR)
            hand_over(sp)
            srcs = [t["L0_ffn_gate_w"], t["L0_ffn_up_w"], t["L0_ffn_down_w"]]

            def load_w(k, e):
                if k < 2:
                    src = srcs[k][bass.ds(e, 1), :, :].rearrange("e (c f) d -> f (e c) d", c=FC)
                else:
                    src = srcs[k][bass.ds(e, 1), :, :].rearrange("e h (c f) -> h (e c) f", c=FC)
                sp.dma_start(w_nat[k][:, :, :], src).then_inc(wn_ld[k], 16)

            for k in range(3):
                load_w(k, 0)
            with sp.Fori(0, NE - 1) as e:
                for k in range(3):
                    sp.wait_ge(wn_tr, e * 3 + k + 1)
                    load_w(k, e + 1)
            sp.wait_ge(c3, C3N)
            sp.dma_start(slots[PAD_ROW:PAD_ROW + NE * P, :].rearrange("(b p) w -> p b w", p=P), pad_rows[:, NE:2 * NE, :]).then_inc(pad_w, 16)
            sp.wait_ge(tab, TABN)
            for k in range(2):
                sp.wait_ge(sc_d[k], 16 * 4 * NPAIR // 2)
            for e in range(NE):
                at = sp.value_load(pad_at[0:1, e:e + 1], min_val=e * CAP, max_val=e * CAP + TOKENS)
                sp.dma_start(slots[bass.ds(at, P), :], pad_rows[:, e, :]).then_inc(pad_w, 16)
            sp.wait_ge(pad_w, 16 * NE + 16)

            def load_tile(i, q, turn):
                wait(sp, m_lo, i - DEPTH + 1)
                at = sp.value_load(tile_row[0:1, bass.ds(i, 1)], min_val=0, max_val=PAD_ROW + (NE - 1) * P)
                sp.dma_start(xs_in[q][:, :], slots[bass.ds(at, P), :]).then_inc(xs_ld[q], 16)
            tiles(sp, (load_tile, 0))

            for q in range(DEPTH):
                sp.wait_ge(p_sc[q], 16 * NTILE // DEPTH)
            by_token = parts[0:TOKENS * TOPK, :].rearrange("(k m s) d -> s k m d", k=TOPK, s=S)

            def load_y(g, q):
                for k in range(TOPK):
                    sp.dma_start(y_in[q][:, k, :, :], by_token[:, k, bass.ds(g * 4, 4), :]).then_inc(f_ld[q], 16)

            def store(g, q):
                sp.wait_ge(f_n, g + 1)
                sp.dma_start(out_rows[:, bass.ds(g * 4, 4), :], f_o[q][:, :, :]).then_inc(f_w[q], 16)

            load_y(0, 0)
            load_y(1, 1)
            with sp.Fori(0, NG // 2 - 1) as i:
                for q in range(2):
                    store(i * 2 + q, q)
                    load_y(i * 2 + q + 2, q)
            for q in range(2):
                store(NG - 2 + q, q)
            for q in range(2):
                sp.wait_ge(f_w[q], 16 * NG // 2)

        @block.gpsimd
        def _(pool):
            def const(tile, fills, value):
                if const.n:
                    pool.wait_ge(s_pool, const.n)
                nc.gpsimd.memset(tile, value).then_inc(s_pool, 1)
                for op, base, pattern, cm, fill in fills:
                    const.n += 1
                    pool.wait_ge(s_pool, const.n)
                    nc.gpsimd.affine_select(out=tile, in_=tile, compare_op=op, fill=fill, base=base,
                                            pattern=pattern, channel_multiplier=cm).then_inc(s_pool, 1)
                const.n += 1
            const.n = 0
            const(ident[:, :], [(ALU.not_equal, 0, [[-1, P]], 1, 1.0)], 0.0)
            const(ident_bf[:, :], [(ALU.not_equal, 0, [[-1, P]], 1, 1.0)], 0.0)
            const(after[:, :], [(ALU.is_gt, 0, [[-1, P]], 1, 0.0)], 1.0)
            const(upto[:, :, :], [(ALU.is_ge, 0, [[0, NH], [1, P]], -1, 0.0)], 1.0)
            const(future[:, :, :], [(ALU.is_gt, 0, [[0, NH], [-1, P]], 1, 0.0)], NEG)
            const(ones_f[:, :], [], 1.0)
            const(half_ones[:, :], [], 1.0)
            for p in range(2):
                const(xh[p][:, :, :].bitcast(F32), [], 0.0)
                const(xl[p][:, :, :].bitcast(F32), [], 0.0)
            const(minus_half[:, :], [], -0.5)
            const(eps_pool[:, :], [], EPS)
            for j in range(2):
                const(nm_part[j][:, :, :], [], 0.0)
            for q in range(HG):
                const(sel_sum[:, 32 * q:32 * q + 32], [(ALU.not_equal, -(32 * q + HD), [[0, 32]], 1, 1.0)], 0.0)
            const(sel_max[:, :, :], [(ALU.not_equal, -HEADS * i, [[-1, HEADS], [0, P]], 1, 1.0) for i in range(NPART)], 0.0)
            const(mask_q[:, :, :], [(ALU.is_gt, 0, [[0, HG], [1, P]], -1, 0.0)], NEG)
            const(mask_k[:, :, :], [(ALU.is_gt, 0, [[0, HG], [-1, P]], 1, 0.0)], NEG)
            const(wo_pad[:, :, :], [], 0.0)
            for p in range(2):
                for j in range(2):
                    const(v_pad[p][j][:, :, :], [], 0.0)
                    const(v_pad[p][j][:, :, HD:HD + 1], [], 1.0)
            assert const.n == POOLN, const.n

            def ua_step(n, j):
                wait(pool, sg_ps[j], n)
                nc.gpsimd.tensor_tensor(ua[j][:, :, :], upto[:, :, :],
                                        dt_a[:, bass.ds(n * 2 + j, 1), :].rearrange("p b h -> p (b h)")[:, :, None].to_broadcast([P, NH, S]),
                                        ALU.mult).then_inc(ua_r[j], 1)

            def skip_step(n, j):
                pool.wait_ge(w_raw[j], n + 1)
                nc.gpsimd.tensor_tensor(w_sb[j][:, :, :], w_sb[j][:, :, :], d_diag[:, :, :],
                                        ALU.add).then_inc(w_r[j], 1)

            pool.wait_ge(s_dt, 4)
            pool.wait_ge(s_prep, PREP)
            for j in range(2):
                ua_step(0, j)

            def rms_step(n, p):
                pool.wait_ge(o_ev[1], n + 1)
                nc.gpsimd.tensor_tensor(r_gate[p][:, :], ss_eps[p][:, :], minus_half[:, :], ALU.pow).then_inc(rg_r, 1)

            def ln_rstd(n, p, base):
                pool.wait_ge(ln_v, (n + base) * 2 + 2)
                nc.gpsimd.tensor_tensor(v_eps[p][:, :], mv[p][:, :, 1], eps_pool[:, :], ALU.add).then_inc(ln_e, 1)
                pool.wait_ge(ln_e, n + base + 1)
                nc.gpsimd.tensor_tensor(r_ln[p][:, :], v_eps[p][:, :], minus_half[:, :], ALU.pow).then_inc(ln_r, 1)

            def body(n, p, nxt, nxt2, turn):
                for j in range(2):
                    if nxt:
                        ua_step(n + 1, j)
                    skip_step(n, j)
                rms_step(n, p)
                ln_rstd(n, p, 0)
            pairs(pool, body)

            made = [0]

            def const3(ins):
                made[0] += 1
                ins.then_inc(c3, 1)

            def sel3(tile, op, base_, pattern, fill):
                pool.wait_ge(c3, made[0])
                const3(nc.gpsimd.affine_select(out=tile, in_=tile, compare_op=op, fill=fill, base=base_, pattern=pattern,
                                               channel_multiplier=-1))
            const3(nc.gpsimd.memset(before[:, :], 1.0))
            sel3(before[:, :], ALU.is_gt, 0, [[1, P]], 0.0)
            const3(nc.gpsimd.memset(ones_b[:, :], 1.0))
            const3(nc.gpsimd.iota(iota_e[:, :], pattern=[[1, NE]], base=0, channel_multiplier=0, allow_small_or_imprecise_dtypes=True))
            const3(nc.gpsimd.iota(e_base[:, :], pattern=[[CAP, NE]], base=0, channel_multiplier=0, allow_small_or_imprecise_dtypes=True))
            const3(nc.gpsimd.iota(base[:, :], pattern=[[CAP, NE]], base=0, channel_multiplier=0, allow_small_or_imprecise_dtypes=True))
            const3(nc.gpsimd.iota(place[:, :, :], pattern=[[S, NB], [TOKENS, TOPK]], base=0, channel_multiplier=1, allow_small_or_imprecise_dtypes=True))
            assert made[0] == C2N

            def scatter(n, p, j, k):
                if j == 0 and k == 0:
                    pool.wait_ge(r_slot, n + 1)
                    wait_apart(pool, row_c, n + 1, n)
                nc.gpsimd.indirect_dma_start(out=slots, out_offset=bass.IndirectOffsetOnAxis(ap=slot_i[p][:, 2 * j + k:2 * j + k + 1], axis=0),
                                             in_=row[p][k][:, j, :], in_offset=None).then_inc(sc_d[p], 16)

            def half(n, p, turn, j, has):
                if j == 0 and has(-1):
                    ln_rstd(n - 1, 1 - p, NPAIR)
                if j == 1 and has(-2):
                    for b in range(2):
                        for k in range(TOPK):
                            scatter(n - 2, p, b, k)
            rounds_of_pairs(pool, half)
            hand_over(pool)
            const3(nc.gpsimd.memset(pad_rows[:, :, 0:D + 1], 0.0))
            const3(nc.gpsimd.iota(pad_rows[:, :, D + 1], pattern=[[P, 2 * NE]], base=TOKENS * TOPK, channel_multiplier=1, allow_small_or_imprecise_dtypes=True))
            const3(nc.gpsimd.iota(tile_no[:, :], pattern=[[1, NTILE]], base=0, channel_multiplier=0, allow_small_or_imprecise_dtypes=True))
            const3(nc.gpsimd.memset(minus_half4[:, :], -0.5))
            assert made[0] == C3N

            def scatter_parts(i, q, turn):
                wait_apart(pool, m_y, i + 1, i + NPAIR)
                nc.gpsimd.indirect_dma_start(out=parts, out_offset=bass.IndirectOffsetOnAxis(ap=part_i[q][:, 0:1], axis=0),
                                             in_=y_out[q][:, :], in_offset=None).then_inc(p_sc[q], 16)
            tiles(pool, (scatter_parts, 0))
            with pool.Fori(0, NG // 2) as i:
                for q in range(2):
                    pool.wait_ge(f_v, i * 2 + q + 1)
                    nc.gpsimd.tensor_tensor(f_r[q][:, :], f_ve[q][:, :], minus_half4[:, :], ALU.pow).then_inc(f_rr, 1)

        def dt_products(pe, g):
            pe.wait_ge(s_xT, g + 1)
            for k in range(4):
                m = 4 * g + k
                last = pe.matmul(bank[2][:, NH * m:NH * m + NH], xT[:, m, :], w_in[:, DTC:DTC + NH], start=True, stop=True)
            last.then_inc(s_dtps, 1)

        @block.tensor
        def _(pe):
            pe.wait_ge(s_pool, 10)
            for g in range(NB // 4):
                pe.wait_ge(s_xl[g], 16)
                if g >= 2:
                    pe.wait_ge(s_xT, g - 1)
                for k in range(4):
                    last = pe.transpose(bank[g % 2][:, k * P:(k + 1) * P], x_nat[:, 4 * g + k, :], ident[:, :])
                last.then_inc(s_xtr, 1)
                if g == 0:
                    pe.wait_ge(s_win, 16)
                if g >= 1:
                    dt_products(pe, g - 1)
            dt_products(pe, NB // 4 - 1)

            pe.wait_ge(s_prep, PREP)
            pe.wait_ge(s_pool, POOLN)
            pe.wait_ge(s_dt, 1)

            pe.wait_ge(s_cbrow, 1)

            def front_bc(n, p):
                pe.wait_ge(split_lo, n + 1)
                wait(pe, bc_gated, n)
                o = bank[0][:, 0:2 * S]
                pe.matmul(o, cb_rows[:, DI:CC], half_ones[:, :], start=True, stop=False)
                for k in range(TAPS):
                    for wt, xx in ((wconv_h, xh), (wconv_h, xl), (wconv_l, xh)):
                        last = pe.matmul(o, wt[:, k, DI:CC], xx[p][:, :, k:k + S], start=False,
                                         stop=(k == TAPS - 1 and wt is wconv_l))
                last.then_inc(bc_ps, 1)

            def front_z(n, p):
                wait(pe, z_ev, n)
                for h in range(NH):
                    o = bank[1][:, h * 2 * S:(h + 1) * 2 * S]
                    for q, (wt, xx) in enumerate(((wz_h, xh), (wz_h, xl), (wz_l, xh))):
                        last = pe.matmul(o, wt[:, h * P:(h + 1) * P], xx[p][:, :, TAPS - 1:TAPS - 1 + S],
                                         start=(q == 0), stop=(q == 2))
                last.then_inc(z_ps, 1)

            def front_x(n, p, j):
                wait(pe, x_gated[j], n)
                o = bank[2 + j][:, 0:DI]
                pe.matmul(o, half_ones[:, 0:P], cb_rows[:, 0:DI], start=True, stop=False)
                for k in range(TAPS):
                    for xx, wt in ((xh, wconv_h), (xl, wconv_h), (xh, wconv_l)):
                        last = pe.matmul(o, xx[p][:, j, k:k + S], wt[:, k, 0:DI], start=False,
                                         stop=(k == TAPS - 1 and wt is wconv_l))
                last.then_inc(x_ps[j], 1)

            def seg(n, p, j):
                pe.wait_ge(bc_gated, n + 1)
                pe.wait_ge(ua_r[j], n + 1)
                wait(pe, w_raw[j], n)
                b = bank[4 + j]
                pe.matmul(b[:, 0:S], b_sb[p][:, j * S:(j + 1) * S], c_sb[p][:, j * S:(j + 1) * S], start=True, stop=True)
                o = b[:, S:S + NH * S]
                pe.matmul(o, ident_bf[:, :], future[:, :, :], start=True, stop=False)
                pe.matmul(o, after[:, :], ua[j][:, :, :], start=False, stop=True).then_inc(sg_ps[j], 1)

            def yy(n, p, j):
                pe.wait_ge(w_r[j], n + 1)
                pe.wait_ge(xdt_r[j], n + 1)
                if j == 0:
                    wait(pe, y_r[1], n)
                else:
                    pe.wait_ge(y_r[0], n + 1)
                for h in range(NH):
                    last = pe.matmul(bank[6][:, h * S:(h + 1) * S], xdt[p][j][:, h * P:(h + 1) * P],
                                     w_sb[j][:, h, :], start=True, stop=True)
                last.then_inc(y_ps[j], 1)

            def oo(n, p, j):
                pe.wait_ge(sq_r[j], n + 1)
                if j == 0:
                    wait(pe, o_ev[1], n)
                else:
                    pe.wait_ge(o_ev[0], n + 1)
                for h in range(NH):
                    pe.matmul(bank[7][:, 0:D], y_sb[j][:, h, :], w_out[:, h, :], start=(h == 0), stop=(h == 1))
                for h in range(NH):
                    last = pe.matmul(bank[7][:, D:D + 1], sq_sb[j][:, h, :], ones_f[:, :], start=(h == 0), stop=(h == 1))
                last.then_inc(o_ps[j], 1)

            front_bc(0, 0)
            front_z(0, 0)
            front_x(0, 0, 0)
            front_x(0, 0, 1)

            def body(n, p, nxt, nxt2, turn):
                seg(n, p, 0)
                if nxt:
                    front_bc(n + 1, 1 - p)
                seg(n, p, 1)
                if nxt:
                    front_z(n + 1, 1 - p)
                yy(n, p, 0)
                if nxt:
                    front_x(n + 1, 1 - p, 0)
                yy(n, p, 1)
                oo(n, p, 0)
                if nxt:
                    front_x(n + 1, 1 - p, 1)
                oo(n, p, 1)
            pairs(pe, body)

            pe.wait_ge(s_wx, 64)
            for k, name in enumerate(("wq", "wk", "wv", "wo")):
                last = pe.transpose(bank[0][:, k * P:(k + 1) * P], wx_nat[name][:, :], ident[:, :])
            last.then_inc(s_wT, 4)
            pe.wait_ge(rw_ld, 16)
            pe.transpose(bank[1][:, 0:NE], rw_nat[:, :], ident[0:NE, 0:NE]).then_inc(rw_t, 1)
            def front_tr(n, p, k):
                pe.wait_ge(a_ld[p], k * 32 + 32)
                wait(pe, v_r, n)
                wait(pe, rt, (n - 4) * RT + 1 if not isinstance(n, int) or n >= 4 else 0)
                for a in range(2):
                    for j in range(2):
                        last = pe.transpose(bank[0][:, (2 * a + j) * P:(2 * a + j + 1) * P], a_in[p][:, a, j, :], ident[:, :])
                last.then_inc(tr_ps, 1)

            def front_qk(n, p):
                pe.wait_ge(aT_r, n + 1)
                wait(pe, q_st, 3 * n)
                wait(pe, rt, (n - 4) * RT + 13 if not isinstance(n, int) or n >= 4 else 0)
                for a, name in ((0, "wq"), (1, "wk")):
                    last = pe.matmul(bank[1][:, a * 2 * S:(a + 1) * 2 * S], wx_T[name][:, :], a_T[p][:, a, :], start=True, stop=True)
                last.then_inc(qk_ps, 1)

            def front_v(n, p):
                for j in range(2):
                    last = pe.matmul(bank[0][:, j * P:(j + 1) * P], a_T[p][:, 1, j * S:(j + 1) * S], wx_T["wv"][:, :], start=True, stop=True)
                last.then_inc(v_ps, 1)

            def scores(n, p, j, g, k):
                m = n * 2 + j
                if g == 0:
                    pe.wait_ge(st_ld[p], k * 96 + 96)
                    wait(pe, nmT_r, m)
                if g >= 2:
                    pe.wait_ge(red, m * 4 + g - 1)
                elif g == 1:
                    wait(pe, red, m * 4)
                b = bank[2 + g % 2]
                pe.matmul(b[:, :], ident_bf[:, :], mask_q[:, :, :], start=True, stop=False)
                for q in range(HG):
                    h = HG * g + q
                    last = pe.matmul(b[:, q * P:(q + 1) * P], stack[p][0][:, h, j * S:(j + 1) * S], stack[p][1][:, h, j * S:(j + 1) * S],
                                     start=False, stop=(q == HG - 1))
                last.then_inc(s_ps[g % 2], 1)

            def turn_max(n, j):
                m = n * 2 + j
                pe.wait_ge(nm_s, m * 4 + 4)
                pe.transpose(bank[2][:, 0:P // 2].bitcast(BF16), nm_part[j][:, :, :].rearrange("p i h -> p (i h)"),
                             ident_bf[:, :]).then_inc(nmT_ps, 1)

            def scores_T(n, p, j, g):
                m = n * 2 + j
                if g == 0:
                    pe.wait_ge(nmT_r, m + 1)
                if g >= 2:
                    pe.wait_ge(p_r, m * 4 + g - 1)
                else:
                    wait(pe, p_r, m * 4)
                b = bank[4 + g % 2]
                pe.matmul(b[:, :], ident_bf[:, :], mask_k[:, :, :], start=True, stop=False)
                for q in range(HG):
                    h = HG * g + q
                    o = b[:, q * P:(q + 1) * P]
                    pe.matmul(o, stack[p][1][:, h, j * S:(j + 1) * S], stack[p][0][:, h, j * S:(j + 1) * S], start=False, stop=False)
                    last = pe.matmul(o, sel_max[:, h, :], nm_T[j][:, :], start=False, stop=(q == HG - 1))
                last.then_inc(t_ps, 1)

            def values(n, p, j, g):
                m = n * 2 + j
                pe.wait_ge(p_r, m * 4 + g + 1)
                if g == 0:
                    pe.wait_ge(v_r, n + 1)
                    wait(pe, att_r, m)
                for q in range(HG):
                    last = pe.matmul(bank[6][32 * q:32 * q + 32, g * P:(g + 1) * P], v_pad[p][j][:, HG * g + q, :],
                                     pT[j][:, g, q * P:(q + 1) * P], start=True, stop=True)
                if g == HG - 1:
                    last.then_inc(pv_ps, 1)

            def sums(n, j):
                m = n * 2 + j
                pe.wait_ge(att_r, m + 1)
                wait(pe, ln_x, (m + NPAIR * 2))
                pe.matmul(bank[7][:, :], sel_sum[:, :], att[j][:, :], start=True, stop=True).then_inc(z2_ps, 1)

            def out_proj(n, j):
                m = n * 2 + j
                pe.wait_ge(an_r, m + 1)
                for g in range(HG):
                    last = pe.matmul(bank[7][:, 0:D], att[j][:, g * P:(g + 1) * P], wo_pad[:, g, :], start=(g == 0), stop=(g == HG - 1))
                last.then_inc(o2_ps, 1)

            pe.wait_ge(s_wTr, 4)
            pe.wait_ge(s_wop, 16 * HEADS)

            def turn_x2(n, p):
                pe.wait_ge(row_c, n + 1)
                wait(pe, v_r, n + 4 if not isinstance(n, int) else min(n + 4, NPAIR))
                for j in range(2):
                    last = pe.transpose(bank[0][:, j * P:(j + 1) * P], row[p][0][:, j, 0:D], ident[:, :])
                last.then_inc(r_tr, 1)

            def logits(n, p):
                pe.wait_ge(r_T, n + 1)
                for j in range(2):
                    last = pe.matmul(bank[0][:, 2 * S + j * NE:2 * S + (j + 1) * NE], x2T[p][:, j * S:(j + 1) * S], rw_T[:, :], start=True, stop=True)
                last.then_inc(r_lg, 1)

            def counts(n, p):
                pe.wait_ge(rt, n * RT + 8)
                wait(pe, q_st, 3 * (n + 4) if not isinstance(n, int) else min(3 * (n + 4), 3 * NPAIR))
                pe.matmul(bank[1][:, 0:NE], before[:, :], both[p][:, 0, :], start=True, stop=True)
                pe.matmul(bank[1][:, NE:2 * NE], before[:, :], both[p][:, 1, :], start=True, stop=False)
                pe.matmul(bank[1][:, NE:2 * NE], ones_b[:, :], both[p][:, 0, :], start=False, stop=True)
                pe.matmul(bank[1][:, 2 * NE:3 * NE], ones_b[:, :], both[p][:, 0, :], start=True, stop=False)
                pe.matmul(bank[1][:, 2 * NE:3 * NE], ones_b[:, :], both[p][:, 1, :], start=False, stop=True).then_inc(r_cnt, 1)

            def half(n, p, turn, j, has):
                np_, nj = (n, 1) if j == 0 else (n + 1, 0)
                bn, bj = (n - 1, 1) if j == 0 else (n, 0)
                cur, nxt, bef = has(0), has(1 if j else 0), has(0 if j else -1)
                nbuf = pair_at(n, p, turn, 1 if j else 0)

                def S_(g):
                    if nxt:
                        scores(nbuf[0], nbuf[1], nj, g, nbuf[2])

                def T_(g):
                    if cur:
                        scores_T(n, p, j, g)

                def V_(g):
                    if cur:
                        values(n, p, j, g)
                if j == 0 and has(-2):
                    turn_x2(n - 2, p)
                T_(0)
                S_(0)
                if j == 1 and has(-2):
                    counts(n - 2, p)
                T_(1)
                S_(1)
                if j == 0 and has(-2):
                    logits(n - 2, p)
                if j == 1 and has(2):
                    front_tr(*pair_at(n, p, turn, 2))
                if bef:
                    sums(bn, bj)
                V_(0)
                S_(2)
                T_(2)
                V_(1)
                if j == 1 and has(2):
                    front_qk(n + 2, p)
                    front_v(n + 2, p)
                S_(3)
                T_(3)
                V_(2)
                if bef:
                    out_proj(bn, bj)
                if nxt:
                    turn_max(np_, nj)
                V_(3)
            pe.wait_ge(rw_r, 1)
            pe.wait_ge(c3, C2N)
            rounds_of_pairs(pe, half)
            pe.wait_ge(ln_d, 2 * NPAIR)
            hand_over(pe)
            with pe.Fori(0, NE) as e:
                for k in range(3):
                    pe.wait_ge(wn_ld[k], e * 16 + 16)
                    pe.wait_ge(wn_free[k], e + 1)
                    for c in range(FC):
                        last = pe.transpose(bank[1 + k][:, c * P:(c + 1) * P], w_nat[k][:, c, :], ident[:, :])
                    last.then_inc(wn_tr, 1)

            pe.wait_ge(tab, TABN)

            def turn_tile(i, q, turn):
                pe.wait_ge(xs_ld[q], turn * 16 + 16)
                wait(pe, m_lo, i)
                pe.transpose(bank[0][:, 0:P], xs_in[q][:, 0:D], ident[:, :]).then_inc(m_tr, 1)

            def gate_up(i, q, turn):
                col = pe.value_load(tile_col[0:1, bass.ds(i, 1)], min_val=0, max_val=(NE - 1) * F)
                pe.wait_ge(m_lo, i + 1)
                for w, b, s_, free in ((wg, bank[1], m_g, m_sg), (wu, bank[2], m_u, m_hid)):
                    wait(pe, free, i)
                    for z_, (xx, part) in enumerate(((xeh, 0), (xel, 0), (xeh, 1))):
                        last = pe.matmul(b[:, :], xx[q][:, :], w[part][:, bass.ds(col, F)], start=(z_ == 0), stop=(z_ == 2))
                    last.then_inc(s_, 1)

            def turn_hid(i, q, turn):
                pe.wait_ge(m_hid, i + 1)
                wait(pe, m_hT, i)
                for c in range(FC):
                    last = pe.transpose(bank[3][:, c * P:(c + 1) * P], hid[q % 2][:, c * P:(c + 1) * P], ident[:, :])
                last.then_inc(m_ht, 1)

            def down(i, q, turn):
                col = pe.value_load(tile_col[0:1, bass.ds(i, 1)], min_val=0, max_val=(NE - 1) * F)
                pe.wait_ge(m_hT, i + 1)
                wait(pe, m_y, i)
                for c in range(FC):
                    last = pe.matmul(bank[4][:, 0:D], hT[q % 2][:, c * P:(c + 1) * P], wd[:, bass.ds(col + c * P, P)],
                                     start=(c == 0), stop=(c == FC - 1))
                last.then_inc(m_o, 1)
            tiles(pe, (turn_tile, 1), (gate_up, 0), (turn_hid, -1), (down, -2))

        @block.scalar
        def _(act):
            nc.scalar.preload_act_table_set("natural_log_exp_and_others")
            for g in range(NB // 4):
                act.wait_ge(s_xtr, g + 1)
                nc.scalar.activation(xT[:, 4 * g:4 * g + 4, :], bank[g % 2][:, :].rearrange("p (b s) -> p b s", b=4),
                                     ACT.Copy).then_inc(s_xT, 1)
            act.wait_ge(s_w, 16 * 7)
            nc.scalar.activation(a_neg[:, :], a_log[:, :], ACT.Exp).then_inc(s_aprep, 1)
            act.wait_ge(s_dt, 1)
            nc.scalar.activation(dt_e[:, :, :], dt_v[:, :, :], ACT.Abs).then_inc(s_dtx, 1)
            act.wait_ge(s_dtx, 1)
            nc.scalar.activation(dt_e[:, :, :], dt_e[:, :, :], ACT.Exp, scale=-1.0).then_inc(s_dtx, 1)
            act.wait_ge(s_dtx, 2)
            nc.scalar.activation(dt_e[:, :, :], dt_e[:, :, :], ACT.Ln, bias=1.0).then_inc(s_dtx, 1)
            nc.scalar.preload_act_table_set("exp_and_others")

            def hi(n, p):
                if not isinstance(n, int) or n >= 2:
                    act.wait_ge(x_ps[1], n - 1)
                nc.scalar.activation(xh[p][:, :, TAPS - 1:TAPS - 1 + S], xT[:, bass.ds(n * 2, 2), :], ACT.Copy).then_inc(split_hi, 1)

            def tanh_bc(n):
                act.wait_ge(bc_ps, n + 1)
                nc.scalar.activation(t_bc[:, :], bank[0][:, 0:2 * S], ACT.Tanh, scale=0.5).then_inc(t_bc_r, 1)

            def z_copy(n, p):
                act.wait_ge(z_ps, n + 1)
                if not isinstance(n, int) or n >= 2:
                    act.wait_ge(y_r[1], n - 1)
                nc.scalar.activation(z_sb[p][:, :, :].rearrange("p h s -> p (h s)"), bank[1][:, :], ACT.Copy).then_inc(z_ev, 1)

            def tanh_x(n, j):
                act.wait_ge(x_ps[j], n + 1)
                nc.scalar.activation(t_x[j][:, :], bank[2 + j][:, 0:DI], ACT.Tanh, scale=0.5).then_inc(t_x_r[j], 1)

            def xdt_step(n, p, j):
                act.wait_ge(x_gated[j], n + 1)
                if not isinstance(n, int) or n >= 2:
                    act.wait_ge(y_ps[j], n - 1)
                for h in range(NH):
                    last = nc.scalar.activation(xdt[p][j][:, h * P:(h + 1) * P], x_s[j][:, h * P:(h + 1) * P], ACT.Copy,
                                                scale=dt_half[:, bass.ds(n * 2 + j, 1), h])
                last.then_inc(xdt_r[j], 1)

            def e_step(n, j):
                act.wait_ge(sg_ps[j], n + 1)
                wait(act, w_raw[j], n)
                nc.scalar.activation(e_sb[j][:, :, :].rearrange("p h s -> p (h s)"), bank[4 + j][:, S:S + NH * S],
                                     ACT.Exp).then_inc(e_r[j], 1)

            def sq_step(n, j):
                act.wait_ge(y_r[j], n + 1)
                wait(act, o_ps[j], n)
                nc.scalar.activation(sq_sb[j][:, :, :], y_sb[j][:, :, :], ACT.Square, scale=1.0 / 16).then_inc(sq_r[j], 1)

            act.wait_ge(s_pool, POOLN)
            act.wait_ge(s_dt, 4)
            hi(0, 0)
            hi(1, 1)
            tanh_bc(0)
            z_copy(0, 0)
            for j in range(2):
                tanh_x(0, j)
                xdt_step(0, 0, j)

            def body(n, p, nxt, nxt2, turn):
                e_step(n, 0)
                if nxt:
                    tanh_bc(n + 1)
                e_step(n, 1)
                if nxt:
                    z_copy(n + 1, 1 - p)
                sq_step(n, 0)
                if nxt:
                    tanh_x(n + 1, 0)
                    xdt_step(n + 1, 1 - p, 0)
                sq_step(n, 1)
                if nxt2:
                    hi(n + 2, p)
                if nxt:
                    tanh_x(n + 1, 1)
                    xdt_step(n + 1, 1 - p, 1)
            pairs(act, body)
            for k, name in enumerate(("wq", "wk", "wv", "wo")):
                act.wait_ge(s_wT, 4)
                nc.scalar.activation(wx_T[name][:, :], bank[0][:, k * P:(k + 1) * P], ACT.Copy).then_inc(s_wTr, 1)
            act.wait_ge(rw_t, 1)
            nc.scalar.activation(rw_T[:, :], bank[1][:, 0:NE], ACT.Copy).then_inc(rw_r, 1)
            nc.scalar.preload_act_table_set("natural_log_exp_and_others")

            def copy_aT(n, p):
                act.wait_ge(tr_ps, n + 1)
                nc.scalar.activation(a_T[p][:, :, :].rearrange("p a s -> p (a s)"), bank[0][:, :], ACT.Copy).then_inc(aT_r, 1)

            def first_part(n, p, k):
                act.wait_ge(qk_ps, n + 1)
                if not isinstance(n, int) or n >= 2:
                    act.wait_ge(scr_w[p], k * 80)
                nc.scalar.activation(qk_part[p][:, 0, :, :].rearrange("p a s -> p (a s)"), bank[1][:, :], ACT.Copy).then_inc(qa_r, 1)

            def copy_v(n, p):
                act.wait_ge(v_ps, n + 1)
                for j in range(2):
                    last = nc.scalar.activation(v_pad[p][j][:, :, 0:HD],
                                                bank[0][:, j * P:(j + 1) * P].rearrange("p (h d) -> p h d", d=HD), ACT.Copy)
                last.then_inc(v_r, 1)

            def exps(n, j, g):
                m = n * 2 + j
                act.wait_ge(t_ps, m * 4 + g + 1)
                nc.scalar.activation(pT[j][:, g, :], bank[4 + g % 2][:, :], ACT.Exp, scale=HD ** -0.5).then_inc(p_r, 1)

            def copy_att(n, j):
                m = n * 2 + j
                act.wait_ge(pv_ps, m + 1)
                wait(act, o2_ps, m - 1)
                nc.scalar.activation(att[j][:, :], bank[6][:, :], ACT.Copy).then_inc(att_r, 1)

            def invert(n, j):
                m = n * 2 + j
                act.wait_ge(z2_ps, m + 1)
                nc.scalar.activation(inv[j][:, :], bank[7][:, :], ACT.Ln).then_inc(lnz, 1)
                act.wait_ge(lnz, m + 1)
                nc.scalar.activation(inv[j][:, :], inv[j][:, :], ACT.Exp, scale=-1.0).then_inc(inv_r, 1)

            def copy_row(n, p, turn):
                act.wait_ge(ln_d, NPAIR + n + 1)
                wait(act, sc_d[p], turn * 64)
                for k in range(TOPK):
                    nc.scalar.activation(row[p][k][:, :, 0:D], x_nat[:, bass.ds(n * 2, 2), :], ACT.Copy)
                    last = nc.scalar.activation(row[p][k][:, :, D + 1], place[:, bass.ds(n * 2, 2), k], ACT.Copy)
                last.then_inc(row_c, 1)

            def half(n, p, turn, j, has):
                bn, bj = (n - 1, 1) if j == 0 else (n, 0)
                cur, bef = has(0), has(0 if j else -1)
                if bef:
                    copy_att(bn, bj)
                if j == 0 and has(1):
                    copy_v(n + 1, 1 - p)
                if j == 0 and has(-2):
                    act.wait_ge(r_tr, n - 1)
                    nc.scalar.activation(x2T[p][:, :], bank[0][:, 0:2 * S], ACT.Copy).then_inc(r_T, 1)
                if cur:
                    exps(n, j, 0)
                if j == 1 and has(-2):
                    act.wait_ge(rt, (n - 2) * RT + 5)
                    nc.scalar.activation(ex[p][:, :, :], ex[p][:, :, :], ACT.Exp).then_inc(r_ex, 1)
                if cur:
                    exps(n, j, 1)
                if j == 1 and has(2):
                    copy_aT(n + 2, p)
                if bef:
                    invert(bn, bj)
                if cur:
                    exps(n, j, 2)
                if j == 1 and has(2):
                    first_part(*pair_at(n, p, turn, 2))
                if cur:
                    exps(n, j, 3)
                if j == 1 and has(-1):
                    copy_row(*pair_at(n, p, turn, -1))
            act.wait_ge(c3, C2N)
            rounds_of_pairs(act, half)
            hand_over(act)
            act.nop().then_inc(wn_free[2], 1)
            with act.Fori(0, NE) as e:
                for k, dst in enumerate((wg[0], wu[0], wd)):
                    act.wait_ge(wn_tr, e * 3 + k + 1)
                    nc.scalar.activation(dst[:, bass.ds(e * F, F)], bank[1 + k][:, :], ACT.Copy).then_inc(wn_hi if k < 2 else wn_free[2], 1)

            nc.scalar.preload_act_table_set("silu_and_others")

            def hi_tile(i, q, turn):
                act.wait_ge(m_tr, i + 1)
                wait(act, m_u, i - DEPTH + 1)
                nc.scalar.activation(xeh[q][:, :], bank[0][:, 0:P], ACT.Copy).then_inc(m_hi, 1)

            def silu(i, q, turn):
                act.wait_ge(m_g, i + 1)
                wait(act, m_hid, i - 1)
                nc.scalar.activation(sg[q % 2][:, :], bank[1][:, :], ACT.Silu).then_inc(m_sg, 1)

            def copy_hT(i, q, turn):
                act.wait_ge(m_ht, i + 1)
                wait(act, m_o, i - 1)
                nc.scalar.activation(hT[q % 2][:, :], bank[3][:, :], ACT.Copy).then_inc(m_hT, 1)
            tiles(act, (hi_tile, 1), (silu, 0), (copy_hT, -1))

            def norm(g, q, turn):
                act.wait_ge(f_bb, g + 1)
                wait(act, f_w[q], turn * 16)
                for b in range(4):
                    last = nc.scalar.activation(f_o[q][:, b, :], fin[q][:, b, :], ACT.Identity, bias=f_b[q][:, b:b + 1],
                                                scale=f_r[q][:, b:b + 1])
                last.then_inc(f_n, 1)
            for q in range(2):
                norm(q, q, 0)
            with act.Fori(1, NG // 2) as i:
                for q in range(2):
                    norm(i * 2 + q, q, i)

        @block.vector
        def _(dve):
            made = [0]

            def prep(ins):
                made[0] += 1
                ins.then_inc(s_prep, 1)
                dve.wait_ge(s_prep, made[0])

            dve.wait_ge(s_w, 16 * 7)
            dve.wait_ge(s_win, 16)
            dve.wait_ge(s_pool, 10)
            prep(nc.vector.tensor_copy(wz_h[:, :], w_in[:, 0:DI]))
            prep(nc.vector.tensor_tensor(wz_l[:, :], w_in[:, 0:DI], wz_h[:, :].bitcast(F32), ALU.subtract))
            for k in range(TAPS):
                prep(nc.vector.tensor_tensor(wconv[:, k, :], cw[:, k, :], w_in[:, ZX:ZX + CC], ALU.mult))
            prep(nc.vector.tensor_copy(cb_part[0][:, :], cb[:, :]))
            prep(nc.vector.tensor_copy(wconv_h[:, :, :], wconv[:, :, :]))
            prep(nc.vector.tensor_tensor(wconv_l[:, :, :], wconv[:, :, :], wconv_h[:, :, :].bitcast(F32), ALU.subtract))
            prep(nc.vector.tensor_tensor(cb_rest[:, :], cb[:, :], cb_part[0][:, :], ALU.subtract))
            prep(nc.vector.tensor_copy(cb_part[1][:, :], cb_rest[:, :]))
            prep(nc.vector.tensor_tensor(cb_part[2][:, :], cb_rest[:, :], cb_part[1][:, :], ALU.subtract))
            prep(nc.vector.tensor_scalar(cb_rows[:, :], cb_part[0][:, :], ident[0:3, 0:1], None, ALU.mult))
            for i in (1, 2):
                prep(nc.vector.scalar_tensor_tensor(out=cb_rows[:, :], in0=cb_part[i][:, :], scalar=ident[0:3, i:i + 1],
                                                    in1=cb_rows[:, :], op0=ALU.mult, op1=ALU.add))
            nc.vector.nop().then_inc(s_cbrow, 1)
            for h in range(NH):
                prep(nc.vector.tensor_scalar(w_out[:, h, :], w_out[:, h, :], nscale[:, h:h + 1], None, ALU.mult))
                prep(nc.vector.tensor_scalar(d_diag[:, h, :], ident[:, :], d_skip[:, h:h + 1], None, ALU.mult))
            assert made[0] == PREP, made[0]
            dve.wait_ge(s_dtps, NB // 4)
            nc.vector.tensor_tensor(dt_v[:, :, :], bank[2][:, 0:NB * NH].rearrange("p (b h) -> p b h", h=NH),
                                    dt_bias[:, None, :].to_broadcast([P, NB, NH]), ALU.add).then_inc(s_dt, 1)
            dve.wait_ge(s_dtx, 3)
            nc.vector.scalar_tensor_tensor(out=dt_v[:, :, :], in0=dt_v[:, :, :], scalar=0.0, in1=dt_e[:, :, :],
                                           op0=ALU.max, op1=ALU.add).then_inc(s_dt, 1)
            dve.wait_ge(s_dt, 2)
            nc.vector.tensor_scalar(dt_half[:, :, :], dt_v[:, :, :], 0.5, None, ALU.mult).then_inc(s_dt, 1)
            dve.wait_ge(s_aprep, 1)
            nc.vector.scalar_tensor_tensor(out=dt_a[:, :, :], in0=dt_v[:, :, :], scalar=-1.0,
                                           in1=a_neg[:, None, :].to_broadcast([P, NB, NH]), op0=ALU.mult,
                                           op1=ALU.mult).then_inc(s_dt, 1)

            def lo(n, p):
                dve.wait_ge(split_hi, n + 1)
                nc.vector.tensor_tensor(xl[p][:, :, TAPS - 1:TAPS - 1 + S], xT[:, bass.ds(n * 2, 2), :],
                                        xh[p][:, :, TAPS - 1:TAPS - 1 + S].bitcast(F32), ALU.subtract).then_inc(split_lo, 1)

            def gate_bc(n, p):
                dve.wait_ge(t_bc_r, n + 1)
                if not isinstance(n, int) or n >= 2:
                    dve.wait_ge(sg_ps[1], n - 1)
                for half, dst in ((0, b_sb[p]), (NS, c_sb[p])):
                    last = nc.vector.scalar_tensor_tensor(out=dst[:, :], in0=t_bc[half:half + NS, :], scalar=1.0,
                                                          in1=bank[0][half:half + NS, 0:2 * S], op0=ALU.add, op1=ALU.mult)
                last.then_inc(bc_gated, 1)

            def gate_x(n, j):
                dve.wait_ge(t_x_r[j], n + 1)
                wait(dve, xdt_r[j], n)
                nc.vector.scalar_tensor_tensor(out=x_s[j][:, :], in0=t_x[j][:, :], scalar=1.0, in1=bank[2 + j][:, 0:DI],
                                               op0=ALU.add, op1=ALU.mult).then_inc(x_gated[j], 1)

            def w_step(n, j):
                dve.wait_ge(e_r[j], n + 1)
                wait(dve, y_ps[j], n)
                nc.vector.scalar_tensor_tensor(out=w_sb[j][:, :, :], in0=e_sb[j][:, :, :], scalar=0.25,
                                               in1=bank[4 + j][:, None, 0:S].to_broadcast([P, NH, S]),
                                               op0=ALU.mult, op1=ALU.mult).then_inc(w_raw[j], 1)

            def y_step(n, p, j):
                dve.wait_ge(y_ps[j], n + 1)
                dve.wait_ge(z_ev, n + 1)
                wait(dve, o_ps[j], n)
                wait(dve, sq_r[j], n)
                nc.vector.tensor_tensor(y_sb[j][:, :, :], z_sb[p][:, :, j * S:(j + 1) * S],
                                        bank[6][:, 0:NH * S].rearrange("p (h s) -> p h s", h=NH), ALU.mult).then_inc(y_r[j], 1)

            def o_step(n, p, j):
                dve.wait_ge(o_ps[j], n + 1)
                nc.vector.tensor_copy(pr[p][j][:, :], bank[7][:, 0:D])
                nc.vector.tensor_scalar(ss_eps[p][:, j:j + 1], bank[7][:, D:D + 1], EPS, None, ALU.add).then_inc(o_ev[j], 1)

            def ln_stats(n, p, base):
                for j in range(2):
                    dve.wait_ge(ln_x, (n + base) * 2 + j + 1)
                    nc.vector.bn_stats(stats[p][j][:, :], xr[p][j][:, :]).then_inc(ln_s, 1)
                wait_apart(dve, ln_s, (n + base) * 2 + 2)
                for j in range(2):
                    nc.vector.bn_aggr(mv[p][:, j, :], stats[p][j][:, :]).then_inc(ln_v, 1)

            def ln_first(n, p):
                dve.wait_ge(rg_r, n + 1)
                for j in range(2):
                    nc.vector.scalar_tensor_tensor(out=xr[p][j][:, None, :], in0=pr[p][j][:, None, :], scalar=r_gate[p][:, j:j + 1],
                                                   in1=x_nat[:, bass.ds(n * 2 + j, 1), :], op0=ALU.mult, op1=ALU.add).then_inc(ln_x, 1)
                ln_stats(n, p, 0)

            def ln_norm(n, p, base):
                dve.wait_ge(ln_r, n + base + 1)
                for j in range(2):
                    last = nc.vector.tensor_scalar(x_nat[:, bass.ds(n * 2 + j, 1), :], xr[p][j][:, None, :], mv[p][:, j, 0:1],
                                                   r_ln[p][:, j:j + 1], ALU.subtract, ALU.mult)
                last.then_inc(ln_d, 1)

            dve.wait_ge(s_pool, POOLN)
            lo(0, 0)
            lo(1, 1)
            gate_bc(0, 0)
            gate_x(0, 0)
            gate_x(0, 1)

            def body(n, p, nxt, nxt2, turn):
                w_step(n, 0)
                if nxt:
                    gate_bc(n + 1, 1 - p)
                w_step(n, 1)
                y_step(n, p, 0)
                if nxt:
                    gate_x(n + 1, 0)
                y_step(n, p, 1)
                if nxt2:
                    lo(n + 2, p)
                o_step(n, p, 0)
                if nxt:
                    gate_x(n + 1, 1)
                o_step(n, p, 1)
                ln_first(n, p)
                ln_norm(n, p, 0)
            pairs(dve, body)
            def split_qk(n, p):
                dve.wait_ge(qa_r, n + 1)
                qk = bank[1][:, :].rearrange("p (a s) -> p a s", a=2)
                nc.vector.tensor_tensor(qk_rest[:, :, :], qk, qk_part[p][:, 0, :, :], ALU.subtract).then_inc(q_st, 1)
                dve.wait_ge(q_st, 3 * n + 1)
                nc.vector.tensor_copy(qk_part[p][:, 1, :, :], qk_rest[:, :, :]).then_inc(q_st, 1)
                dve.wait_ge(q_st, 3 * n + 2)
                nc.vector.tensor_tensor(qk_part[p][:, 2, :, :], qk_rest[:, :, :], qk_part[p][:, 1, :, :], ALU.subtract).then_inc(q_st, 1)

            def reduce_max(n, j, g):
                m = n * 2 + j
                dve.wait_ge(s_ps[g % 2], 2 * m + g // 2 + 1)
                nc.vector.tensor_reduce(mx[j][:, HG * g:HG * g + HG], bank[2 + g % 2][:, :].rearrange("p (h k) -> p h k", h=HG),
                                        AX_X, ALU.max).then_inc(red, 1)

            def split_max(n, j):
                m = n * 2 + j
                dve.wait_ge(red, m * 4 + 4)
                nc.vector.tensor_scalar(nm_part[j][:, 0, :], mx[j][:, :], -1.0, None, ALU.mult).then_inc(nm_s, 1)
                dve.wait_ge(nm_s, m * 4 + 1)
                nc.vector.scalar_tensor_tensor(out=nm_rest[j][:, :], in0=mx[j][:, :], scalar=-1.0, in1=nm_part[j][:, 0, :],
                                               op0=ALU.mult, op1=ALU.subtract).then_inc(nm_s, 1)
                dve.wait_ge(nm_s, m * 4 + 2)
                nc.vector.tensor_copy(nm_part[j][:, 1, :], nm_rest[j][:, :]).then_inc(nm_s, 1)
                dve.wait_ge(nm_s, m * 4 + 3)
                nc.vector.tensor_tensor(nm_part[j][:, 2, :], nm_rest[j][:, :], nm_part[j][:, 1, :], ALU.subtract).then_inc(nm_s, 1)

            def copy_nmT(n, j):
                m = n * 2 + j
                dve.wait_ge(nmT_ps, m + 1)
                nc.vector.tensor_copy(nm_T[j][:, :], bank[2][0:NPART * HEADS, 0:P // 2].bitcast(BF16)).then_inc(nmT_r, 1)

            def normalise(n, j):
                m = n * 2 + j
                dve.wait_ge(inv_r, m + 1)
                nc.vector.tensor_tensor(att[j][:, :], att[j][:, :], inv[j][:, :], ALU.mult).then_inc(an_r, 1)

            def residual(n, p, j):
                m = n * 2 + j
                dve.wait_ge(o2_ps, m + 1)
                nc.vector.tensor_tensor(xr[p][j][:, None, :], x_nat[:, bass.ds(m, 1), :], bank[7][:, None, 0:D], ALU.add).then_inc(ln_x, 1)

            def link(n, at, ins, apart=False):
                ins.then_inc(rt, 1)
                if apart:
                    wait_apart(dve, rt, n * RT + at)
                else:
                    dve.wait_ge(rt, n * RT + at)

            def route_top(n, p):
                dve.wait_ge(r_lg, n + 1)
                link(n, 1, nc.vector.tensor_copy(lg[p][:, :, :], bank[0][:, 2 * S:2 * S + 2 * NE].rearrange("p (b e) -> p b e", e=NE)), apart=True)
                nc.vector.max(top[p][:, 0, :], lg[p][:, 0, :])
                link(n, 2, nc.vector.max(top[p][:, 1, :], lg[p][:, 1, :]), apart=True)
                nc.vector.max_index(top_i[p][:, 0, :], top[p][:, 0, :], lg[p][:, 0, :])
                link(n, 3, nc.vector.max_index(top_i[p][:, 1, :], top[p][:, 1, :], lg[p][:, 1, :]))
                link(n, 4, nc.vector.tensor_tensor(ex[p][:, :, 0:NE], lg[p][:, :, :], top[p][:, :, 0:1].to_broadcast([P, 2, NE]), ALU.subtract))
                link(n, 5, nc.vector.tensor_tensor(ex[p][:, :, NE], top[p][:, :, 1], top[p][:, :, 0], ALU.subtract))

            def route_hot(n, p):
                link(n, 6, nc.vector.tensor_copy(top_f[p][:, :, :], top_i[p][:, :, 0:TOPK]))
                link(n, 7, nc.vector.tensor_tensor(hot[p][:, :, :, :].rearrange("p b k e -> p (b k) e"),
                                                   top_f[p][:, :, :].rearrange("p b k -> p (b k)")[:, :, None].to_broadcast([P, 2 * TOPK, NE]),
                                                   iota_e[:, None, :].to_broadcast([P, 2 * TOPK, NE]), ALU.is_equal))
                link(n, 8, nc.vector.tensor_tensor(both[p][:, :, :], hot[p][:, :, 0, :], hot[p][:, :, 1, :], ALU.add))

            def route_weights(n, p, turn):
                dve.wait_ge(r_ex, n + 1)
                link(n, 9, nc.vector.tensor_reduce(esum[p][:, :], ex[p][:, :, 0:NE], AX_X, ALU.add))
                wait(dve, sc_d[p], turn * 64)
                link(n, 10, nc.vector.reciprocal(row[p][0][:, :, D], esum[p][:, :]))
                link(n, 11, nc.vector.tensor_tensor(row[p][1][:, :, D], row[p][0][:, :, D], ex[p][:, :, NE], ALU.mult))

            def route_slots(n, p):
                dve.wait_ge(r_cnt, n + 1)
                link(n, 12, nc.vector.tensor_tensor(pos[p][:, :, :], bank[1][:, 0:2 * NE].rearrange("p (b e) -> p b e", e=NE),
                                                    base[:, None, :].to_broadcast([P, 2, NE]), ALU.add))
                link(n, 13, nc.vector.tensor_tensor(base[:, :], bank[1][:, 2 * NE:3 * NE], base[:, :], ALU.add))
                link(n, 14, nc.vector.tensor_tensor(picked[p][:, :, :, :], hot[p][:, :, :, :],
                                                    pos[p][:, :, None, :].to_broadcast([P, 2, TOPK, NE]), ALU.mult))
                link(n, 15, nc.vector.tensor_reduce(slot_f[p][:, :], picked[p][:, :, :, :].rearrange("p b k e -> p (b k) e"), AX_X, ALU.add))
                nc.vector.tensor_copy(slot_i[p][:, :], slot_f[p][:, :]).then_inc(r_slot, 1)

            def half(n, p, turn, j, has):
                np_, nj = (n, 1) if j == 0 else (n + 1, 0)
                bn, bj = (n - 1, 1) if j == 0 else (n, 0)
                bp = (1 - p) if j == 0 else p
                nxt, bef = has(1 if j else 0), has(0 if j else -1)
                if nxt:
                    reduce_max(np_, nj, 0)
                if j == 1 and has(-2):
                    route_weights(*pair_at(n, p, turn, -2))
                if nxt:
                    reduce_max(np_, nj, 1)
                if j == 0 and has(-2):
                    route_top(n - 2, p)
                if j == 1 and has(-1):
                    ln_norm(n - 1, 1 - p, NPAIR)
                if j == 1 and has(-2):
                    route_slots(n - 2, p)
                if nxt:
                    reduce_max(np_, nj, 2)
                if bef:
                    normalise(bn, bj)
                if nxt:
                    reduce_max(np_, nj, 3)
                    split_max(np_, nj)
                    copy_nmT(np_, nj)
                if bef:
                    residual(bn, bp, bj)
                if j == 0 and has(-2):
                    route_hot(n - 2, p)
                if j == 0 and has(-1):
                    ln_stats(n - 1, 1 - p, NPAIR)
                if j == 1 and has(2):
                    split_qk(n + 2, p)
            dve.wait_ge(c3, C2N)
            rounds_of_pairs(dve, half)
            hand_over(dve)
            for k in range(2):
                dve.nop().then_inc(wn_free[k], 1)
            with dve.Fori(0, NE) as e:
                for k, dst in enumerate((wg, wu)):
                    dve.wait_ge(wn_hi, e * 2 + k + 1)
                    nc.vector.tensor_tensor(dst[1][:, bass.ds(e * F, F)], bank[1 + k][:, :],
                                            dst[0][:, bass.ds(e * F, F)].bitcast(F32), ALU.subtract).then_inc(wn_free[k], 1)
            at = [0]

            def link(ins):
                at[0] += 1
                ins.then_inc(tab, 1)
                dve.wait_ge(tab, at[0])

            one = slice(0, 1)
            ROUND = float(2 ** 23)
            dve.wait_ge(rt, NPAIR * RT)
            dve.wait_ge(c3, C3N)
            link(nc.vector.tensor_tensor(cnt[:, :], base[one, :], e_base[one, :], ALU.subtract))
            link(nc.vector.tensor_scalar(ntile[:, :], cnt[:, :], 1.0 / P, (P - 1) / (2.0 * P), ALU.mult, ALU.add))
            link(nc.vector.tensor_scalar(ntile[:, :], ntile[:, :], ROUND, ROUND, ALU.add, ALU.subtract))
            link(nc.vector.memset(start[:, 0:1], 0.0))
            for e in range(NE):
                link(nc.vector.tensor_tensor(start[:, e + 1:e + 2], start[:, e:e + 1], ntile[:, e:e + 1], ALU.add))
            link(nc.vector.tensor_scalar(coef[:, :], ntile[:, :], -float(P), float(CAP), ALU.mult, ALU.add))
            link(nc.vector.tensor_tensor(passed[:, :, :], start[:, None, 1:NE + 1].to_broadcast([1, NTILE, NE]),
                                         tile_no[:, :, None].to_broadcast([1, NTILE, NE]), ALU.is_le))
            link(nc.vector.tensor_reduce(tile_e[:, :], passed[:, :, :], AX_X, ALU.add))
            link(nc.vector.tensor_tensor(passed_c[:, :, :], passed[:, :, :], coef[:, None, :].to_broadcast([1, NTILE, NE]), ALU.mult))
            link(nc.vector.tensor_reduce(tile_r[:, :], passed_c[:, :, :], AX_X, ALU.add))
            link(nc.vector.scalar_tensor_tensor(out=tile_row[:, :], in0=tile_no[:, :], scalar=float(P), in1=tile_r[:, :],
                                                op0=ALU.mult, op1=ALU.add))
            link(nc.vector.tensor_scalar(tile_col[:, :], tile_e[:, :], float(NE - 1), float(F), ALU.min, ALU.mult))
            link(nc.vector.tensor_copy(pad_at[:, :], base[one, :]))
            assert at[0] == TABN, at

            def lo_tile(i, q, turn):
                dve.wait_ge(m_hi, i + 1)
                wait(dve, m_y, i - DEPTH + 1)
                nc.vector.tensor_copy(w_place[q][:, :], xs_in[q][:, D:D + 2])
                nc.vector.tensor_tensor(xel[q][:, :], bank[0][:, 0:P], xeh[q][:, :].bitcast(F32), ALU.subtract).then_inc(m_lo, 1)

            def mul_up(i, q, turn):
                dve.wait_ge(m_sg, i + 1)
                dve.wait_ge(m_u, i + 1)
                wait(dve, m_ht, i - 1)
                nc.vector.tensor_tensor(hid[q % 2][:, :], sg[q % 2][:, :], bank[2][:, :], ALU.mult).then_inc(m_hid, 1)

            def scale_out(i, q, turn):
                dve.wait_ge(m_o, i + 1)
                wait(dve, p_sc[q], turn * 16)
                nc.vector.tensor_copy(part_i[q][:, :], w_place[q][:, 1:2])
                nc.vector.tensor_scalar(y_out[q][:, :], bank[4][:, 0:D], w_place[q][:, 0:1], None, ALU.mult).then_inc(m_y, 1)
            tiles(dve, (lo_tile, 1), (mul_up, 0), (scale_out, -2))

            def finish(g, q, turn):
                FC_ = 8
                dve.wait_ge(f_ld[q], turn * 32 + 32)
                wait(dve, f_n, g - 1) if isinstance(g, int) else dve.wait_ge(f_n, g - 1)
                nc.vector.tensor_tensor(fin[q][:, :, :], y_in[q][:, 0, :, :], y_in[q][:, 1, :, :], ALU.add).then_inc(f_c, 1)
                dve.wait_ge(f_c, g * FC_ + 1)
                nc.vector.tensor_tensor(fin[q][:, :, :], fin[q][:, :, :], x_nat[:, bass.ds(g * 4, 4), :], ALU.add).then_inc(f_c, 1)
                dve.wait_ge(f_c, g * FC_ + 2)
                for b in range(4):
                    last = nc.vector.bn_stats(f_st[q][:, b, :], fin[q][:, b, :])
                last.then_inc(f_c, 1)
                wait_apart(dve, f_c, g * FC_ + 3)
                for b in range(4):
                    last = nc.vector.bn_aggr(f_mv[q][:, b, :], f_st[q][:, b, :])
                last.then_inc(f_c, 1)
                dve.wait_ge(f_c, g * FC_ + 4)
                nc.vector.tensor_scalar(f_ve[q][:, :], f_mv[q][:, :, 1], EPS, None, ALU.add).then_inc(f_v, 1)
                dve.nop().then_inc(f_c, 4)
                dve.wait_ge(f_rr, g + 1)
                nc.vector.scalar_tensor_tensor(out=f_b[q][:, :], in0=f_mv[q][:, :, 0], scalar=-1.0, in1=f_r[q][:, :],
                                               op0=ALU.mult, op1=ALU.mult).then_inc(f_bb, 1)
            for q in range(2):
                finish(q, q, 0)
            with dve.Fori(1, NG // 2) as i:
                for q in range(2):
                    finish(i * 2 + q, q, i)


POOLN = 5 * 2 + 2 + 4 + 4 + 8 + 4 + 4 + 1 + 8
PREP = 19
C2N = 7
C3N = 11
RT = 15
TABN = 20


_INS = ["x", "ctx_1024", "L0_attn_W_in", "L0_attn_conv_w", "L0_attn_conv_b", "L0_attn_dt_bias", "L0_attn_A_log",
        "L0_attn_D", "L0_attn_norm_scale", "L0_attn_W_out", "L0_xattn_wq", "L0_xattn_wk", "L0_xattn_wv", "L0_xattn_wo",
        "L0_ffn_router_w", "L0_ffn_gate_w", "L0_ffn_up_w", "L0_ffn_down_w"]


def kernel(**inputs):
    import numpy as _np
    import concourse.bacc as _bacc
    from concourse import mybir as _mybir
    from concourse.bass_utils import run_bass_kernel_spmd as _run

    nc = _bacc.Bacc("TRN2", target_bir_lowering=False, num_devices=1)
    arrays, aps = {}, {}
    for name in _INS:
        a = _np.ascontiguousarray(inputs[name])
        arrays[f"in_{name}_dram"] = a
        aps[name] = nc.dram_tensor(f"in_{name}_dram", a.shape, _mybir.dt.from_np(a.dtype), kind="ExternalInput").ap()
    out = nc.dram_tensor("out_0_dram", inputs["x"].shape, _mybir.dt.float32, kind="ExternalOutput").ap()
    build(nc, aps, out)
    r = _run(nc, [arrays], core_ids=[0])
    return r.results[0]["out_0_dram"]
```

```python
from contextlib import ExitStack

import concourse.bass as bass
from concourse import mybir

F32 = mybir.dt.float32
F32R = mybir.dt.float32r
BF16 = mybir.dt.bfloat16
I32 = mybir.dt.int32
ALU = mybir.AluOpType
ACT = mybir.ActivationFunctionType
AX_X = mybir.AxisListType.X
P = 128
EPS = 1e-5
NEG = -30000.0

POOLN = 5 * 2 + 2 + 4 + 4 + 8 + 4 + 4 + 1 + 8
POOL1 = 18
PREP = 19
C2N = 7
C3N = 11
RT = 15
TABN = 20


def build(nc, t, out):
    NB, S, D = t["x"].shape
    DI = t["L0_attn_W_out"].shape[0]
    NH = t["L0_attn_D"].shape[0]
    TAPS, _, CC = t["L0_attn_conv_w"].shape
    NS = (CC - DI) // 2
    NPAIR = NB // 2
    assert (S, D, DI, NH, TAPS, NS) == (P, P, 2 * P, 2, 4, 64)
    ZX = DI
    DTC = DI + CC

    x_rows = t["x"].rearrange("b s d -> s b d")
    ctx_rows = t["ctx_1024"].rearrange("b s d -> s b d")
    out_rows = out.rearrange("b s d -> s b d")

    with ExitStack() as ctx:
        own = [ctx]

        def sb(name, shape, dt=F32):
            return own[-1].enter_context(nc.sbuf_tensor(name, shape, dt))

        def sem(name):
            return ctx.enter_context(nc.semaphore(name))

        def sem2(name):
            return [sem(name + "0"), sem(name + "1")]

        bank = [ctx.enter_context(nc.psum_tensor(f"bank{i}", [P, 512], F32)) for i in range(8)]

        ident = sb("ident", [P, P])
        x_nat = sb("x_nat", [P, NB, D])
        minus_half = sb("minus_half", [P, 2])
        eps_pool = sb("eps_pool", [P, 2])
        spare_pool = sb("spare_pool", [1, 1])
        spare_dve = sb("spare_dve", [1, 1])
        xr = [[sb(f"xr{p}{j}", [P, D]) for j in range(2)] for p in range(2)]
        stats = [[sb(f"stats{p}{j}", [P, 6]) for j in range(2)] for p in range(2)]
        mv = [sb(f"mv{p}", [P, 2, 2]) for p in range(2)]
        v_eps = [sb(f"v_eps{p}", [P, 2]) for p in range(2)]
        r_ln = [sb(f"r_ln{p}", [P, 2]) for p in range(2)]
        NE = t["L0_ffn_gate_w"].shape[0]
        F = t["L0_ffn_gate_w"].shape[1]
        TOPK = 2
        TOKENS = NB * S
        CAP = TOKENS + P
        WIDE = D + 2
        rw_nat = sb("rw_nat", [NE, D])
        rw_T = sb("rw_T", [P, NE])
        before = sb("before", [P, P], BF16)
        ones_b = sb("ones_b", [P, P], BF16)
        iota_e = sb("iota_e", [P, NE])
        e_base = sb("e_base", [P, NE])
        base = sb("base", [P, NE])
        place = sb("place", [P, NB, TOPK])
        row = [[sb(f"row{p}{k}", [P, 2, WIDE]) for k in range(TOPK)] for p in range(2)]
        x2T = [sb(f"x2T{p}", [P, 2 * S]) for p in range(2)]
        lg = [sb(f"lg{p}", [P, 2, NE]) for p in range(2)]
        top = [sb(f"top{p}", [P, 2, 8]) for p in range(2)]
        top_i = [sb(f"top_i{p}", [P, 2, 8], mybir.dt.uint32) for p in range(2)]
        ex = [sb(f"ex{p}", [P, 2, NE + 1]) for p in range(2)]
        esum = [sb(f"esum{p}", [P, 2]) for p in range(2)]
        top_f = [sb(f"top_f{p}", [P, 2, TOPK]) for p in range(2)]
        hot = [sb(f"hot{p}", [P, 2, TOPK, NE]) for p in range(2)]
        both = [sb(f"both{p}", [P, 2, NE], BF16) for p in range(2)]
        pos = [sb(f"pos{p}", [P, 2, NE]) for p in range(2)]
        picked = [sb(f"picked{p}", [P, 2, TOPK, NE]) for p in range(2)]
        slot_f = [sb(f"slot_f{p}", [P, 2 * TOPK]) for p in range(2)]
        slot_i = [sb(f"slot_i{p}", [P, 2 * TOPK], I32) for p in range(2)]
        FC = F // P
        w_nat = [[sb(f"w_nat{k}{b}", [P, FC, P]) for b in range(2)] for k in range(3)]
        early = ExitStack()
        own.append(early)
        ident_bf = sb("ident_bf", [P, P], BF16)
        ones_f = sb("ones_f", [P, 1])
        ones_rows = sb("ones_bf", [3, 2 * P], BF16)
        after = sb("after", [P, P])
        upto = sb("upto", [P, NH, P])
        future = sb("future", [P, NH, P], BF16)
        w_in = sb("w_in", [P, 2 * DI + 2 * NS + NH])
        wz_h = sb("wz_h", [P, DI], F32R)
        wz_l = sb("wz_l", [P, DI], F32R)
        cb = sb("cb", [3, CC])
        cb_part = [sb(f"cb_part{i}", [3, CC], BF16) for i in range(3)]
        cb_rest = sb("cb_rest", [3, CC])
        cb_rows = sb("cb_rows", [3, CC], BF16)
        w_out = sb("w_out", [P, NH, D])
        nscale = sb("nscale", [P, NH])
        a_log = sb("a_log", [P, NH])
        a_neg = sb("a_neg", [P, NH])
        dt_bias = sb("dt_bias", [P, NH])
        d_skip = sb("d_skip", [P, NH])
        d_diag = sb("d_diag", [P, NH, P])
        dt_v = sb("dt_v", [P, NB, NH])
        dt_e = sb("dt_e", [P, NB, NH])
        dt_half = sb("dt_half", [P, NB, NH])
        dt_a = sb("dt_a", [P, NB, NH])
        xh = [sb(f"xh{p}", [P, 2, S + 4], F32R) for p in range(2)]
        xl = [sb(f"xl{p}", [P, 2, S + 4], F32R) for p in range(2)]
        t_bc = sb("t_bc", [P, 2 * S])
        b_sb = [sb(f"b_sb{p}", [NS, 2 * S]) for p in range(2)]
        c_sb = [sb(f"c_sb{p}", [NS, 2 * S]) for p in range(2)]
        z_sb = [sb(f"z_sb{p}", [P, NH, 2 * S]) for p in range(2)]
        t_x = [sb(f"t_x{j}", [P, DI]) for j in range(2)]
        x_s = [sb(f"x_s{j}", [P, DI]) for j in range(2)]
        xdt = [[sb(f"xdt{p}{j}", [P, DI]) for j in range(2)] for p in range(2)]
        ua = [sb(f"ua{j}", [P, NH, S]) for j in range(2)]
        e_sb = [sb(f"e_sb{j}", [P, NH, S]) for j in range(2)]
        w_sb = [sb(f"w_sb{j}", [P, NH, S]) for j in range(2)]
        y_sb = [sb(f"y_sb{j}", [P, NH, S]) for j in range(2)]
        sq_sb = [sb(f"sq_sb{j}", [P, NH, S]) for j in range(2)]

        pr = [[sb(f"pr{p}{j}", [P, D]) for j in range(2)] for p in range(2)]
        ss_eps = [sb(f"ss_eps{p}", [P, 2]) for p in range(2)]
        r_gate = [sb(f"r_gate{p}", [P, 2]) for p in range(2)]
        HEADS, HD, HG = 16, 8, 4
        NPART = 3
        KROWS = NPART * NPART * HD
        wx_nat = {k: sb(f"{k}_nat", [P, D]) for k in ("wq", "wk", "wv", "wo")}
        wx_T = {k: sb(f"{k}_T", [P, D]) for k in ("wq", "wk", "wv", "wo")}
        wo_pad = sb("wo_pad", [P, HG, D])
        sel_sum = sb("sel_sum", [P, P])
        sel_max = sb("sel_max", [NPART * HEADS, HEADS, P], BF16)
        mask_q = sb("mask_q", [P, HG, P], BF16)
        mask_k = sb("mask_k", [P, HG, P], BF16)
        a_in = [sb(f"a_in{p}", [P, 2, 2, D]) for p in range(2)]
        a_T = [sb(f"a_T{p}", [P, 2, 2 * S]) for p in range(2)]
        qk_part = [sb(f"qk_part{p}", [P, NPART, 2, 2 * S], BF16) for p in range(2)]
        qk_rest = sb("qk_rest", [P, 2, 2 * S])
        v_pad = [[sb(f"v_pad{p}{j}", [P, HEADS, 32]) for j in range(2)] for p in range(2)]
        mx = [sb(f"mx{j}", [P, HEADS]) for j in range(2)]
        nm_part = [sb(f"nm_part{j}", [P, P // HEADS, HEADS], BF16) for j in range(2)]
        nm_rest = [sb(f"nm_rest{j}", [P, HEADS]) for j in range(2)]
        nm_T = [sb(f"nm_T{j}", [NPART * HEADS, P], BF16) for j in range(2)]
        pT = [sb(f"pT{j}", [P, HG, HG * P]) for j in range(2)]
        att = [sb(f"att{j}", [P, HG * P]) for j in range(2)]
        inv = [sb(f"inv{j}", [P, HG * P]) for j in range(2)]
        scr = [nc.dram_tensor(f"scr{p}", (HEADS, 5, HD, 2, 2 * S), BF16, kind="Internal").ap() for p in range(2)]

        first = ExitStack()
        own.append(first)
        cw = sb("cw", [P, TAPS, CC])
        wconv = sb("wconv", [P, TAPS, CC])
        wconv_h = sb("wconv_h", [P, TAPS, CC], F32R)
        wconv_l = sb("wconv_l", [P, TAPS, CC], F32R)
        xT = sb("xT", [P, NB, S])
        first.close()
        own.pop()
        stack = [[sb(f"stack{p}{s_}", [KROWS, HEADS, 2 * S], BF16) for s_ in range(2)] for p in range(2)]
        early.close()
        own.pop()
        NTILE = TOKENS * TOPK // P + NE
        PAD_ROW = NE * CAP
        slots = nc.dram_tensor("slots", (PAD_ROW + NE * P, WIDE), F32, kind="Internal").ap()
        parts = nc.dram_tensor("parts", (TOKENS * TOPK + 2 * NE * P, D), F32, kind="Internal").ap()
        pad_rows = sb("pad_rows", [P, 2 * NE, WIDE])
        tile_no = sb("tile_no", [1, NTILE])
        cnt = sb("cnt", [1, NE])
        ntile = sb("ntile", [1, NE])
        start = sb("start", [1, NE + 1])
        coef = sb("coef", [1, NE])
        passed = sb("passed", [1, NTILE, NE])
        passed_c = sb("passed_c", [1, NTILE, NE])
        tile_e = sb("tile_e", [1, NTILE])
        tile_r = sb("tile_r", [1, NTILE])
        tile_col = sb("tile_col", [1, NTILE], I32)
        tile_row = sb("tile_row", [1, NTILE], I32)
        pad_at = sb("pad_at", [1, NE], I32)
        w_all = sb("w_all", [P, 5, NE * F], F32R)
        wg, wu, wd = (w_all[:, 0, :], w_all[:, 1, :]), (w_all[:, 2, :], w_all[:, 3, :]), w_all[:, 4, :].bitcast(F32)
        DEPTH = 4
        xs_in = [sb(f"xs_in{q}", [P, WIDE]) for q in range(DEPTH)]
        w_place = [sb(f"w_place{q}", [P, 2]) for q in range(DEPTH)]
        half_x = [sb(f"half_x{q}", [P, D]) for q in range(DEPTH)]
        xeh = [sb(f"xeh{q}", [P, P], F32R) for q in range(DEPTH)]
        xel = [sb(f"xel{q}", [P, P], F32R) for q in range(DEPTH)]
        sg = [sb(f"sg{q}", [P, F]) for q in range(2)]
        hid = [sb(f"hid{q}", [P, F]) for q in range(2)]
        hT = [sb(f"hT{q}", [P, F]) for q in range(2)]
        y_out = [sb(f"y_out{q}", [P, D]) for q in range(DEPTH)]
        part_i = [sb(f"part_i{q}", [P, 1], I32) for q in range(DEPTH)]
        NG = NB // 4
        NQ = 4
        y_in = [sb(f"y_in{q}", [P, TOPK, 4, D]) for q in range(NQ)]
        fin = [sb(f"fin{q}", [P, 4, D]) for q in range(NQ)]
        f_st = [sb(f"f_st{q}", [P, 4, 6]) for q in range(NQ)]
        f_mv = [sb(f"f_mv{q}", [P, 4, 2]) for q in range(NQ)]
        f_ve = [sb(f"f_ve{q}", [P, 4]) for q in range(NQ)]
        f_r = [sb(f"f_r{q}", [P, 4]) for q in range(NQ)]
        f_b = [sb(f"f_b{q}", [P, 4]) for q in range(NQ)]
        f_o = [sb(f"f_o{q}", [P, 4, D]) for q in range(NQ)]
        minus_half4 = sb("minus_half4", [P, 4])

        s_w = sem("weights_loaded")
        s_win = sem("w_in_loaded")
        s_xl = [sem(f"x_loaded{g}") for g in range(NB // 4)]
        s_pool = sem("pool_consts")
        s_prep = sem("dve_prep")
        s_aprep = sem("act_prep")
        s_cbrow = sem("conv_bias_rows")
        s_xtr = sem("x_transposed")
        s_xT = sem("xT_ready")
        s_dtps = sem("dt_psum")
        s_dt = sem("dt_ready")
        s_dtx = sem("dt_exp")
        split_hi, split_lo = sem("split_hi"), sem("split_lo")
        bc_ps, z_ps, x_ps = sem("bc_ps"), sem("z_ps"), sem2("x_ps")
        t_bc_r, z_ev, t_x_r = sem("t_bc_r"), sem("z_ev"), sem2("t_x_r")
        bc_gated, x_gated, xdt_r = sem("bc_gated"), sem2("x_gated"), sem2("xdt_r")
        ua_r, sg_ps, e_r = sem2("ua_r"), sem2("sg_ps"), sem2("e_r")
        w_raw, w_r = sem2("w_raw"), sem2("w_r")
        y_ps, y_r, sq_r = sem2("y_ps"), sem2("y_r"), sem2("sq_r")
        o_ps, o_ev = sem2("o_ps"), sem2("o_ev")
        rg_r = sem("rg_r")
        ln_x, ln_s, ln_v, ln_r, ln_d = sem("ln_x"), sem("ln_s"), sem("ln_v"), sem("ln_r"), sem("ln_done")
        ln_e = sem("ln_e")
        s_wx = sem("attn_weights_loaded")
        s_wT = sem("attn_weights_T")
        s_wTr = sem("attn_weights_T_ready")
        s_wop = sem("wo_pad_written")
        a_ld = sem2("a_loaded")
        tr_ps, aT_r, qk_ps, qa_r, q_st, v_ps, v_r = (sem(n) for n in ("tr_ps", "aT_r", "qk_ps", "qa_r", "q_split", "v_ps", "v_r"))
        scr_w, st_ld = sem2("scratch_written"), sem2("stack_loaded")
        s_ps, red = sem2("s_ps"), sem("red")
        nm_s, nmT_ps, nmT_r = sem("nm_split"), sem("nmT_ps"), sem("nmT_r")
        t_ps, p_r, pv_ps, att_r = sem("t_ps"), sem("p_r"), sem("pv_ps"), sem("att_r")
        z2_ps, lnz, inv_r, an_r, o2_ps = (sem(n) for n in ("z2_ps", "ln_of_sum", "inv_r", "an_r", "o2_ps"))

        spare_w = sem("spare_written")
        early_done = sem("early_phases_done")
        c3, rw_ld, rw_t, rw_r = sem("consts3"), sem("rw_loaded"), sem("rw_turned"), sem("rw_ready")
        pad_w = sem("pad_rows_written")
        row_c, r_tr, r_T, r_lg = sem("row_copied"), sem("r_tr"), sem("r_T"), sem("r_logits")
        rt, r_ex, r_cnt, r_slot, sc_d = sem("rt_chain"), sem("r_ex"), sem("r_cnt"), sem("r_slot"), sem2("scattered")
        tab = sem("table_chain")
        wn_ld = [sem2(f"wn_ld{k}") for k in range(3)]
        wn_tr, wn_hi, wn_taken = sem("wn_tr"), sem("wn_hi"), [sem(f"wn_taken{k}") for k in range(3)]
        xs_ld = [sem(f"xs_loaded{q}") for q in range(DEPTH)]
        m_tr, m_hi, m_lo, m_g, m_u = (sem(n) for n in ("m_tr", "m_hi", "m_lo", "m_g", "m_u"))
        m_sg, m_hid, m_ht, m_hT, m_o, m_y, m_half = (sem(n) for n in ("m_sg", "m_hid", "m_ht", "m_hT", "m_o", "m_y", "m_half"))
        p_sc = [sem(f"parts_scattered{q}") for q in range(DEPTH)]
        f_ld = [sem(f"f_loaded{q}") for q in range(NQ)]
        f_mom = sem("f_moments")
        f_c, f_v, f_rr, f_bb, f_n, f_w = sem("f_summed"), sem("f_v"), sem("f_rr"), sem("f_bb"), sem("f_n"), [sem(f"f_written{q}") for q in range(NQ)]

        block = ctx.enter_context(nc.Block())

        def hand_over(eng):
            eng.drain().then_inc(early_done, 1)
            eng.wait_ge(early_done, 5)
        turned = ((bank[2], bank[3], bank[4]), (bank[5], bank[6], bank[1]))
        C0 = D

        def wait(eng, s, v):
            if not isinstance(v, int) or v > 0:
                eng.wait_ge(s, v)

        def wait_apart(eng, s, v, written=0):
            eng.wait_ge(s, v)
            if eng is nc.gpsimd:
                wait(eng, spare_w, written)
                nc.gpsimd.tensor_tensor(spare_pool[:, :], minus_half[0:1, 0:1], minus_half[0:1, 0:1], ALU.add).then_inc(spare_w, 1)
            else:
                nc.vector.memset(spare_dve[:, :], 0.0)

        def pad_experts(eng, experts):
            eng.wait_ge(tab, 1)
            for k in range(2):
                eng.wait_ge(sc_d[k], 16 * 4 * NPAIR // 2)
            for e in experts:
                at = eng.value_load(pad_at[0:1, e:e + 1], min_val=e * CAP, max_val=e * CAP + TOKENS)
                eng.dma_start(slots[bass.ds(at, P), :], pad_rows[:, e, :]).then_inc(pad_w, 16)

        def tiles(eng, *steps):
            def rounds(turn):
                for u in range(DEPTH):
                    for step, ahead in steps:
                        i = turn * DEPTH + u + ahead
                        if not isinstance(turn, int) or 0 <= i < NTILE:
                            step(i, (u + ahead) % DEPTH, turn + (u + ahead) // DEPTH)
            rounds(-1)
            rounds(0)
            with eng.Fori(1, NTILE // DEPTH - 1) as turn:
                rounds(turn)
            rounds(NTILE // DEPTH - 1)
            rounds(NTILE // DEPTH)

        def rounds_of_pairs(eng, half):
            def a_round(n, p, turn):
                for j in range(2):
                    half(n, p, turn, j, lambda k: not isinstance(n, int) or 0 <= n + k < NPAIR)
            for n in range(-1, 4):
                a_round(n, n % 2, n // 2)
            with eng.Fori(2, NPAIR // 2 - 1) as i:
                a_round(i * 2, 0, i)
                a_round(i * 2 + 1, 1, i)
            for n in range(NPAIR - 2, NPAIR):
                a_round(n, n % 2, n // 2)
            last_half(half, 0)

        def last_half(half, i):
            n = NPAIR + i // 2
            half(n, n % 2, n // 2, i % 2, lambda k: 0 <= n + k < NPAIR)

        def finish_and_turn(half, turn_experts):
            for i in range(1, 4):
                last_half(half, i)
                turn_experts(range(i - 1, i))

        def pair_at(n, p, turn, k):
            return n + k, (p + k) % 2, turn + (p + k) // 2

        def pairs(eng, body):
            body(0, 0, True, True, 0)
            body(1, 1, True, True, 0)
            with eng.Fori(1, NPAIR // 2 - 1) as i:
                body(i * 2, 0, True, True, i)
                body(i * 2 + 1, 1, True, True, i)
            body(NPAIR - 2, 0, True, False, NPAIR // 2 - 1)
            body(NPAIR - 1, 1, False, False, NPAIR // 2 - 1)

        @block.sync
        def _(sp):
            for g in range(2):
                sp.dma_start(x_nat[:, 4 * g:4 * g + 4, :], x_rows[:, 4 * g:4 * g + 4, :]).then_inc(s_xl[g], 16)
            sp.dma_start(w_in[:, :], t["L0_attn_W_in"]).then_inc(s_win, 16)
            sp.dma_start(cw[:, :, :].rearrange("p k c -> p (k c)"),
                         t["L0_attn_conv_w"].rearrange("k a c -> a (k c)").to_broadcast([P, TAPS * CC])).then_inc(s_w, 16)
            sp.dma_start(cb[:, :], t["L0_attn_conv_b"][None, :].to_broadcast([3, CC])).then_inc(s_w, 16)
            sp.dma_start(w_out[:, :, :], t["L0_attn_W_out"].rearrange("(h p) e -> p h e", p=P)).then_inc(s_w, 16)
            with nc.allow_non_contiguous_dma(reason="256 scales, once"):
                sp.dma_start(nscale[:, :], t["L0_attn_norm_scale"].rearrange("(h p) -> p h", p=P)).then_inc(s_w, 16)
            for dst, name in ((a_log, "A_log"), (dt_bias, "dt_bias"), (d_skip, "D")):
                sp.dma_start(dst[:, :], t["L0_attn_" + name][None, :].to_broadcast([P, NH])).then_inc(s_w, 16)
            for g in range(2, NB // 4):
                sp.dma_start(x_nat[:, 4 * g:4 * g + 4, :], x_rows[:, 4 * g:4 * g + 4, :]).then_inc(s_xl[g], 16)
            for k in ("wq", "wk", "wv", "wo"):
                sp.dma_start(wx_nat[k][:, :], t["L0_xattn_" + k]).then_inc(s_wx, 16)
            sp.dma_start(rw_nat[:, :], t["L0_ffn_router_w"]).then_inc(rw_ld, 16)
            sp.wait_ge(s_wTr, 4)
            sp.wait_ge(s_pool, POOLN)
            for h in range(HEADS):
                g, q = divmod(h, HG)
                sp.dma_start(wo_pad[32 * q:32 * q + HD, g, :], wx_T["wo"][HD * h:HD * h + HD, :]).then_inc(s_wop, 16)

            def load_a(n, p):
                if isinstance(n, int) and n < 2:
                    sp.wait_ge(ln_d, n + 1)
                else:
                    sp.wait_ge(ln_d, NPAIR)
                    sp.wait_ge(tr_ps, n - 1)
                sp.dma_start(a_in[p][:, 0, :, :], x_nat[:, bass.ds(n * 2, 2), :]).then_inc(a_ld[p], 16)
                sp.dma_start(a_in[p][:, 1, :, :], ctx_rows[:, bass.ds(n * 2, 2), :]).then_inc(a_ld[p], 16)

            def restack(n, p, k):
                sp.wait_ge(q_st, 3 * n + 3)
                w = scr[p]
                for i in range(NPART):
                    sp.dma_start(w[:, i, :, :, :].rearrange("h d a s -> h d (a s)"),
                                 qk_part[p][:, i, :, :].rearrange("q a s -> q (a s)")).then_inc(scr_w[p], 16)
                for i in range(2):
                    sp.dma_start(w[:, NPART + i, :, 1, :], qk_part[p][:, i, 1, :]).then_inc(scr_w[p], 16)
                sp.wait_ge(scr_w[p], k * 80 + 80)
                if not isinstance(n, int) or n >= 2:
                    sp.wait_ge(t_ps, 8 * n - 8)
                for s_ in range(NPART):
                    for a, first in ((0, 0), (1, s_)):
                        sp.dma_start(stack[p][a][24 * s_:24 * s_ + 24, :, :],
                                     w[:, first:first + NPART, :, a, :].rearrange("h i d s -> (i d) h s")).then_inc(st_ld[p], 16)

            load_a(0, 0)
            load_a(1, 1)
            restack(0, 0, 0)

            def half(n, p, turn, j, has):
                if j == 0 and has(0) and has(2):
                    load_a(n + 2, p)
                if j == 1 and has(2):
                    restack(*pair_at(n, p, turn, 2))
            srcs = [t["L0_ffn_gate_w"], t["L0_ffn_up_w"], t["L0_ffn_down_w"]]

            def load_w(k, e):
                wait(sp, wn_tr, (e - 2) * 3 + k + 1)
                if k < 2:
                    src = srcs[k][e:e + 1, :, :].rearrange("e (c f) d -> f (e c) d", c=FC)
                else:
                    src = srcs[k][e:e + 1, :, :].rearrange("e h (c f) -> h (e c) f", c=FC)
                sp.dma_start(w_nat[k][e % 2][:, :, :], src).then_inc(wn_ld[k][e % 2], 16)

            for e in range(2):
                for k in range(3):
                    load_w(k, e)

            rounds_of_pairs(sp, half)
            for i in range(1, 4):
                last_half(half, i)
            hand_over(sp)
            for e in range(2, NE):
                for k in range(3):
                    load_w(k, e)
            sp.wait_ge(c3, C3N)
            sp.dma_start(slots[PAD_ROW:PAD_ROW + NE * P, :].rearrange("(b p) w -> p b w", p=P), pad_rows[:, NE:2 * NE, :]).then_inc(pad_w, 16)
            pad_experts(sp, range(0, NE // 2))
            sp.wait_ge(pad_w, 16 * NE + 16)
            sp.wait_ge(tab, TABN)

            def load_tile(i, q, turn):
                wait(sp, m_lo, i - DEPTH + 1)
                wait(sp, m_half, i - DEPTH + 1)
                at = sp.value_load(tile_row[0:1, bass.ds(i, 1)], min_val=0, max_val=PAD_ROW + (NE - 1) * P)
                sp.dma_start(xs_in[q][:, :], slots[bass.ds(at, P), :]).then_inc(xs_ld[q], 16)
            tiles(sp, (load_tile, 0))

            for q in range(DEPTH):
                sp.wait_ge(p_sc[q], 16 * NTILE // DEPTH)
            by_token = parts[0:TOKENS * TOPK, :].rearrange("(k m s) d -> s k m d", k=TOPK, s=S)

            def load_y(g):
                wait(sp, f_c, g - NQ + 1)
                for k in range(TOPK):
                    sp.dma_start(y_in[g % NQ][:, k, :, :], by_token[:, k, g * 4:g * 4 + 4, :]).then_inc(f_ld[g % NQ], 16)

            for g in range(NG):
                load_y(g)
            for g in range(NG):
                sp.wait_ge(f_n, g + 1)
                sp.dma_start(out_rows[:, g * 4:g * 4 + 4, :], f_o[g % NQ][:, :, :]).then_inc(f_w[g % NQ], 16)
            for q in range(NQ):
                sp.wait_ge(f_w[q], 16 * NG // NQ)

        @block.gpsimd
        def _(pool):
            written = [0]

            def const(tile, fills, value):
                if written[0]:
                    pool.wait_ge(s_pool, written[0])
                nc.gpsimd.memset(tile, value).then_inc(s_pool, 1)
                for op, base, pattern, cm, fill in fills:
                    written[0] += 1
                    pool.wait_ge(s_pool, written[0])
                    nc.gpsimd.affine_select(out=tile, in_=tile, compare_op=op, fill=fill, base=base,
                                            pattern=pattern, channel_multiplier=cm).then_inc(s_pool, 1)
                written[0] += 1
            const(ident[:, :], [(ALU.not_equal, 0, [[-1, P]], 1, 1.0)], 0.0)
            const(ident_bf[:, :], [(ALU.not_equal, 0, [[-1, P]], 1, 1.0)], 0.0)
            const(after[:, :], [(ALU.is_gt, 0, [[-1, P]], 1, 0.0)], 1.0)
            const(upto[:, :, :], [(ALU.is_ge, 0, [[0, NH], [1, P]], -1, 0.0)], 1.0)
            const(future[:, :, :], [(ALU.is_gt, 0, [[0, NH], [-1, P]], 1, 0.0)], NEG)
            const(ones_f[:, :], [], 1.0)
            const(ones_rows[:, :], [], 1.0)
            for p in range(2):
                const(xh[p][:, :, :].bitcast(F32), [], 0.0)
                const(xl[p][:, :, :].bitcast(F32), [], 0.0)
            const(minus_half[:, :], [], -0.5)
            const(eps_pool[:, :], [], EPS)
            assert written[0] == POOL1, written[0]
            for j in range(2):
                const(nm_part[j][:, :, :], [], 0.0)
            for q in range(HG):
                const(sel_sum[:, 32 * q:32 * q + 32], [(ALU.not_equal, -(32 * q + HD), [[0, 32]], 1, 1.0)], 0.0)
            const(sel_max[:, :, :], [(ALU.not_equal, -HEADS * i, [[-1, HEADS], [0, P]], 1, 1.0) for i in range(NPART)], 0.0)
            const(mask_q[:, :, :], [(ALU.is_gt, 0, [[0, HG], [1, P]], -1, 0.0)], NEG)
            const(mask_k[:, :, :], [(ALU.is_gt, 0, [[0, HG], [-1, P]], 1, 0.0)], NEG)
            const(wo_pad[:, :, :], [], 0.0)
            for p in range(2):
                for j in range(2):
                    const(v_pad[p][j][:, :, :], [], 0.0)
                    const(v_pad[p][j][:, :, HD:HD + 1], [], 1.0)
            assert written[0] == POOLN, written[0]
            made = [0]

            def const3(ins):
                made[0] += 1
                ins.then_inc(c3, 1)

            def sel3(tile, op, base_, pattern, fill):
                pool.wait_ge(c3, made[0])
                const3(nc.gpsimd.affine_select(out=tile, in_=tile, compare_op=op, fill=fill, base=base_, pattern=pattern,
                                               channel_multiplier=-1))
            const3(nc.gpsimd.memset(before[:, :], 1.0))
            sel3(before[:, :], ALU.is_gt, 0, [[1, P]], 0.0)
            const3(nc.gpsimd.memset(ones_b[:, :], 1.0))
            const3(nc.gpsimd.iota(iota_e[:, :], pattern=[[1, NE]], base=0, channel_multiplier=0, allow_small_or_imprecise_dtypes=True))
            const3(nc.gpsimd.iota(e_base[:, :], pattern=[[CAP, NE]], base=0, channel_multiplier=0, allow_small_or_imprecise_dtypes=True))
            const3(nc.gpsimd.iota(base[:, :], pattern=[[CAP, NE]], base=0, channel_multiplier=0, allow_small_or_imprecise_dtypes=True))
            const3(nc.gpsimd.iota(place[:, :, :], pattern=[[S, NB], [TOKENS, TOPK]], base=0, channel_multiplier=1, allow_small_or_imprecise_dtypes=True))
            assert made[0] == C2N

            def ua_step(n, j):
                wait(pool, sg_ps[j], n)
                nc.gpsimd.tensor_tensor(ua[j][:, :, :], upto[:, :, :],
                                        dt_a[:, bass.ds(n * 2 + j, 1), :].rearrange("p b h -> p (b h)")[:, :, None].to_broadcast([P, NH, S]),
                                        ALU.mult).then_inc(ua_r[j], 1)

            def skip_step(n, j):
                pool.wait_ge(w_raw[j], n + 1)
                nc.gpsimd.tensor_tensor(w_sb[j][:, :, :], w_sb[j][:, :, :], d_diag[:, :, :],
                                        ALU.add).then_inc(w_r[j], 1)

            pool.wait_ge(s_dt, 4)
            pool.wait_ge(s_prep, PREP)
            for j in range(2):
                ua_step(0, j)

            def rms_step(n, p):
                pool.wait_ge(o_ev[1], n + 1)
                nc.gpsimd.tensor_tensor(r_gate[p][:, :], ss_eps[p][:, :], minus_half[:, :], ALU.pow).then_inc(rg_r, 1)

            def ln_rstd(n, p, base):
                pool.wait_ge(ln_v, (n + base) * 2 + 2)
                nc.gpsimd.tensor_tensor(v_eps[p][:, :], mv[p][:, :, 1], eps_pool[:, :], ALU.add).then_inc(ln_e, 1)
                pool.wait_ge(ln_e, n + base + 1)
                nc.gpsimd.tensor_tensor(r_ln[p][:, :], v_eps[p][:, :], minus_half[:, :], ALU.pow).then_inc(ln_r, 1)

            def body(n, p, nxt, nxt2, turn):
                for j in range(2):
                    if nxt:
                        ua_step(n + 1, j)
                    skip_step(n, j)
                if not isinstance(n, int) or n:
                    ln_rstd(n - 1, 1 - p, 0)
                rms_step(n, p)
            pairs(pool, body)
            ln_rstd(NPAIR - 1, 1, 0)

            pool.drain().then_inc(early_done, 1)

            def scatter(n, p, j, k):
                if j == 0 and k == 0:
                    pool.wait_ge(r_slot, n + 1)
                    wait_apart(pool, row_c, n + 1, n)
                nc.gpsimd.indirect_dma_start(out=slots, out_offset=bass.IndirectOffsetOnAxis(ap=slot_i[p][:, 2 * j + k:2 * j + k + 1], axis=0),
                                             in_=row[p][k][:, j, :], in_offset=None).then_inc(sc_d[p], 16)

            def half(n, p, turn, j, has):
                if j == 0 and has(-1):
                    ln_rstd(n - 1, 1 - p, NPAIR)
                if j == 1 and has(-2):
                    for b in range(2):
                        for k in range(TOPK):
                            scatter(n - 2, p, b, k)
            rounds_of_pairs(pool, half)
            pool.wait_ge(early_done, 5)
            const3(nc.gpsimd.memset(pad_rows[:, :, 0:D + 1], 0.0))
            const3(nc.gpsimd.iota(pad_rows[:, :, D + 1], pattern=[[P, 2 * NE]], base=TOKENS * TOPK, channel_multiplier=1, allow_small_or_imprecise_dtypes=True))
            const3(nc.gpsimd.iota(tile_no[:, :], pattern=[[1, NTILE]], base=0, channel_multiplier=0, allow_small_or_imprecise_dtypes=True))
            const3(nc.gpsimd.memset(minus_half4[:, :], -0.5))
            assert made[0] == C3N
            for i in range(1, 4):
                last_half(half, i)

            def scatter_parts(i, q, turn):
                wait_apart(pool, m_y, i + 1, i + NPAIR)
                nc.gpsimd.indirect_dma_start(out=parts, out_offset=bass.IndirectOffsetOnAxis(ap=part_i[q][:, 0:1], axis=0),
                                             in_=y_out[q][:, :], in_offset=None).then_inc(p_sc[q], 16)
            tiles(pool, (scatter_parts, 0))
            for g in range(NG):
                pool.wait_ge(f_v, g + 1)
                nc.gpsimd.tensor_tensor(f_r[g % NQ][:, :], f_ve[g % NQ][:, :], minus_half4[:, :], ALU.pow).then_inc(f_rr, 1)

        def dt_products(pe, g):
            pe.wait_ge(s_xT, g + 1)
            for k in range(4):
                m = 4 * g + k
                last = pe.matmul(bank[6][:, NH * m:NH * m + NH], xT[:, m, :], w_in[:, DTC:DTC + NH], start=True, stop=True)
            last.then_inc(s_dtps, 1)

        @block.tensor
        def _(pe):
            pe.wait_ge(s_pool, 10)
            for g in range(NB // 4):
                pe.wait_ge(s_xl[g], 16)
                if g >= 2:
                    pe.wait_ge(s_xT, g - 1)
                for k in range(4):
                    last = pe.transpose(bank[g % 2][:, k * P:(k + 1) * P], x_nat[:, 4 * g + k, :], ident[:, :])
                last.then_inc(s_xtr, 1)
                if g == 0:
                    pe.wait_ge(s_win, 16)
                if g >= 1:
                    dt_products(pe, g - 1)
            dt_products(pe, NB // 4 - 1)

            pe.wait_ge(s_wx, 64)
            for k, name in enumerate(("wq", "wk", "wv", "wo")):
                last = pe.transpose(bank[4][:, k * P:(k + 1) * P], wx_nat[name][:, :], ident[:, :])
            last.then_inc(s_wT, 4)
            pe.wait_ge(rw_ld, 16)
            pe.transpose(bank[5][:, 0:NE], rw_nat[:, :], ident[0:NE, 0:NE]).then_inc(rw_t, 1)

            pe.wait_ge(s_prep, PREP)
            pe.wait_ge(s_pool, POOL1)

            pe.wait_ge(s_cbrow, 1)

            def front_tr(n, p, k):
                pe.wait_ge(a_ld[p], k * 32 + 32)
                wait(pe, v_r, n)
                wait(pe, rt, (n - 4) * RT + 1 if not isinstance(n, int) or n >= 4 else 0)
                for a in range(2):
                    for j in range(2):
                        last = pe.transpose(bank[0][:, (2 * a + j) * P:(2 * a + j + 1) * P], a_in[p][:, a, j, :], ident[:, :])
                last.then_inc(tr_ps, 1)

            def front_qk(n, p):
                pe.wait_ge(aT_r, n + 1)
                wait(pe, q_st, 3 * n)
                for a, name in ((0, "wq"), (1, "wk")):
                    last = pe.matmul(bank[1][:, a * 2 * S:(a + 1) * 2 * S], wx_T[name][:, :], a_T[p][:, a, :], start=True, stop=True)
                last.then_inc(qk_ps, 1)

            def front_v(n, p):
                for j in range(2):
                    last = pe.matmul(bank[0][:, j * P:(j + 1) * P], a_T[p][:, 1, j * S:(j + 1) * S], wx_T["wv"][:, :], start=True, stop=True)
                last.then_inc(v_ps, 1)

            def front_bc(n, p):
                pe.wait_ge(split_lo, n + 1)
                wait(pe, bc_gated, n)
                o = bank[0][:, 0:2 * S]
                pe.matmul(o, cb_rows[:, DI:CC], ones_rows[:, :], start=True, stop=False)
                for k in range(TAPS):
                    for wt, xx in ((wconv_h, xh), (wconv_h, xl), (wconv_l, xh)):
                        last = pe.matmul(o, wt[:, k, DI:CC], xx[p][:, :, k:k + S], start=False,
                                         stop=(k == TAPS - 1 and wt is wconv_l))
                last.then_inc(bc_ps, 1)

            def front_z(n, p):
                wait(pe, z_ev, n)
                for h in range(NH):
                    o = bank[1][:, h * 2 * S:(h + 1) * 2 * S]
                    for q, (wt, xx) in enumerate(((wz_h, xh), (wz_h, xl), (wz_l, xh))):
                        last = pe.matmul(o, wt[:, h * P:(h + 1) * P], xx[p][:, :, TAPS - 1:TAPS - 1 + S],
                                         start=(q == 0), stop=(q == 2))
                last.then_inc(z_ps, 1)

            def front_x(n, p, j):
                wait(pe, x_gated[j], n)
                o = bank[2 + j][:, 0:DI]
                pe.matmul(o, ones_rows[:, 0:P], cb_rows[:, 0:DI], start=True, stop=False)
                for k in range(TAPS):
                    for xx, wt in ((xh, wconv_h), (xl, wconv_h), (xh, wconv_l)):
                        last = pe.matmul(o, xx[p][:, j, k:k + S], wt[:, k, 0:DI], start=False,
                                         stop=(k == TAPS - 1 and wt is wconv_l))
                last.then_inc(x_ps[j], 1)

            def seg(n, p, j):
                pe.wait_ge(bc_gated, n + 1)
                pe.wait_ge(ua_r[j], n + 1)
                wait(pe, w_raw[j], n)
                if isinstance(n, int) and n == 0:
                    pe.wait_ge(rw_r, 1) if j else pe.wait_ge(s_wTr, 4)
                b = bank[4 + j]
                pe.matmul(b[:, 0:S], b_sb[p][:, j * S:(j + 1) * S], c_sb[p][:, j * S:(j + 1) * S], start=True, stop=True)
                o = b[:, S:S + NH * S]
                pe.matmul(o, ident_bf[:, :], future[:, :, :], start=True, stop=False)
                pe.matmul(o, after[:, :], ua[j][:, :, :], start=False, stop=True).then_inc(sg_ps[j], 1)

            def yy(n, p, j):
                pe.wait_ge(w_r[j], n + 1)
                pe.wait_ge(xdt_r[j], n + 1)
                if j == 0:
                    wait(pe, y_r[1], n)
                else:
                    pe.wait_ge(y_r[0], n + 1)
                for h in range(NH):
                    last = pe.matmul(bank[6][:, h * S:(h + 1) * S], xdt[p][j][:, h * P:(h + 1) * P],
                                     w_sb[j][:, h, :], start=True, stop=True)
                last.then_inc(y_ps[j], 1)

            def oo(n, p, j):
                pe.wait_ge(sq_r[j], n + 1)
                if j == 0:
                    wait(pe, o_ev[1], n)
                else:
                    pe.wait_ge(o_ev[0], n + 1)
                for h in range(NH):
                    pe.matmul(bank[7][:, 0:D], y_sb[j][:, h, :], w_out[:, h, :], start=(h == 0), stop=(h == 1))
                for h in range(NH):
                    last = pe.matmul(bank[7][:, D:D + 1], sq_sb[j][:, h, :], ones_f[:, :], start=(h == 0), stop=(h == 1))
                last.then_inc(o_ps[j], 1)

            front_bc(0, 0)
            front_z(0, 0)
            front_x(0, 0, 0)
            front_x(0, 0, 1)

            def body(n, p, nxt, nxt2, turn):
                seg(n, p, 0)
                if nxt:
                    front_bc(n + 1, 1 - p)
                if not nxt:
                    front_tr(0, 0, 0)
                seg(n, p, 1)
                if nxt:
                    front_z(n + 1, 1 - p)
                else:
                    pe.wait_ge(z_ev, NPAIR)
                    front_qk(0, 0)
                    front_v(0, 0)
                yy(n, p, 0)
                if nxt:
                    front_x(n + 1, 1 - p, 0)
                yy(n, p, 1)
                oo(n, p, 0)
                if nxt:
                    front_x(n + 1, 1 - p, 1)
                oo(n, p, 1)
            pairs(pe, body)

            def scores(n, p, j, g, k):
                m = n * 2 + j
                if g == 0:
                    pe.wait_ge(st_ld[p], k * 96 + 96)
                    wait(pe, nmT_r, m)
                if g >= 2:
                    pe.wait_ge(red, m * 4 + g - 1)
                elif g == 1:
                    wait(pe, red, m * 4)
                b = bank[2 + g % 2]
                pe.matmul(b[:, :], ident_bf[:, :], mask_q[:, :, :], start=True, stop=False)
                for q in range(HG):
                    h = HG * g + q
                    last = pe.matmul(b[:, q * P:(q + 1) * P], stack[p][0][:, h, j * S:(j + 1) * S], stack[p][1][:, h, j * S:(j + 1) * S],
                                     start=False, stop=(q == HG - 1))
                last.then_inc(s_ps[g % 2], 1)

            def turn_max(n, j):
                m = n * 2 + j
                pe.wait_ge(nm_s, m * 4 + 4)
                pe.transpose(bank[2][:, 0:P // 2].bitcast(BF16), nm_part[j][:, :, :].rearrange("p i h -> p (i h)"),
                             ident_bf[:, :]).then_inc(nmT_ps, 1)

            def scores_T(n, p, j, g):
                m = n * 2 + j
                if g == 0:
                    pe.wait_ge(nmT_r, m + 1)
                if g >= 2:
                    pe.wait_ge(p_r, m * 4 + g - 1)
                else:
                    wait(pe, p_r, m * 4)
                b = bank[4 + g % 2]
                pe.matmul(b[:, :], ident_bf[:, :], mask_k[:, :, :], start=True, stop=False)
                for q in range(HG):
                    h = HG * g + q
                    o = b[:, q * P:(q + 1) * P]
                    pe.matmul(o, stack[p][1][:, h, j * S:(j + 1) * S], stack[p][0][:, h, j * S:(j + 1) * S], start=False, stop=False)
                    last = pe.matmul(o, sel_max[:, h, :], nm_T[j][:, :], start=False, stop=(q == HG - 1))
                last.then_inc(t_ps, 1)

            def values(n, p, j, g):
                m = n * 2 + j
                pe.wait_ge(p_r, m * 4 + g + 1)
                if g == 0:
                    pe.wait_ge(v_r, n + 1)
                    wait(pe, att_r, m)
                for q in range(HG):
                    last = pe.matmul(bank[6][32 * q:32 * q + 32, g * P:(g + 1) * P], v_pad[p][j][:, HG * g + q, :],
                                     pT[j][:, g, q * P:(q + 1) * P], start=True, stop=True)
                if g == HG - 1:
                    last.then_inc(pv_ps, 1)

            def sums(n, j):
                m = n * 2 + j
                pe.wait_ge(att_r, m + 1)
                wait(pe, ln_x, (m + NPAIR * 2))
                if j == 0:
                    wait(pe, rt, (n - 2) * RT + 10 if not isinstance(n, int) or n >= 2 else 0)
                pe.matmul(bank[7][:, :], sel_sum[:, :], att[j][:, :], start=True, stop=True).then_inc(z2_ps, 1)

            def out_proj(n, j):
                m = n * 2 + j
                pe.wait_ge(an_r, m + 1)
                for g in range(HG):
                    last = pe.matmul(bank[7][:, 0:D], att[j][:, g * P:(g + 1) * P], wo_pad[:, g, :], start=(g == 0), stop=(g == HG - 1))
                last.then_inc(o2_ps, 1)

            pe.wait_ge(s_wTr, 4)
            pe.wait_ge(s_wop, 16 * HEADS)

            def turn_x2(n, p):
                pe.wait_ge(row_c, n + 1)
                wait(pe, v_r, n + 4 if not isinstance(n, int) else min(n + 4, NPAIR))
                for j in range(2):
                    last = pe.transpose(bank[0][:, j * P:(j + 1) * P], row[p][0][:, j, 0:D], ident[:, :])
                last.then_inc(r_tr, 1)

            def logits(n, p):
                pe.wait_ge(r_T, n + 1)
                for j in range(2):
                    last = pe.matmul(bank[0][:, 2 * S + j * NE:2 * S + (j + 1) * NE], x2T[p][:, j * S:(j + 1) * S], rw_T[:, :], start=True, stop=True)
                last.then_inc(r_lg, 1)

            def counts(n, p):
                pe.wait_ge(rt, n * RT + 8)
                wait(pe, ln_x, 2 * (n + 2) + 2 * NPAIR if not isinstance(n, int) else min(2 * (n + 2), 2 * NPAIR) + 2 * NPAIR)
                pe.matmul(bank[7][:, C0:C0 + NE], before[:, :], both[p][:, 0, :], start=True, stop=True)
                pe.matmul(bank[7][:, C0 + NE:C0 + 2 * NE], before[:, :], both[p][:, 1, :], start=True, stop=False)
                pe.matmul(bank[7][:, C0 + NE:C0 + 2 * NE], ones_b[:, :], both[p][:, 0, :], start=False, stop=True)
                pe.matmul(bank[7][:, C0 + 2 * NE:C0 + 3 * NE], ones_b[:, :], both[p][:, 0, :], start=True, stop=False)
                pe.matmul(bank[7][:, C0 + 2 * NE:C0 + 3 * NE], ones_b[:, :], both[p][:, 1, :], start=False, stop=True).then_inc(r_cnt, 1)

            def half(n, p, turn, j, has):
                np_, nj = (n, 1) if j == 0 else (n + 1, 0)
                bn, bj = (n - 1, 1) if j == 0 else (n, 0)
                cur, nxt, bef = has(0), has(1 if j else 0), has(0 if j else -1)
                nbuf = pair_at(n, p, turn, 1 if j else 0)

                def S_(g):
                    if nxt:
                        scores(nbuf[0], nbuf[1], nj, g, nbuf[2])

                def T_(g):
                    if cur:
                        scores_T(n, p, j, g)

                def V_(g):
                    if cur:
                        values(n, p, j, g)
                T_(0)
                if j == 1 and has(2):
                    front_tr(*pair_at(n, p, turn, 2))
                S_(0)
                if j == 1 and has(-2):
                    counts(n - 2, p)
                T_(1)
                if j == 1 and has(2):
                    front_qk(n + 2, p)
                S_(1)
                if bef:
                    sums(bn, bj)
                if j == 0 and has(-2):
                    turn_x2(n - 2, p)
                V_(0)
                S_(2)
                if j == 0 and has(-2):
                    logits(n - 2, p)
                T_(2)
                V_(1)
                if j == 1 and has(2):
                    front_v(n + 2, p)
                S_(3)
                T_(3)
                V_(2)
                if bef:
                    out_proj(bn, bj)
                if nxt:
                    turn_max(np_, nj)
                V_(3)
            pe.wait_ge(rw_r, 1)
            pe.wait_ge(c3, C2N)
            rounds_of_pairs(pe, half)
            hand_over(pe)

            def turn_experts(experts):
                for e in experts:
                    for k in range(3):
                        pe.wait_ge(wn_ld[k][e % 2], e // 2 * 16 + 16)
                        wait(pe, wn_taken[k], e - 1)
                        for c in range(FC):
                            last = pe.transpose(turned[e % 2][k][:, c * P:(c + 1) * P], w_nat[k][e % 2][:, c, :], ident[:, :])
                        last.then_inc(wn_tr, 1)
            finish_and_turn(half, turn_experts)
            turn_experts(range(3, NE))

            pe.wait_ge(tab, TABN)

            def turn_tile(i, q, turn):
                pe.wait_ge(xs_ld[q], turn * 16 + 16)
                wait(pe, m_lo, i)
                pe.transpose(bank[0][:, 0:P], xs_in[q][:, 0:D], ident[:, :]).then_inc(m_tr, 1)

            cols = {}

            def find_first(i, q, turn):
                if q == 0:
                    cols[0] = pe.value_load(tile_col[0:1, bass.ds(i, 1)], min_val=0, max_val=(NE - 1) * F)

            def find_others(i, q, turn):
                if q == 0:
                    first = i - 2 if not isinstance(i, int) or i else 0
                    number = DEPTH + 2 if not isinstance(i, int) or i else DEPTH
                    _, got = nc.values_load_multi_w_load_instructions(
                        tile_col[0:1, bass.ds(first, number)], engines=[mybir.EngineType.PE], min_val=0, max_val=(NE - 1) * F,
                        skip_runtime_bounds_check_because="the table holds min(expert, NE - 1) * F")
                    for k in range(number):
                        cols[k - number + DEPTH] = got[k]

            def gate_up(i, q, turn):
                mine = w_all[:, 0:4, bass.ds(cols[q], F)]
                pe.wait_ge(m_lo, i + 1)
                for w, b, s_, free in ((0, bank[1], m_g, m_sg), (2, bank[2], m_u, m_hid)):
                    wait(pe, free, i)
                    for z_, (xx, part) in enumerate(((xeh, 0), (xel, 0), (xeh, 1))):
                        last = pe.matmul(b[:, :], xx[q][:, :], mine[:, w + part, :], start=(z_ == 0), stop=(z_ == 2))
                    last.then_inc(s_, 1)

            def turn_hid(i, q, turn):
                pe.wait_ge(m_hid, i + 1)
                wait(pe, m_hT, i)
                for c in range(FC):
                    last = pe.transpose(bank[3][:, c * P:(c + 1) * P], hid[q % 2][:, c * P:(c + 1) * P], ident[:, :])
                last.then_inc(m_ht, 1)

            def down(i, q, turn):
                last_two = isinstance(i, int) and i >= NTILE - 2
                mine = w_all[:, 4:5, bass.ds(cols[q if last_two else (q + 2) % DEPTH - 2], F)].bitcast(F32)
                pe.wait_ge(m_hT, i + 1)
                wait(pe, m_y, i)
                for c in range(FC):
                    last = pe.matmul(bank[4][:, 0:D], hT[q % 2][:, c * P:(c + 1) * P], mine[:, 0, c * P:(c + 1) * P],
                                     start=(c == 0), stop=(c == FC - 1))
                last.then_inc(m_o, 1)
            tiles(pe, (find_first, 0), (turn_tile, 1), (gate_up, 0), (find_others, 0), (turn_hid, -1), (down, -2))

        @block.scalar
        def _(act):
            nc.scalar.preload_act_table_set("natural_log_exp_and_others")
            for g in range(NB // 4):
                act.wait_ge(s_xtr, g + 1)
                nc.scalar.activation(xT[:, 4 * g:4 * g + 4, :], bank[g % 2][:, :].rearrange("p (b s) -> p b s", b=4),
                                     ACT.Copy).then_inc(s_xT, 1)
            act.wait_ge(s_w, 16 * 7)
            nc.scalar.activation(a_neg[:, :], a_log[:, :], ACT.Exp).then_inc(s_aprep, 1)
            def hi(n, p):
                if not isinstance(n, int) or n >= 2:
                    act.wait_ge(x_ps[1], n - 1)
                nc.scalar.activation(xh[p][:, :, TAPS - 1:TAPS - 1 + S], xT[:, bass.ds(n * 2, 2), :], ACT.Copy).then_inc(split_hi, 1)

            act.wait_ge(s_pool, POOL1)
            hi(0, 0)
            hi(1, 1)
            act.wait_ge(s_dt, 1)
            nc.scalar.activation(dt_e[:, :, :], dt_v[:, :, :], ACT.Abs).then_inc(s_dtx, 1)
            act.wait_ge(s_dtx, 1)
            nc.scalar.activation(dt_e[:, :, :], dt_e[:, :, :], ACT.Exp, scale=-1.0).then_inc(s_dtx, 1)
            act.wait_ge(s_dtx, 2)
            nc.scalar.activation(dt_e[:, :, :], dt_e[:, :, :], ACT.Ln, bias=1.0).then_inc(s_dtx, 1)
            nc.scalar.preload_act_table_set("exp_and_others")

            def tanh_bc(n):
                act.wait_ge(bc_ps, n + 1)
                nc.scalar.activation(t_bc[:, :], bank[0][:, 0:2 * S], ACT.Tanh, scale=0.5).then_inc(t_bc_r, 1)

            def z_copy(n, p):
                act.wait_ge(z_ps, n + 1)
                if not isinstance(n, int) or n >= 2:
                    act.wait_ge(y_r[1], n - 1)
                nc.scalar.activation(z_sb[p][:, :, :].rearrange("p h s -> p (h s)"), bank[1][:, :], ACT.Copy).then_inc(z_ev, 1)

            def tanh_x(n, j):
                act.wait_ge(x_ps[j], n + 1)
                nc.scalar.activation(t_x[j][:, :], bank[2 + j][:, 0:DI], ACT.Tanh, scale=0.5).then_inc(t_x_r[j], 1)

            def xdt_step(n, p, j):
                act.wait_ge(x_gated[j], n + 1)
                if not isinstance(n, int) or n >= 2:
                    act.wait_ge(y_ps[j], n - 1)
                for h in range(NH):
                    last = nc.scalar.activation(xdt[p][j][:, h * P:(h + 1) * P], x_s[j][:, h * P:(h + 1) * P], ACT.Copy,
                                                scale=dt_half[:, bass.ds(n * 2 + j, 1), h])
                last.then_inc(xdt_r[j], 1)

            def e_step(n, j):
                act.wait_ge(sg_ps[j], n + 1)
                wait(act, w_raw[j], n)
                nc.scalar.activation(e_sb[j][:, :, :].rearrange("p h s -> p (h s)"), bank[4 + j][:, S:S + NH * S],
                                     ACT.Exp).then_inc(e_r[j], 1)

            def sq_step(n, j):
                act.wait_ge(y_r[j], n + 1)
                wait(act, o_ps[j], n)
                nc.scalar.activation(sq_sb[j][:, :, :], y_sb[j][:, :, :], ACT.Square, scale=1.0 / 16).then_inc(sq_r[j], 1)

            def copy_aT(n, p):
                act.wait_ge(tr_ps, n + 1)
                nc.scalar.activation(a_T[p][:, :, :].rearrange("p a s -> p (a s)"), bank[0][:, :], ACT.Copy).then_inc(aT_r, 1)

            def first_part(n, p, k):
                act.wait_ge(qk_ps, n + 1)
                if not isinstance(n, int) or n >= 2:
                    act.wait_ge(scr_w[p], k * 80)
                nc.scalar.activation(qk_part[p][:, 0, :, :].rearrange("p a s -> p (a s)"), bank[1][:, :], ACT.Copy).then_inc(qa_r, 1)

            for k, name in enumerate(("wq", "wk", "wv", "wo")):
                act.wait_ge(s_wT, 4)
                nc.scalar.activation(wx_T[name][:, :], bank[4][:, k * P:(k + 1) * P], ACT.Copy).then_inc(s_wTr, 1)
            act.wait_ge(rw_t, 1)
            nc.scalar.activation(rw_T[:, :], bank[5][:, 0:NE], ACT.Copy).then_inc(rw_r, 1)
            act.wait_ge(s_dt, 4)
            tanh_bc(0)
            z_copy(0, 0)
            for j in range(2):
                tanh_x(0, j)
                xdt_step(0, 0, j)

            def body(n, p, nxt, nxt2, turn):
                e_step(n, 0)
                if nxt:
                    tanh_bc(n + 1)
                if not nxt:
                    copy_aT(0, 0)
                e_step(n, 1)
                if nxt:
                    z_copy(n + 1, 1 - p)
                else:
                    first_part(0, 0, 0)
                sq_step(n, 0)
                if nxt:
                    tanh_x(n + 1, 0)
                    xdt_step(n + 1, 1 - p, 0)
                sq_step(n, 1)
                if nxt2:
                    hi(n + 2, p)
                if nxt:
                    tanh_x(n + 1, 1)
                    xdt_step(n + 1, 1 - p, 1)
            pairs(act, body)
            nc.scalar.preload_act_table_set("natural_log_exp_and_others")

            def copy_v(n, p):
                act.wait_ge(v_ps, n + 1)
                for j in range(2):
                    last = nc.scalar.activation(v_pad[p][j][:, :, 0:HD],
                                                bank[0][:, j * P:(j + 1) * P].rearrange("p (h d) -> p h d", d=HD), ACT.Copy)
                last.then_inc(v_r, 1)

            def exps(n, j, g):
                m = n * 2 + j
                act.wait_ge(t_ps, m * 4 + g + 1)
                nc.scalar.activation(pT[j][:, g, :], bank[4 + g % 2][:, :], ACT.Exp, scale=HD ** -0.5).then_inc(p_r, 1)

            def copy_att(n, j):
                m = n * 2 + j
                act.wait_ge(pv_ps, m + 1)
                wait(act, o2_ps, m - 1)
                nc.scalar.activation(att[j][:, :], bank[6][:, :], ACT.Copy).then_inc(att_r, 1)

            def invert(n, j):
                m = n * 2 + j
                act.wait_ge(z2_ps, m + 1)
                nc.scalar.activation(inv[j][:, :], bank[7][:, :], ACT.Ln).then_inc(lnz, 1)
                act.wait_ge(lnz, m + 1)
                nc.scalar.activation(inv[j][:, :], inv[j][:, :], ACT.Exp, scale=-1.0).then_inc(inv_r, 1)

            def copy_row(n, p, turn):
                act.wait_ge(ln_d, NPAIR + n + 1)
                wait(act, sc_d[p], turn * 64)
                for k in range(TOPK):
                    nc.scalar.activation(row[p][k][:, :, 0:D], x_nat[:, bass.ds(n * 2, 2), :], ACT.Copy)
                    last = nc.scalar.activation(row[p][k][:, :, D + 1], place[:, bass.ds(n * 2, 2), k], ACT.Copy)
                last.then_inc(row_c, 1)

            def half(n, p, turn, j, has):
                bn, bj = (n - 1, 1) if j == 0 else (n, 0)
                cur, bef = has(0), has(0 if j else -1)
                if bef:
                    copy_att(bn, bj)
                if j == 0 and has(1):
                    copy_v(n + 1, 1 - p)
                if j == 1 and has(2):
                    copy_aT(n + 2, p)
                if cur:
                    exps(n, j, 0)
                if j == 1 and has(2):
                    first_part(*pair_at(n, p, turn, 2))
                if cur:
                    exps(n, j, 1)
                if j == 0 and has(-2):
                    act.wait_ge(r_tr, n - 1)
                    nc.scalar.activation(x2T[p][:, :], bank[0][:, 0:2 * S], ACT.Copy).then_inc(r_T, 1)
                if bef:
                    invert(bn, bj)
                if cur:
                    exps(n, j, 2)
                    exps(n, j, 3)
                if j == 1 and has(-2):
                    act.wait_ge(rt, (n - 2) * RT + 5)
                    nc.scalar.activation(ex[p][:, :, :], ex[p][:, :, :], ACT.Exp).then_inc(r_ex, 1)
                if j == 1 and has(-1):
                    copy_row(*pair_at(n, p, turn, -1))
            act.wait_ge(c3, C2N)
            rounds_of_pairs(act, half)
            hand_over(act)

            def turn_experts(experts):
                for e in experts:
                    for k, dst in enumerate((wg[0], wu[0], wd)):
                        act.wait_ge(wn_tr, e * 3 + k + 1)
                        nc.scalar.activation(dst[:, e * F:(e + 1) * F], turned[e % 2][k][:, :], ACT.Copy).then_inc(wn_hi if k < 2 else wn_taken[2], 1)
            finish_and_turn(half, turn_experts)
            turn_experts(range(3, 5))
            act.wait_ge(c3, C3N)
            pad_experts(act, range(NE // 2, NE))
            turn_experts(range(5, NE))
            nc.scalar.preload_act_table_set("silu_and_others")

            def hi_tile(i, q, turn):
                act.wait_ge(m_tr, i + 1)
                wait(act, m_u, i - DEPTH + 1)
                wait(act, m_y, i - DEPTH + 1)
                nc.scalar.activation(xeh[q][:, :], bank[0][:, 0:P], ACT.Copy).then_inc(m_hi, 1)
                nc.scalar.activation(half_x[q][:, :], xs_in[q][:, 0:D], ACT.Copy, scale=0.5).then_inc(m_half, 1)

            def silu(i, q, turn):
                act.wait_ge(m_g, i + 1)
                wait(act, m_hid, i - 1)
                nc.scalar.activation(sg[q % 2][:, :], bank[1][:, :], ACT.Silu).then_inc(m_sg, 1)

            def copy_hT(i, q, turn):
                act.wait_ge(m_ht, i + 1)
                wait(act, m_o, i - 1)
                nc.scalar.activation(hT[q % 2][:, :], bank[3][:, :], ACT.Copy).then_inc(m_hT, 1)
            tiles(act, (hi_tile, 1), (silu, 0), (copy_hT, -1))

            for g in range(NG):
                q = g % NQ
                act.wait_ge(f_bb, g + 1)
                wait(act, f_w[q], g // NQ * 16)
                for b in range(4):
                    last = nc.scalar.activation(f_o[q][:, b, :], fin[q][:, b, :], ACT.Identity, bias=f_b[q][:, b:b + 1],
                                                scale=f_r[q][:, b:b + 1])
                last.then_inc(f_n, 1)

        @block.vector
        def _(dve):
            made = [0]

            def prep(ins):
                made[0] += 1
                ins.then_inc(s_prep, 1)
                dve.wait_ge(s_prep, made[0])

            dve.wait_ge(s_w, 16 * 7)
            dve.wait_ge(s_win, 16)
            dve.wait_ge(s_pool, 10)
            prep(nc.vector.tensor_copy(wz_h[:, :], w_in[:, 0:DI]))
            prep(nc.vector.tensor_tensor(wz_l[:, :], w_in[:, 0:DI], wz_h[:, :].bitcast(F32), ALU.subtract))
            for k in range(TAPS):
                prep(nc.vector.tensor_tensor(wconv[:, k, :], cw[:, k, :], w_in[:, ZX:ZX + CC], ALU.mult))
            prep(nc.vector.tensor_copy(cb_part[0][:, :], cb[:, :]))
            prep(nc.vector.tensor_copy(wconv_h[:, :, :], wconv[:, :, :]))
            prep(nc.vector.tensor_tensor(wconv_l[:, :, :], wconv[:, :, :], wconv_h[:, :, :].bitcast(F32), ALU.subtract))
            prep(nc.vector.tensor_tensor(cb_rest[:, :], cb[:, :], cb_part[0][:, :], ALU.subtract))
            prep(nc.vector.tensor_copy(cb_part[1][:, :], cb_rest[:, :]))
            prep(nc.vector.tensor_tensor(cb_part[2][:, :], cb_rest[:, :], cb_part[1][:, :], ALU.subtract))
            prep(nc.vector.tensor_scalar(cb_rows[:, :], cb_part[0][:, :], ident[0:3, 0:1], None, ALU.mult))
            for i in (1, 2):
                prep(nc.vector.scalar_tensor_tensor(out=cb_rows[:, :], in0=cb_part[i][:, :], scalar=ident[0:3, i:i + 1],
                                                    in1=cb_rows[:, :], op0=ALU.mult, op1=ALU.add))
            nc.vector.nop().then_inc(s_cbrow, 1)
            for h in range(NH):
                prep(nc.vector.tensor_scalar(w_out[:, h, :], w_out[:, h, :], nscale[:, h:h + 1], None, ALU.mult))
                prep(nc.vector.tensor_scalar(d_diag[:, h, :], ident[:, :], d_skip[:, h:h + 1], None, ALU.mult))
            assert made[0] == PREP, made[0]
            def lo(n, p):
                dve.wait_ge(split_hi, n + 1)
                nc.vector.tensor_tensor(xl[p][:, :, TAPS - 1:TAPS - 1 + S], xT[:, bass.ds(n * 2, 2), :],
                                        xh[p][:, :, TAPS - 1:TAPS - 1 + S].bitcast(F32), ALU.subtract).then_inc(split_lo, 1)

            dve.wait_ge(s_pool, POOL1)
            lo(0, 0)
            lo(1, 1)
            dve.wait_ge(s_dtps, NB // 4)
            nc.vector.tensor_tensor(dt_v[:, :, :], bank[6][:, 0:NB * NH].rearrange("p (b h) -> p b h", h=NH),
                                    dt_bias[:, None, :].to_broadcast([P, NB, NH]), ALU.add).then_inc(s_dt, 1)
            dve.wait_ge(s_dtx, 3)
            nc.vector.scalar_tensor_tensor(out=dt_v[:, :, :], in0=dt_v[:, :, :], scalar=0.0, in1=dt_e[:, :, :],
                                           op0=ALU.max, op1=ALU.add).then_inc(s_dt, 1)
            dve.wait_ge(s_dt, 2)
            nc.vector.tensor_scalar(dt_half[:, :, :], dt_v[:, :, :], 0.5, None, ALU.mult).then_inc(s_dt, 1)
            dve.wait_ge(s_aprep, 1)
            nc.vector.scalar_tensor_tensor(out=dt_a[:, :, :], in0=dt_v[:, :, :], scalar=-1.0,
                                           in1=a_neg[:, None, :].to_broadcast([P, NB, NH]), op0=ALU.mult,
                                           op1=ALU.mult).then_inc(s_dt, 1)

            def gate_bc(n, p):
                dve.wait_ge(t_bc_r, n + 1)
                if not isinstance(n, int) or n >= 2:
                    dve.wait_ge(sg_ps[1], n - 1)
                for half, dst in ((0, b_sb[p]), (NS, c_sb[p])):
                    last = nc.vector.scalar_tensor_tensor(out=dst[:, :], in0=t_bc[half:half + NS, :], scalar=1.0,
                                                          in1=bank[0][half:half + NS, 0:2 * S], op0=ALU.add, op1=ALU.mult)
                last.then_inc(bc_gated, 1)

            def gate_x(n, j):
                dve.wait_ge(t_x_r[j], n + 1)
                wait(dve, xdt_r[j], n)
                nc.vector.scalar_tensor_tensor(out=x_s[j][:, :], in0=t_x[j][:, :], scalar=1.0, in1=bank[2 + j][:, 0:DI],
                                               op0=ALU.add, op1=ALU.mult).then_inc(x_gated[j], 1)

            def w_step(n, j):
                dve.wait_ge(e_r[j], n + 1)
                wait(dve, y_ps[j], n)
                nc.vector.scalar_tensor_tensor(out=w_sb[j][:, :, :], in0=e_sb[j][:, :, :], scalar=0.25,
                                               in1=bank[4 + j][:, None, 0:S].to_broadcast([P, NH, S]),
                                               op0=ALU.mult, op1=ALU.mult).then_inc(w_raw[j], 1)

            def y_step(n, p, j):
                dve.wait_ge(y_ps[j], n + 1)
                dve.wait_ge(z_ev, n + 1)
                wait(dve, o_ps[j], n)
                wait(dve, sq_r[j], n)
                nc.vector.tensor_tensor(y_sb[j][:, :, :], z_sb[p][:, :, j * S:(j + 1) * S],
                                        bank[6][:, 0:NH * S].rearrange("p (h s) -> p h s", h=NH), ALU.mult).then_inc(y_r[j], 1)

            def o_step(n, p, j):
                dve.wait_ge(o_ps[j], n + 1)
                nc.vector.tensor_copy(pr[p][j][:, :], bank[7][:, 0:D])
                nc.vector.tensor_scalar(ss_eps[p][:, j:j + 1], bank[7][:, D:D + 1], EPS, None, ALU.add).then_inc(o_ev[j], 1)

            def ln_stats(n, p, base):
                for j in range(2):
                    dve.wait_ge(ln_x, (n + base) * 2 + j + 1)
                    nc.vector.bn_stats(stats[p][j][:, :], xr[p][j][:, :]).then_inc(ln_s, 1)
                wait_apart(dve, ln_s, (n + base) * 2 + 2)
                for j in range(2):
                    nc.vector.bn_aggr(mv[p][:, j, :], stats[p][j][:, :]).then_inc(ln_v, 1)

            def ln_first(n, p):
                dve.wait_ge(rg_r, n + 1)
                for j in range(2):
                    nc.vector.scalar_tensor_tensor(out=xr[p][j][:, None, :], in0=pr[p][j][:, None, :], scalar=r_gate[p][:, j:j + 1],
                                                   in1=x_nat[:, bass.ds(n * 2 + j, 1), :], op0=ALU.mult, op1=ALU.add).then_inc(ln_x, 1)
                ln_stats(n, p, 0)

            def ln_norm(n, p, base):
                dve.wait_ge(ln_r, n + base + 1)
                for j in range(2):
                    last = nc.vector.tensor_scalar(x_nat[:, bass.ds(n * 2 + j, 1), :], xr[p][j][:, None, :], mv[p][:, j, 0:1],
                                                   r_ln[p][:, j:j + 1], ALU.subtract, ALU.mult)
                last.then_inc(ln_d, 1)

            def split_qk(n, p):
                dve.wait_ge(qa_r, n + 1)
                qk = bank[1][:, :].rearrange("p (a s) -> p a s", a=2)
                nc.vector.tensor_tensor(qk_rest[:, :, :], qk, qk_part[p][:, 0, :, :], ALU.subtract).then_inc(q_st, 1)
                dve.wait_ge(q_st, 3 * n + 1)
                nc.vector.tensor_copy(qk_part[p][:, 1, :, :], qk_rest[:, :, :]).then_inc(q_st, 1)
                dve.wait_ge(q_st, 3 * n + 2)
                nc.vector.tensor_tensor(qk_part[p][:, 2, :, :], qk_rest[:, :, :], qk_part[p][:, 1, :, :], ALU.subtract).then_inc(q_st, 1)

            gate_bc(0, 0)
            gate_x(0, 0)
            gate_x(0, 1)

            def body(n, p, nxt, nxt2, turn):
                before_it = not isinstance(n, int) or n
                w_step(n, 0)
                if nxt:
                    gate_bc(n + 1, 1 - p)
                w_step(n, 1)
                if before_it:
                    ln_first(n - 1, 1 - p)
                y_step(n, p, 0)
                if not nxt:
                    split_qk(0, 0)
                if nxt:
                    gate_x(n + 1, 0)
                y_step(n, p, 1)
                o_step(n, p, 0)
                if nxt2:
                    lo(n + 2, p)
                if nxt:
                    gate_x(n + 1, 1)
                if before_it:
                    ln_norm(n - 1, 1 - p, 0)
                o_step(n, p, 1)
            pairs(dve, body)
            ln_first(NPAIR - 1, 1)
            ln_norm(NPAIR - 1, 1, 0)
            def reduce_max(n, j, g):
                m = n * 2 + j
                dve.wait_ge(s_ps[g % 2], 2 * m + g // 2 + 1)
                nc.vector.tensor_reduce(mx[j][:, HG * g:HG * g + HG], bank[2 + g % 2][:, :].rearrange("p (h k) -> p h k", h=HG),
                                        AX_X, ALU.max).then_inc(red, 1)

            def split_max(n, j):
                m = n * 2 + j
                dve.wait_ge(red, m * 4 + 4)
                nc.vector.tensor_scalar(nm_part[j][:, 0, :], mx[j][:, :], -1.0, None, ALU.mult).then_inc(nm_s, 1)
                dve.wait_ge(nm_s, m * 4 + 1)
                nc.vector.scalar_tensor_tensor(out=nm_rest[j][:, :], in0=mx[j][:, :], scalar=-1.0, in1=nm_part[j][:, 0, :],
                                               op0=ALU.mult, op1=ALU.subtract).then_inc(nm_s, 1)
                dve.wait_ge(nm_s, m * 4 + 2)
                nc.vector.tensor_copy(nm_part[j][:, 1, :], nm_rest[j][:, :]).then_inc(nm_s, 1)
                dve.wait_ge(nm_s, m * 4 + 3)
                nc.vector.tensor_tensor(nm_part[j][:, 2, :], nm_rest[j][:, :], nm_part[j][:, 1, :], ALU.subtract).then_inc(nm_s, 1)

            def copy_nmT(n, j):
                m = n * 2 + j
                dve.wait_ge(nmT_ps, m + 1)
                nc.vector.tensor_copy(nm_T[j][:, :], bank[2][0:NPART * HEADS, 0:P // 2].bitcast(BF16)).then_inc(nmT_r, 1)

            def normalise(n, j):
                m = n * 2 + j
                dve.wait_ge(inv_r, m + 1)
                nc.vector.tensor_tensor(att[j][:, :], att[j][:, :], inv[j][:, :], ALU.mult).then_inc(an_r, 1)

            def residual(n, p, j):
                m = n * 2 + j
                dve.wait_ge(o2_ps, m + 1)
                nc.vector.tensor_tensor(xr[p][j][:, None, :], x_nat[:, bass.ds(m, 1), :], bank[7][:, None, 0:D], ALU.add).then_inc(ln_x, 1)

            def link(n, at, ins, apart=False):
                ins.then_inc(rt, 1)
                if apart:
                    wait_apart(dve, rt, n * RT + at)
                else:
                    dve.wait_ge(rt, n * RT + at)

            def route_top(n, p):
                dve.wait_ge(r_lg, n + 1)
                link(n, 1, nc.vector.tensor_copy(lg[p][:, :, :], bank[0][:, 2 * S:2 * S + 2 * NE].rearrange("p (b e) -> p b e", e=NE)), apart=True)
                nc.vector.max(top[p][:, 0, :], lg[p][:, 0, :])
                link(n, 2, nc.vector.max(top[p][:, 1, :], lg[p][:, 1, :]), apart=True)
                nc.vector.max_index(top_i[p][:, 0, :], top[p][:, 0, :], lg[p][:, 0, :])
                link(n, 3, nc.vector.max_index(top_i[p][:, 1, :], top[p][:, 1, :], lg[p][:, 1, :]))
                link(n, 4, nc.vector.tensor_tensor(ex[p][:, :, 0:NE], lg[p][:, :, :], top[p][:, :, 0:1].to_broadcast([P, 2, NE]), ALU.subtract))
                link(n, 5, nc.vector.tensor_tensor(ex[p][:, :, NE], top[p][:, :, 1], top[p][:, :, 0], ALU.subtract))

            def route_hot(n, p):
                link(n, 6, nc.vector.tensor_copy(top_f[p][:, :, :], top_i[p][:, :, 0:TOPK]))
                link(n, 7, nc.vector.tensor_tensor(hot[p][:, :, :, :].rearrange("p b k e -> p (b k) e"),
                                                   top_f[p][:, :, :].rearrange("p b k -> p (b k)")[:, :, None].to_broadcast([P, 2 * TOPK, NE]),
                                                   iota_e[:, None, :].to_broadcast([P, 2 * TOPK, NE]), ALU.is_equal))
                link(n, 8, nc.vector.tensor_tensor(both[p][:, :, :], hot[p][:, :, 0, :], hot[p][:, :, 1, :], ALU.add))

            def route_count(n, p):
                dve.wait_ge(r_cnt, n + 1)
                link(n, 9, nc.vector.tensor_tensor(pos[p][:, :, :], bank[7][:, C0:C0 + 2 * NE].rearrange("p (b e) -> p b e", e=NE),
                                                   base[:, None, :].to_broadcast([P, 2, NE]), ALU.add))
                link(n, 10, nc.vector.tensor_tensor(base[:, :], bank[7][:, C0 + 2 * NE:C0 + 3 * NE], base[:, :], ALU.add))

            def route_rows(n, p, turn):
                link(n, 11, nc.vector.tensor_tensor(picked[p][:, :, :, :], hot[p][:, :, :, :],
                                                    pos[p][:, :, None, :].to_broadcast([P, 2, TOPK, NE]), ALU.mult))
                link(n, 12, nc.vector.tensor_reduce(slot_f[p][:, :], picked[p][:, :, :, :].rearrange("p b k e -> p (b k) e"), AX_X, ALU.add))
                dve.wait_ge(r_ex, n + 1)
                link(n, 13, nc.vector.tensor_reduce(esum[p][:, :], ex[p][:, :, 0:NE], AX_X, ALU.add))
                wait(dve, sc_d[p], turn * 64)
                link(n, 14, nc.vector.reciprocal(row[p][0][:, :, D], esum[p][:, :]))
                link(n, 15, nc.vector.tensor_tensor(row[p][1][:, :, D], row[p][0][:, :, D], ex[p][:, :, NE], ALU.mult))
                nc.vector.tensor_copy(slot_i[p][:, :], slot_f[p][:, :]).then_inc(r_slot, 1)

            def half(n, p, turn, j, has):
                np_, nj = (n, 1) if j == 0 else (n + 1, 0)
                bn, bj = (n - 1, 1) if j == 0 else (n, 0)
                bp = (1 - p) if j == 0 else p
                nxt, bef = has(1 if j else 0), has(0 if j else -1)
                if nxt:
                    reduce_max(np_, nj, 0)
                if j == 1 and has(-2):
                    route_count(n - 2, p)
                if nxt:
                    reduce_max(np_, nj, 1)
                if j == 1 and has(2):
                    split_qk(n + 2, p)
                if nxt:
                    reduce_max(np_, nj, 2)
                if bef:
                    normalise(bn, bj)
                if nxt:
                    reduce_max(np_, nj, 3)
                    split_max(np_, nj)
                    copy_nmT(np_, nj)
                if j == 1 and has(-1):
                    ln_norm(n - 1, 1 - p, NPAIR)
                if bef:
                    residual(bn, bp, bj)
                if j == 1 and has(-2):
                    route_rows(*pair_at(n, p, turn, -2))
                if j == 0 and has(-2):
                    route_top(n - 2, p)
                    route_hot(n - 2, p)
                if j == 0 and has(-1):
                    ln_stats(n - 1, 1 - p, NPAIR)
            dve.wait_ge(c3, C2N)
            rounds_of_pairs(dve, half)
            hand_over(dve)

            def turn_experts(experts):
                for e in experts:
                    for k, dst in enumerate((wg, wu)):
                        dve.wait_ge(wn_hi, e * 2 + k + 1)
                        nc.vector.tensor_tensor(dst[1][:, e * F:(e + 1) * F], turned[e % 2][k][:, :],
                                                dst[0][:, e * F:(e + 1) * F].bitcast(F32), ALU.subtract).then_inc(wn_taken[k], 1)
            finish_and_turn(half, turn_experts)
            turn_experts(range(3, 5))
            at = [0]

            def link(ins):
                at[0] += 1
                ins.then_inc(tab, 1)
                dve.wait_ge(tab, at[0])

            one = slice(0, 1)
            ROUND = float(2 ** 23)
            dve.wait_ge(rt, NPAIR * RT)
            dve.wait_ge(c3, C3N)
            link(nc.vector.tensor_copy(pad_at[:, :], base[one, :]))
            link(nc.vector.tensor_tensor(cnt[:, :], base[one, :], e_base[one, :], ALU.subtract))
            link(nc.vector.tensor_scalar(ntile[:, :], cnt[:, :], 1.0 / P, (P - 1) / (2.0 * P), ALU.mult, ALU.add))
            link(nc.vector.tensor_scalar(ntile[:, :], ntile[:, :], ROUND, ROUND, ALU.add, ALU.subtract))
            link(nc.vector.memset(start[:, 0:1], 0.0))
            for e in range(NE):
                link(nc.vector.tensor_tensor(start[:, e + 1:e + 2], start[:, e:e + 1], ntile[:, e:e + 1], ALU.add))
            link(nc.vector.tensor_scalar(coef[:, :], ntile[:, :], -float(P), float(CAP), ALU.mult, ALU.add))
            link(nc.vector.tensor_tensor(passed[:, :, :], start[:, None, 1:NE + 1].to_broadcast([1, NTILE, NE]),
                                         tile_no[:, :, None].to_broadcast([1, NTILE, NE]), ALU.is_le))
            link(nc.vector.tensor_reduce(tile_e[:, :], passed[:, :, :], AX_X, ALU.add))
            link(nc.vector.tensor_tensor(passed_c[:, :, :], passed[:, :, :], coef[:, None, :].to_broadcast([1, NTILE, NE]), ALU.mult))
            link(nc.vector.tensor_reduce(tile_r[:, :], passed_c[:, :, :], AX_X, ALU.add))
            link(nc.vector.scalar_tensor_tensor(out=tile_row[:, :], in0=tile_no[:, :], scalar=float(P), in1=tile_r[:, :],
                                                op0=ALU.mult, op1=ALU.add))
            link(nc.vector.tensor_scalar(tile_col[:, :], tile_e[:, :], float(NE - 1), float(F), ALU.min, ALU.mult))
            assert at[0] == TABN, at
            turn_experts(range(5, NE))

            def lo_tile(i, q, turn):
                dve.wait_ge(m_hi, i + 1)
                wait(dve, m_y, i - DEPTH + 1)
                nc.vector.tensor_copy(w_place[q][:, :], xs_in[q][:, D:D + 2])
                nc.vector.tensor_tensor(xel[q][:, :], bank[0][:, 0:P], xeh[q][:, :].bitcast(F32), ALU.subtract).then_inc(m_lo, 1)

            def mul_up(i, q, turn):
                dve.wait_ge(m_sg, i + 1)
                dve.wait_ge(m_u, i + 1)
                wait(dve, m_ht, i - 1)
                nc.vector.tensor_tensor(hid[q % 2][:, :], sg[q % 2][:, :], bank[2][:, :], ALU.mult).then_inc(m_hid, 1)

            def scale_out(i, q, turn):
                dve.wait_ge(m_o, i + 1)
                dve.wait_ge(m_half, i + 1)
                wait(dve, p_sc[q], turn * 16)
                nc.vector.tensor_copy(part_i[q][:, :], w_place[q][:, 1:2])
                nc.vector.scalar_tensor_tensor(out=y_out[q][:, :], in0=bank[4][:, 0:D], scalar=w_place[q][:, 0:1],
                                               in1=half_x[q][:, :], op0=ALU.mult, op1=ALU.add).then_inc(m_y, 1)
            tiles(dve, (lo_tile, 1), (mul_up, 0), (scale_out, -2))

            def add_parts(g):
                q = g % NQ
                dve.wait_ge(f_ld[q], g // NQ * 32 + 32)
                wait(dve, f_n, g - NQ + 1)
                nc.vector.tensor_tensor(fin[q][:, :, :], y_in[q][:, 0, :, :], y_in[q][:, 1, :, :], ALU.add).then_inc(f_c, 1)

            def moments(g):
                q = g % NQ
                dve.wait_ge(f_c, g + 1)
                for b in range(4):
                    last = nc.vector.bn_stats(f_st[q][:, b, :], fin[q][:, b, :])
                last.then_inc(f_mom, 1)

            def moments_end(g):
                q = g % NQ
                dve.wait_ge(f_mom, 2 * g + 1)
                for b in range(4):
                    last = nc.vector.bn_aggr(f_mv[q][:, b, :], f_st[q][:, b, :])
                last.then_inc(f_mom, 1)
                dve.wait_ge(f_mom, 2 * g + 2)
                nc.vector.tensor_scalar(f_ve[q][:, :], f_mv[q][:, :, 1], EPS, None, ALU.add).then_inc(f_v, 1)

            def shift(g):
                q = g % NQ
                dve.wait_ge(f_rr, g + 1)
                nc.vector.scalar_tensor_tensor(out=f_b[q][:, :], in0=f_mv[q][:, :, 0], scalar=-1.0, in1=f_r[q][:, :],
                                               op0=ALU.mult, op1=ALU.mult).then_inc(f_bb, 1)
            add_parts(0)
            for g in range(NG):
                moments(g)
                if g + 1 < NG:
                    add_parts(g + 1)
                moments_end(g)
                if g:
                    shift(g - 1)
            shift(NG - 1)



_INS = ["x", "ctx_1024", "L0_attn_W_in", "L0_attn_conv_w", "L0_attn_conv_b", "L0_attn_dt_bias", "L0_attn_A_log",
        "L0_attn_D", "L0_attn_norm_scale", "L0_attn_W_out", "L0_xattn_wq", "L0_xattn_wk", "L0_xattn_wv", "L0_xattn_wo",
        "L0_ffn_router_w", "L0_ffn_gate_w", "L0_ffn_up_w", "L0_ffn_down_w"]


def kernel(**inputs):
    import numpy as _np
    import concourse.bacc as _bacc
    from concourse import mybir as _mybir
    from concourse.bass_utils import run_bass_kernel_spmd as _run

    nc = _bacc.Bacc("TRN2", target_bir_lowering=False, num_devices=1)
    arrays, aps = {}, {}
    for name in _INS:
        a = _np.ascontiguousarray(inputs[name])
        arrays[f"in_{name}_dram"] = a
        aps[name] = nc.dram_tensor(f"in_{name}_dram", a.shape, _mybir.dt.from_np(a.dtype), kind="ExternalInput").ap()
    out = nc.dram_tensor("out_0_dram", inputs["x"].shape, _mybir.dt.float32, kind="ExternalOutput").ap()
    build(nc, aps, out)
    r = _run(nc, [arrays], core_ids=[0])
    return r.results[0]["out_0_dram"]
```
